# Optimizing a Trainium2 kernel written in Bass

```python
import numpy as np
import jax
import jax.numpy as jnp

def _softmax(x, axis=-1):
    return jax.nn.softmax(x, axis=axis)

def _gelu(x):
    return jax.nn.gelu(x, approximate=True)

def _silu(x):
    return jax.nn.silu(x)

def _sigmoid(x):
    return jax.nn.sigmoid(x)

def _layernorm(x, axis=-1, eps=1e-05):
    m = jnp.mean(x, axis=axis, keepdims=True)
    v = jnp.var(x, axis=axis, keepdims=True)
    return (x - m) / jnp.sqrt(v + eps)

def _scatter_add(tgt, idx, src, axis=0):
    return tgt.at[idx].add(src)

def _segment_sum(src, seg, n):
    return jax.ops.segment_sum(src, seg, n)
kernel_name = 'mk_perceiver_d2_seqx_r4_96bbb4'

def setup_inputs(seed: int=0):
    np.random.seed(seed)
    _w = jnp.asarray

    def _rec_inputs():
        import jax
        import jax.numpy as jnp
        _rk = jax.random.key(seed)
        x = 7.22e-05 + 1 * jax.random.normal(jax.random.fold_in(_rk, 1), (8, 64, 256), jnp.float32)
        _lenS = 64 - jax.random.randint(jax.random.fold_in(_rk, 7), (8,), 0, max(1, 64 // 4) + 1, jnp.int32)
        _lenS2 = 1601 - jax.random.randint(jax.random.fold_in(_rk, 8), (8,), 0, max(1, 1601 // 4) + 1, jnp.int32)
        _ctx_768P = jax.random.normal(jax.random.fold_in(_rk, 11), (8, 16, 192), jnp.float32)
        _ctx_768c = jax.random.dirichlet(jax.random.fold_in(_rk, 511), 0.3 * jnp.ones((16,), jnp.float32), (8, 1601))
        _ctx_768t = jnp.einsum('bsk,bkd->bsd', _ctx_768c, _ctx_768P)
        _ctx_768t = _ctx_768t * jax.lax.rsqrt(jnp.mean(jnp.square(_ctx_768t)) + 1e-12) * 0.953939
        ctx_768 = 2.09791e-05 + 1.00001 * (_ctx_768t + 0.3 * jax.random.normal(jax.random.fold_in(_rk, 611), (8, 1601, 192), jnp.float32))
        return (x, ctx_768)
    x, ctx_768 = _rec_inputs()

    def _L0_xattn_setup():
        import jax, jax.numpy as jnp
        import numpy as np
        HEADS = 8
        DIM_HEAD = 64
        SCALE = DIM_HEAD ** (-0.5)
        key = jax.random.key(seed)
        ks = jax.random.split(key, 7)
        b, n, m = (4, 512, 256)
        qd, cd, inner = (256, 192, HEADS * DIM_HEAD)
        s = lambda fan_in: 1.0 / np.sqrt(fan_in)
        return {'x': jax.random.normal(ks[0], (b, n, qd), jnp.float32), 'context': jax.random.normal(ks[1], (b, m, cd), jnp.float32), 'Wq': jax.random.normal(ks[2], (qd, inner), jnp.float32) * s(qd), 'Wk': jax.random.normal(ks[3], (cd, inner), jnp.float32) * s(cd), 'Wv': jax.random.normal(ks[4], (cd, inner), jnp.float32) * s(cd), 'Wout': jax.random.normal(ks[5], (inner, qd), jnp.float32) * s(inner), 'bout': jax.random.normal(ks[6], (qd,), jnp.float32) * 0.01}
    _L0_xattn_all = _L0_xattn_setup()
    _L0_xattn_in = {k: v for k, v in _L0_xattn_all.items() if k in ('Wq', 'Wk', 'Wv', 'Wout', 'bout')}
    del _L0_xattn_all

    def _L0_attn_setup():
        import jax, jax.numpy as jnp
        import numpy as np
        D_MODEL = 256
        NUM_HEADS = 16
        D_K = D_MODEL // NUM_HEADS
        THETA = 10000.0
        BATCH = 4
        SEQ = 512

        def rope(x, positions, theta=THETA):
            d_k = x.shape[-1]
            inv_freq = theta ** (-jnp.arange(0, d_k, 2, dtype=jnp.float32) / d_k)
            ang = positions[:, None].astype(jnp.float32) * inv_freq[None, :]
            cos, sin = (jnp.cos(ang), jnp.sin(ang))
            x1 = x[..., 0::2]
            x2 = x[..., 1::2]
            r1 = x1 * cos - x2 * sin
            r2 = x1 * sin + x2 * cos
            out = jnp.stack([r1, r2], axis=-1).reshape(x.shape)
            return out.astype(x.dtype)
        key = jax.random.key(seed)
        k0, k1, k2, k3, k4 = jax.random.split(key, 5)
        std_qk = 2.0 / (D_MODEL + D_MODEL)
        x = jax.random.normal(k0, (BATCH, SEQ, D_MODEL), dtype=jnp.float32)
        P_Q = jax.random.normal(k1, (D_MODEL, D_MODEL), dtype=jnp.float32) * std_qk
        P_K = jax.random.normal(k2, (D_MODEL, D_MODEL), dtype=jnp.float32) * std_qk
        P_V = jax.random.normal(k3, (D_MODEL, D_MODEL), dtype=jnp.float32) * std_qk
        P_O = jax.random.normal(k4, (D_MODEL, D_MODEL), dtype=jnp.float32) * std_qk
        return {'x': x, 'P_Q': P_Q, 'P_K': P_K, 'P_V': P_V, 'P_O': P_O}
    _L0_attn_all = _L0_attn_setup()
    _L0_attn_in = {k: v for k, v in _L0_attn_all.items() if k in ('P_Q', 'P_K', 'P_V', 'P_O')}
    del _L0_attn_all

    def _L0_ffn_setup():
        import jax, jax.numpy as jnp
        import numpy as np
        MANT_BITS = 8
        _PWL_X = jnp.linspace(-4.0, 4.0, 33, dtype=jnp.float32)
        _PWL_Y = 0.5 * _PWL_X * (1.0 + jax.lax.erf(_PWL_X / jnp.sqrt(jnp.float32(2.0))))

        def float2fix(x, mantissa_bits):
            s = jnp.float32(2.0 ** mantissa_bits)
            q = jnp.round(x * s) / s
            return x + jax.lax.stop_gradient(q - x)

        def pwlin_gelu_basic(x, mantissa_bits_in, mantissa_bits_out):
            xq = float2fix(x, mantissa_bits_in)
            y = jnp.interp(xq, _PWL_X, _PWL_Y)
            y = jnp.where(xq > 4.0, xq, jnp.where(xq < -4.0, jnp.float32(0.0), y))
            return float2fix(y, mantissa_bits_out)
        key = jax.random.key(seed)
        k_x, k_w1, k_b1, k_w2, k_b2 = jax.random.split(key, 5)
        dim, ff_dim = (256, 1024)
        B, S = (32, 128)
        sc1 = 1.0 / np.sqrt(dim)
        sc2 = 1.0 / np.sqrt(ff_dim)
        return {'x': jax.random.normal(k_x, (B, S, dim), dtype=jnp.float32), 'w1': jax.random.uniform(k_w1, (dim, ff_dim), jnp.float32, -sc1, sc1), 'b1': jax.random.uniform(k_b1, (ff_dim,), jnp.float32, -sc1, sc1), 'w2': jax.random.uniform(k_w2, (ff_dim, dim), jnp.float32, -sc2, sc2), 'b2': jax.random.uniform(k_b2, (dim,), jnp.float32, -sc2, sc2)}
    _L0_ffn_all = _L0_ffn_setup()
    _L0_ffn_in = {k: v for k, v in _L0_ffn_all.items() if k in ('w1', 'b1', 'w2', 'b2')}
    del _L0_ffn_all

    def _L1_xattn_setup():
        import jax, jax.numpy as jnp
        import numpy as np
        HEADS = 16
        DIM_HEAD = 64
        SCALE = DIM_HEAD ** (-0.5)
        QUERY_DIM = 256
        CONTEXT_DIM = 192
        INNER_DIM = HEADS * DIM_HEAD
        key = jax.random.key(seed)
        ks = jax.random.split(key, 7)
        B, Nq, Nk = (8, 1024, 77)
        x = jax.random.normal(ks[0], (B, Nq, QUERY_DIM), dtype=jnp.float32)
        context = jax.random.normal(ks[1], (B, Nk, CONTEXT_DIM), dtype=jnp.float32)
        Wq = jax.random.normal(ks[2], (QUERY_DIM, INNER_DIM), dtype=jnp.float32) * QUERY_DIM ** (-0.5)
        Wk = jax.random.normal(ks[3], (CONTEXT_DIM, INNER_DIM), dtype=jnp.float32) * CONTEXT_DIM ** (-0.5)
        Wv = jax.random.normal(ks[4], (CONTEXT_DIM, INNER_DIM), dtype=jnp.float32) * CONTEXT_DIM ** (-0.5)
        Wo = jax.random.normal(ks[5], (INNER_DIM, QUERY_DIM), dtype=jnp.float32) * INNER_DIM ** (-0.5)
        bo = jnp.zeros((QUERY_DIM,), dtype=jnp.float32)
        return {'x': x, 'context': context, 'Wq': Wq, 'Wk': Wk, 'Wv': Wv, 'Wo': Wo, 'bo': bo}
    _L1_xattn_all = _L1_xattn_setup()
    _L1_xattn_in = {k: v for k, v in _L1_xattn_all.items() if k in ('Wq', 'Wk', 'Wv', 'Wo', 'bo')}
    del _L1_xattn_all

    def _L1_attn_setup():
        import jax, jax.numpy as jnp
        import numpy as np
        D_MODEL = 256
        NHEAD = 16
        HEAD_DIM = D_MODEL // NHEAD
        LN_EPS = 1e-05

        def _layer_norm(x, gamma, beta):
            mu = jnp.mean(x, axis=-1, keepdims=True)
            var = jnp.mean(jnp.square(x - mu), axis=-1, keepdims=True)
            return (x - mu) * jax.lax.rsqrt(var + LN_EPS) * gamma + beta
        key = jax.random.key(seed)
        k1, k2, k3 = jax.random.split(key, 3)
        x = jax.random.normal(k1, (2, 512, D_MODEL), dtype=jnp.float32)
        w_qkv = jax.random.normal(k2, (3 * D_MODEL, D_MODEL), dtype=jnp.float32) * (1.0 / np.sqrt(D_MODEL))
        b_qkv = jax.random.normal(k3, (3 * D_MODEL,), dtype=jnp.float32) * 0.01
        ln_gamma = jnp.ones((D_MODEL,), dtype=jnp.float32)
        ln_beta = jnp.zeros((D_MODEL,), dtype=jnp.float32)
        return {'x': x, 'w_qkv': w_qkv, 'b_qkv': b_qkv, 'ln_gamma': ln_gamma, 'ln_beta': ln_beta}
    _L1_attn_all = _L1_attn_setup()
    _L1_attn_in = {k: v for k, v in _L1_attn_all.items() if k in ('w_qkv', 'b_qkv', 'ln_gamma', 'ln_beta')}
    del _L1_attn_all

    def _L1_ffn_setup():
        import jax, jax.numpy as jnp
        import numpy as np
        TOP_K = 8
        CAPACITY = 128

        def _silu(x):
            return x * jax.nn.sigmoid(x)
        key = jax.random.key(seed)
        ks = jax.random.split(key, 7)
        B, S, H, E, I, Is = (2, 256, 256, 64, 128, 512)
        s = 0.05
        return {'hidden_states': jax.random.normal(ks[0], (B, S, H), jnp.float32), 'gate_w': jax.random.normal(ks[1], (H, E), jnp.float32) * s, 'shared_gate_w': jax.random.normal(ks[2], (H, 1), jnp.float32) * s, 'shared_gate_up_w': jax.random.normal(ks[3], (H, 2 * Is), jnp.float32) * s, 'shared_down_w': jax.random.normal(ks[4], (Is, H), jnp.float32) * s, 'expert_gate_up_w': jax.random.normal(ks[5], (E, H, 2 * I), jnp.float32) * s, 'expert_down_w': jax.random.normal(ks[6], (E, I, H), jnp.float32) * s}
    _L1_ffn_all = _L1_ffn_setup()
    _L1_ffn_in = {k: v for k, v in _L1_ffn_all.items() if k in ('gate_w', 'shared_gate_w', 'shared_gate_up_w', 'shared_down_w', 'expert_gate_up_w', 'expert_down_w')}
    del _L1_ffn_all
    return {'x': x, 'ctx_768': ctx_768, 'L0_xattn_Wq': _L0_xattn_in['Wq'], 'L0_xattn_Wk': _L0_xattn_in['Wk'], 'L0_xattn_Wv': _L0_xattn_in['Wv'], 'L0_xattn_Wout': _L0_xattn_in['Wout'], 'L0_xattn_bout': _L0_xattn_in['bout'], 'L0_attn_P_Q': _L0_attn_in['P_Q'], 'L0_attn_P_K': _L0_attn_in['P_K'], 'L0_attn_P_V': _L0_attn_in['P_V'], 'L0_attn_P_O': _L0_attn_in['P_O'], 'L0_ffn_w1': _L0_ffn_in['w1'], 'L0_ffn_b1': _L0_ffn_in['b1'], 'L0_ffn_w2': _L0_ffn_in['w2'], 'L0_ffn_b2': _L0_ffn_in['b2'], 'L1_xattn_Wq': _L1_xattn_in['Wq'], 'L1_xattn_Wk': _L1_xattn_in['Wk'], 'L1_xattn_Wv': _L1_xattn_in['Wv'], 'L1_xattn_Wo': _L1_xattn_in['Wo'], 'L1_xattn_bo': _L1_xattn_in['bo'], 'L1_attn_w_qkv': _L1_attn_in['w_qkv'], 'L1_attn_b_qkv': _L1_attn_in['b_qkv'], 'L1_attn_ln_gamma': _L1_attn_in['ln_gamma'], 'L1_attn_ln_beta': _L1_attn_in['ln_beta'], 'L1_ffn_gate_w': _L1_ffn_in['gate_w'], 'L1_ffn_shared_gate_w': _L1_ffn_in['shared_gate_w'], 'L1_ffn_shared_gate_up_w': _L1_ffn_in['shared_gate_up_w'], 'L1_ffn_shared_down_w': _L1_ffn_in['shared_down_w'], 'L1_ffn_expert_gate_up_w': _L1_ffn_in['expert_gate_up_w'], 'L1_ffn_expert_down_w': _L1_ffn_in['expert_down_w']}

def reference(x, ctx_768, L0_xattn_Wq, L0_xattn_Wk, L0_xattn_Wv, L0_xattn_Wout, L0_xattn_bout, L0_attn_P_Q, L0_attn_P_K, L0_attn_P_V, L0_attn_P_O, L0_ffn_w1, L0_ffn_b1, L0_ffn_w2, L0_ffn_b2, L1_xattn_Wq, L1_xattn_Wk, L1_xattn_Wv, L1_xattn_Wo, L1_xattn_bo, L1_attn_w_qkv, L1_attn_b_qkv, L1_attn_ln_gamma, L1_attn_ln_beta, L1_ffn_gate_w, L1_ffn_shared_gate_w, L1_ffn_shared_gate_up_w, L1_ffn_shared_down_w, L1_ffn_expert_gate_up_w, L1_ffn_expert_down_w):
    import jax
    import jax.numpy as jnp

    def _L0_xattn_ref(x, context, Wq, Wk, Wv, Wout, bout):
        import jax, jax.numpy as jnp
        import numpy as np
        HEADS = 8
        DIM_HEAD = 64
        SCALE = DIM_HEAD ** (-0.5)
        b, n, _ = x.shape
        m = context.shape[1]
        q = (x @ Wq).reshape(b, n, HEADS, DIM_HEAD)
        k = (context @ Wk).reshape(b, m, HEADS, DIM_HEAD)
        v = (context @ Wv).reshape(b, m, HEADS, DIM_HEAD)
        sim = jnp.einsum('bihd,bjhd->bhij', q, k) * SCALE
        attn = jax.nn.softmax(sim, axis=-1)
        out = jnp.einsum('bhij,bjhd->bihd', attn, v).reshape(b, n, HEADS * DIM_HEAD)
        return out @ Wout + bout

    def _L0_attn_ref(x, P_Q, P_K, P_V, P_O):
        import jax, jax.numpy as jnp
        import numpy as np
        D_MODEL = 256
        NUM_HEADS = 16
        D_K = D_MODEL // NUM_HEADS
        THETA = 10000.0
        BATCH = 4
        SEQ = 512

        def rope(x, positions, theta=THETA):
            d_k = x.shape[-1]
            inv_freq = theta ** (-jnp.arange(0, d_k, 2, dtype=jnp.float32) / d_k)
            ang = positions[:, None].astype(jnp.float32) * inv_freq[None, :]
            cos, sin = (jnp.cos(ang), jnp.sin(ang))
            x1 = x[..., 0::2]
            x2 = x[..., 1::2]
            r1 = x1 * cos - x2 * sin
            r2 = x1 * sin + x2 * cos
            out = jnp.stack([r1, r2], axis=-1).reshape(x.shape)
            return out.astype(x.dtype)
        B, S, _ = x.shape
        positions = jnp.arange(S)

        def proj(P):
            y = jnp.einsum('bsd,ed->bse', x, P)
            return y.reshape(B, S, NUM_HEADS, D_K).transpose(0, 2, 1, 3)
        Q = rope(proj(P_Q), positions)
        K = rope(proj(P_K), positions)
        V = proj(P_V)
        scores = jnp.einsum('bhqd,bhkd->bhqk', Q, K) / jnp.sqrt(jnp.asarray(D_K, x.dtype))
        causal = jnp.tril(jnp.ones((S, S), dtype=bool))
        scores = jnp.where(causal, scores, jnp.asarray(-jnp.inf, scores.dtype))
        attn = jax.nn.softmax(scores, axis=-1)
        out = jnp.einsum('bhqk,bhkd->bhqd', attn, V)
        out = out.transpose(0, 2, 1, 3).reshape(B, S, NUM_HEADS * D_K)
        return jnp.einsum('bse,de->bsd', out, P_O)

    def _L0_ffn_ref(x, w1, b1, w2, b2):
        import jax, jax.numpy as jnp
        import numpy as np
        MANT_BITS = 8
        _PWL_X = jnp.linspace(-4.0, 4.0, 33, dtype=jnp.float32)
        _PWL_Y = 0.5 * _PWL_X * (1.0 + jax.lax.erf(_PWL_X / jnp.sqrt(jnp.float32(2.0))))

        def float2fix(x, mantissa_bits):
            s = jnp.float32(2.0 ** mantissa_bits)
            q = jnp.round(x * s) / s
            return x + jax.lax.stop_gradient(q - x)

        def pwlin_gelu_basic(x, mantissa_bits_in, mantissa_bits_out):
            xq = float2fix(x, mantissa_bits_in)
            y = jnp.interp(xq, _PWL_X, _PWL_Y)
            y = jnp.where(xq > 4.0, xq, jnp.where(xq < -4.0, jnp.float32(0.0), y))
            return float2fix(y, mantissa_bits_out)
        h = jnp.einsum('bsd,df->bsf', x, w1) + b1
        h = float2fix(h, MANT_BITS)
        h = pwlin_gelu_basic(h, MANT_BITS, MANT_BITS)
        h = float2fix(h, MANT_BITS)
        out = jnp.einsum('bsf,fd->bsd', h, w2) + b2
        return float2fix(out, MANT_BITS)

    def _L1_xattn_ref(x, context, Wq, Wk, Wv, Wo, bo):
        import jax, jax.numpy as jnp
        import numpy as np
        HEADS = 16
        DIM_HEAD = 64
        SCALE = DIM_HEAD ** (-0.5)
        QUERY_DIM = 256
        CONTEXT_DIM = 192
        INNER_DIM = HEADS * DIM_HEAD
        B, Nq, _ = x.shape
        Nk = context.shape[1]
        q = x @ Wq
        k = context @ Wk
        v = context @ Wv
        q = q.reshape(B, Nq, HEADS, DIM_HEAD).transpose(0, 2, 1, 3)
        k = k.reshape(B, Nk, HEADS, DIM_HEAD).transpose(0, 2, 1, 3)
        v = v.reshape(B, Nk, HEADS, DIM_HEAD).transpose(0, 2, 1, 3)
        sim = jnp.einsum('bhid,bhjd->bhij', q, k) * SCALE
        attn = jax.nn.softmax(sim, axis=-1)
        out = jnp.einsum('bhij,bhjd->bhid', attn, v)
        out = out.transpose(0, 2, 1, 3).reshape(B, Nq, INNER_DIM)
        return out @ Wo + bo

    def _L1_attn_ref(x, w_qkv, b_qkv, ln_gamma, ln_beta):
        import jax, jax.numpy as jnp
        import numpy as np
        D_MODEL = 256
        NHEAD = 16
        HEAD_DIM = D_MODEL // NHEAD
        LN_EPS = 1e-05

        def _layer_norm(x, gamma, beta):
            mu = jnp.mean(x, axis=-1, keepdims=True)
            var = jnp.mean(jnp.square(x - mu), axis=-1, keepdims=True)
            return (x - mu) * jax.lax.rsqrt(var + LN_EPS) * gamma + beta
        B, L, _ = x.shape
        x_norm = _layer_norm(x, ln_gamma, ln_beta)
        qkv = x_norm @ w_qkv.T + b_qkv
        qkv = qkv.reshape(B, L, 3, NHEAD, HEAD_DIM)
        qkv = jnp.transpose(qkv, (2, 0, 3, 1, 4))
        q, k, v = (qkv[0], qkv[1], qkv[2])
        scale = 1.0 / np.sqrt(HEAD_DIM).astype(np.float32)
        scores = jnp.einsum('bhqd,bhkd->bhqk', q, k) * scale
        attn = jax.nn.softmax(scores, axis=-1)
        out = jnp.einsum('bhqk,bhkd->bhqd', attn, v)
        out = jnp.transpose(out, (0, 2, 1, 3)).reshape(B, L, D_MODEL)
        return out

    def _L1_ffn_ref(hidden_states, gate_w, shared_gate_w, shared_gate_up_w, shared_down_w, expert_gate_up_w, expert_down_w):
        import jax, jax.numpy as jnp
        import numpy as np
        TOP_K = 8
        CAPACITY = 128

        def _silu(x):
            return x * jax.nn.sigmoid(x)
        B, S, H = hidden_states.shape
        x = hidden_states.reshape(-1, H)
        T = x.shape[0]
        E = gate_w.shape[1]
        Is = shared_gate_up_w.shape[1] // 2
        I = expert_gate_up_w.shape[2] // 2
        gu = x @ shared_gate_up_w
        shared = _silu(gu[:, :Is]) * gu[:, Is:] @ shared_down_w
        shared = shared * jax.nn.sigmoid(x @ shared_gate_w)
        logits = x @ gate_w
        probs = jax.nn.softmax(logits.astype(jnp.float32), axis=-1)
        w, idx = jax.lax.top_k(probs, TOP_K)
        w = (w / jnp.sum(w, axis=-1, keepdims=True)).astype(x.dtype)
        e_flat = idx.reshape(-1)
        w_flat = w.reshape(-1)
        A = e_flat.shape[0]
        tok = jnp.arange(A) // TOP_K
        onehot = jax.nn.one_hot(e_flat, E, dtype=jnp.int32)
        pos = jnp.take_along_axis(jnp.cumsum(onehot, axis=0) - 1, e_flat[:, None], axis=1)[:, 0]
        slot = jnp.minimum(pos, CAPACITY)
        buf = jnp.zeros((E, CAPACITY + 1, H), x.dtype).at[e_flat, slot].set(x[tok])
        gu_e = jnp.einsum('ech,ehf->ecf', buf, expert_gate_up_w)
        act = _silu(gu_e[..., :I]) * gu_e[..., I:]
        out_e = jnp.einsum('eci,eih->ech', act, expert_down_w)
        y = out_e[e_flat, slot] * w_flat[:, None]
        y = jnp.where((pos < CAPACITY)[:, None], y, jnp.zeros_like(y))
        y = y.reshape(T, TOP_K, H).sum(axis=1)
        return (y + shared).reshape(B, S, H)
    x = x + _L0_xattn_ref(_layernorm(x, axis=-1), ctx_768, L0_xattn_Wq, L0_xattn_Wk, L0_xattn_Wv, L0_xattn_Wout, L0_xattn_bout)
    x = x + _L0_attn_ref(_layernorm(x, axis=-1), L0_attn_P_Q, L0_attn_P_K, L0_attn_P_V, L0_attn_P_O)
    x = x + _L0_ffn_ref(_layernorm(x, axis=-1), L0_ffn_w1, L0_ffn_b1, L0_ffn_w2, L0_ffn_b2)
    x = x + _L1_xattn_ref(_layernorm(x, axis=-1), ctx_768, L1_xattn_Wq, L1_xattn_Wk, L1_xattn_Wv, L1_xattn_Wo, L1_xattn_bo)
    x = x + _L1_attn_ref(_layernorm(x, axis=-1), L1_attn_w_qkv, L1_attn_b_qkv, L1_attn_ln_gamma, L1_attn_ln_beta)
    x = x + _L1_ffn_ref(_layernorm(x, axis=-1), L1_ffn_gate_w, L1_ffn_shared_gate_w, L1_ffn_shared_gate_up_w, L1_ffn_shared_down_w, L1_ffn_expert_gate_up_w, L1_ffn_expert_down_w)
    return x

_drawn_inputs = setup_inputs


def setup_inputs(seed=0):
    import zlib

    import numpy as np

    out = dict(_drawn_inputs(seed))
    spreads = {'L1_xattn_bo': (0.0, 0.1), 'L1_attn_ln_gamma': (1.0, 0.2), 'L1_attn_ln_beta': (0.0, 0.1)}
    factors = {'L0_xattn_bout': 5.173,
     'L0_attn_P_Q': 41.315,
     'L0_attn_P_K': 39.381,
     'L0_attn_P_V': 8.0,
     'L0_attn_P_O': 8.0,
     'L0_ffn_b1': 5.004,
     'L0_ffn_b2': 3.184,
     'L1_attn_b_qkv': 6.355}
    for name, (base, spread) in spreads.items():
        noise = np.random.default_rng([zlib.crc32(name.encode()), seed]).standard_normal(out[name].shape)
        drawn = base * np.exp(spread * noise) if base else spread * noise
        out[name] = jnp.asarray(drawn.astype(out[name].dtype))
    for name, factor in factors.items():
        out[name] = (out[name] * factor).astype(out[name].dtype)
    return out
```

```python
from contextlib import ExitStack

import numpy as np

import concourse.bass as bass
from concourse import mybir

F32 = mybir.dt.float32
F16 = mybir.dt.float16
ALU = mybir.AluOpType
ACT = mybir.ActivationFunctionType
AXX = mybir.AxisListType.X

P = 128
B, S, D = 8, 64, 256
T = B * S
NT = T // P
NK = 1601
CD = 192
C0, C1 = 128, 64
KT = (NK + P - 1) // P
KL = NK - (KT - 1) * P
NH = 16
DK = D // NH
FF = 1024
E, IE, ISH = 64, 128, 512
TOPK, CAPACITY = 8, 128
EPS = 1e-5
ROUND = 1.5 * 2.0 ** 23
PHASES = 6


def rope_tables():
    freq = np.float32(10000.0) ** (-np.arange(0, DK, 2, dtype=np.float32) / np.float32(DK))
    ang = np.arange(S, dtype=np.float32)[:, None] * freq.astype(np.float32)[None, :]
    cos, sin = np.cos(ang).astype(np.float32), np.sin(ang).astype(np.float32)
    c = np.zeros((DK, S), np.float32)
    s = np.zeros((DK, S), np.float32)
    c[0::2], c[1::2] = cos.T, cos.T
    s[0::2], s[1::2] = -sin.T, sin.T
    return np.tile(c, (P // DK, 1)), np.tile(s, (P // DK, 1))


def perceiver(nc, a, out):
    with ExitStack() as ctx:
        def sb(name, floats, dt=F32):
            return ctx.enter_context(nc.sbuf_tensor(name, [P, floats], dt))

        def sem(name):
            return ctx.enter_context(nc.semaphore(name))

        X_ = sb("X", NT * D)
        X = X_[:, :].rearrange("p (t d) -> p t d", t=NT)
        xnT_ = sb("xnT", 2 * T)
        xnT = xnT_[:, :].rearrange("p (k n) -> p k n", k=2)
        QA = sb("QA", 8 * B * P)
        QB = sb("QB", 8 * B * P)
        A = sb("A", 8 * T)
        CX = sb("CX", 2 * 3 * 1602, F16)
        CR = sb("CR", 2 * KT * 386, F16)
        raw0 = sb("raw0", 1602)
        raw1 = sb("raw1", 1602)
        rawR = sb("rawR", KT * CD)
        Pr = sb("Pr", 2 * 1602)
        PT = sb("PT", 2 * KT * P, F16)
        On = sb("On", CD)
        WVO = sb("WVO", 4096)
        WQK = sb("WQK", 4096)
        bias_row = sb("bias_row", D)
        ident = sb("ident", P)
        cosT = sb("cosT", S)
        sinT = sb("sinT", S)
        cmask = sb("cmask", S)
        small = sb("small", 512)
        PS = ctx.enter_context(nc.psum_tensor("PS", [P, 8, 512], F32))

        XN = A[:, 0:NT * D].rearrange("p (t d) -> p t d", t=NT)
        stats = small[:, 0:24].rearrange("p (t s) -> p t s", t=NT)
        mv = small[:, 24:32].rearrange("p (t s) -> p t s", t=NT)
        std = small[:, 32:36]
        rstd = small[:, 36:40]
        eps_c = small[:, 40:41]
        nmax = small[:, 42:44]
        rden = small[:, 44:45]
        b1_c = small[:, 48:56]
        gel0 = small[:, 56:57]
        gel1 = small[:, 57:58]

        s_const = sem("s_const")
        s_x = sem("s_x")
        s_memset = sem("s_memset")
        vch = sem("vch")
        ach = sem("ach")
        gch = sem("gch")
        count = {"v": 0, "a": 0, "g": 0}

        def vlink(eng, ins):
            count["v"] += 1
            ins.then_inc(vch, 1)
            eng.wait_ge(vch, count["v"])

        def glink(eng, ins):
            count["g"] += 1
            ins.then_inc(gch, 1)
            eng.wait_ge(gch, count["g"])

        LN = {k: sem(f"ln_{k}") for k in ("var", "std", "xn", "T", "xnT")}
        NORMS = {n: (i + (i > 4), NT * i) for i, n in enumerate(("l0x", "l0a", "l0f", "l1x", "l1a", "l1m"))}

        def ln_vector(v, n, affine=None):
            z, (norms, tiles) = LN, NORMS[n]
            src = X
            for rnd in range(2 if affine else 1):
                for t in range(NT):
                    i = v.bn_stats(stats[:, t, :], src[:, t, :])
                vlink(v, i)
                for t in range(NT):
                    i = v.bn_aggr(mv[:, t, :], stats[:, t, :])
                i.then_inc(z["var"], 1)
                v.wait_ge(z["std"], norms + rnd + 1)
                vlink(v, v.reciprocal(rstd, std))
                for t in range(NT):
                    i = v.tensor_scalar(XN[:, t, :], src[:, t, :], mv[:, t, 0:1], rstd[:, t:t + 1],
                                        ALU.subtract, ALU.mult)
                    if affine:
                        vlink(v, i)
                    else:
                        i.then_inc(z["xn"], 1)
                src = XN
            if affine:
                gamma, beta, landed = affine
                v.wait_ge(landed, 32)
                for t in range(NT):
                    vlink(v, v.tensor_tensor(XN[:, t, :], XN[:, t, :], gamma, ALU.mult))
                    v.tensor_tensor(XN[:, t, :], XN[:, t, :], beta, ALU.add).then_inc(z["xn"], 1)

        def ln_scalar(s, n, rounds=1):
            z, (norms, tiles) = LN, NORMS[n]
            for r in range(rounds):
                s.wait_ge(z["var"], norms + r + 1)
                s.activation(std, mv[:, :, 1], ACT.Sqrt, bias=eps_c).then_inc(z["std"], 1)
            for t in range(NT):
                s.wait_ge(z["T"], tiles + t + 1)
                s.copy(xnT[:, :, t * P:(t + 1) * P],
                       PS[:, 6 + t % 2, 0:2 * P].rearrange("p (k n) -> p k n", k=2)).then_inc(z["xnT"], 1)

        def ln_tensor(pe, n):
            z, (norms, tiles) = LN, NORMS[n]
            if n == "l0x":
                pe.wait_ge(s_const, 16 * 6)
            for t in range(NT):
                pe.wait_ge(z["xn"], tiles + t + 1)
                if t >= 2:
                    pe.wait_ge(z["xnT"], tiles + t - 1)
                for k in range(2):
                    i = pe.transpose(PS[:, 6 + t % 2, k * P:(k + 1) * P], XN[:, t, k * P:(k + 1) * P], ident[:, :])
                i.then_inc(z["T"], 1)
            pe.wait_ge(z["xnT"], tiles + NT)

        class Cross:

            def __init__(self, n, heads, g0):
                self.wqk = sem(f"{n}_wqk")
                self.wvo = sem(f"{n}_wvo")
                self.bias = sem(f"{n}_bias")
                self.q = sem(f"{n}_q")
                self.qT = sem(f"{n}_qT")
                self.w = sem(f"{n}_w")
                self.wA = sem(f"{n}_wA")
                self.wV = sem(f"{n}_wV")
                self.scores = sem(f"{n}_scores")
                self.nmax = sem(f"{n}_nmax")
                self.exp = sem(f"{n}_exp")
                self.tr = sem(f"{n}_tr")
                self.head = sem(f"{n}_head")
                self.rest = sem(f"{n}_rest")
                self.pv = sem(f"{n}_pv")
                self.on = sem(f"{n}_on")
                self.otr = sem(f"{n}_otr")
                self.oT = sem(f"{n}_oT")
                self.av = sem(f"{n}_av")
                self.ao = sem(f"{n}_ao")
                self.y = sem(f"{n}_y")
                self.yx = sem(f"{n}_yx")
                self.raw = sem(f"{n}_raw")
                self.prep = sem(f"{n}_prep")
                self.n, self.heads, self.np, self.g0 = n, heads, heads // 2, g0
                self.inner = heads * 64
                self.wq = WQK[:, 0:2 * self.inner].rearrange("p (k n) -> p k n", k=2)
                self.wk = WQK[:, 2 * self.inner:2 * self.inner + self.np * 256].rearrange("p (j c) -> p j c", c=256)
                self.wv = WVO[:, 0:2 * self.inner].rearrange("p (k n) -> p k n", k=2)
                self.wo = WVO[:, 2 * self.inner:2 * self.inner + self.np * D].rearrange("p (j n) -> p j n", n=D)
                self.xq = A[:, 0:self.np * T].rearrange("p (j n) -> p j n", j=self.np)
                nu = B * self.np
                self.qa = QA[:, 0:nu * P].bitcast(F16).rearrange("p (u s c) -> p u s c", s=2, c=P)
                self.qb = QB[:, 0:nu * P].bitcast(F16).rearrange("p (u s c) -> p u s c", s=2, c=P)
                self.qa6 = self.qa.rearrange("p (b j) s (h q) -> p b j s h q", b=B, h=2)
                self.qb6 = self.qb.rearrange("p (b j) s (h q) -> p b j s h q", b=B, h=2)
                self.oa = QA[:, 0:nu * P].rearrange("p (u c) -> p u c", c=P)
                self.ob = QB[0:C1, 0:nu * P].rearrange("p (u c) -> p u c", c=P)
                self.oa5 = self.oa.rearrange("p (b j) (h q) -> p b j h q", b=B, h=2)
                self.ob5 = self.ob.rearrange("p (b j) (h q) -> p b j h q", b=B, h=2)

        def raw_loads(sp, L):
            for b in range(B):
                g = L.g0 + b
                if g:
                    sp.wait_ge(L.prep if b else L0.prep, 6 * b if b else 6 * B)
                sp.dma_start(raw0[:, 0:NK], a["ctxT"][b, 0:C0, :]).then_inc(L.raw, 16)
                sp.dma_start(raw1[0:C1, 0:NK], a["ctxT"][b, C0:CD, :]).then_inc(L.raw, 16)
                sp.dma_start(raw1[C1:P, 0:NK], a["ctxT"][b, C0:CD, :]).then_inc(L.raw, 16)
                sp.dma_start(rawR[:, 0:(KT - 1) * CD].rearrange("p (t c) -> p t c", c=CD),
                             a["ctx"][b, 0:(KT - 1) * P, :].rearrange("(t p) c -> p t c", p=P)).then_inc(L.raw, 16)
                sp.dma_start(rawR[0:KL, (KT - 1) * CD:], a["ctx"][b, (KT - 1) * P:, :]).then_inc(L.raw, 16)

        def split_context(g_, L):
            for b in range(B):
                par = (L.g0 + b) % 2
                if b:
                    g_.wait_ge(L.prep, 6 * b)
                cx = CX[:, par * 3 * 1602:(par + 1) * 3 * 1602].rearrange("p (s n) -> p s n", s=3)
                cr = CR[:, par * KT * 386:(par + 1) * KT * 386].rearrange("p (t n) -> p t n", t=KT)
                g_.wait_ge(L.raw, 80 * (b + 1))
                if b >= 2:
                    g_.wait_ge(L.pv, L.np * (b - 1))
                elif L.g0:
                    g_.wait_ge(L0.pv, L0.np * (B - 1 + b))
                rr = rawR[:, :].rearrange("p (t c) -> p t c", c=CD)
                n = [0]

                def done(i):
                    n[0] += 1
                    i.then_inc(L.prep, 1)

                done(g_.tensor_copy(cx[:, 0, 0:NK], raw0[:, 0:NK]))
                done(g_.tensor_copy(cx[:, 2, 0:NK], raw1[:, 0:NK]))
                done(g_.tensor_copy(cr[:, :, 0:CD], rr))
                g_.wait_ge(L.prep, 6 * b + 3)
                done(g_.tensor_tensor(cx[:, 1, 0:NK], raw0[:, 0:NK], cx[:, 0, 0:NK], ALU.subtract))
                g_.wait_ge(L.prep, 6 * b + 4)
                done(g_.tensor_tensor(cx[C1:P, 2, 0:NK], raw1[C1:P, 0:NK], cx[C1:P, 2, 0:NK], ALU.subtract))
                g_.wait_ge(L.prep, 6 * b + 5)
                done(g_.tensor_tensor(cr[:, :, CD + 1:2 * CD + 1], rr, cr[:, :, 0:CD], ALU.subtract))

        def queries_tensor(pe, L):
            pe.wait_ge(L.wqk, 48)
            for j in range(L.np):
                if j >= 2:
                    pe.wait_ge(L.qT, j - 1)
                for k in range(2):
                    i = pe.matmul(PS[:, j % 2, :], L.wq[:, k, j * P:(j + 1) * P], xnT[:, k, :],
                                  start=(k == 0), stop=(k == 1))
                i.then_inc(L.q, 1)
            for h in range(L.heads):
                j, o = h // 2, 64 * (h % 2)
                pe.wait_ge(L.qT, L.np)
                if h >= 2:
                    pe.wait_ge(L.wA, 2 * (h - 1))
                    pe.wait_ge(L.wV, 2 * (h - 1))
                for c in range(2):
                    i = pe.matmul(PS[:, 2 + 2 * (h % 2) + c, :], L.wk[o:o + 64, j, c * P:(c + 1) * P],
                                  L.xq[o:o + 64, j, :], start=True, stop=True)
                    i.then_inc(L.w, 1)

        def queries_scalar(s, L):
            for j in range(L.np):
                s.wait_ge(L.q, j + 1)
                s.activation(L.xq[:, j, :], PS[:, j % 2, :], ACT.Copy, scale=0.125).then_inc(L.qT, 1)
            for h in range(L.heads):
                for c, q6 in ((0, L.qa6), (1, L.qb6)):
                    s.wait_ge(L.w, 2 * h + c + 1)
                    s.copy(q6[:, :, h // 2, 0, h % 2, :],
                           PS[:, 2 + 2 * (h % 2) + c, :].rearrange("p (b q) -> p b q", b=B)).then_inc(L.wA, 1)

        def queries_vector(v, L):
            for h in range(L.heads):
                for c, q6 in ((0, L.qa6), (1, L.qb6)):
                    v.wait_ge(L.wA, 2 * h + c + 1)
                    v.tensor_tensor(q6[:, :, h // 2, 1, h % 2, :],
                                    PS[:, 2 + 2 * (h % 2) + c, :].rearrange("p (b q) -> p b q", b=B),
                                    q6[:, :, h // 2, 0, h % 2, :], ALU.subtract).then_inc(L.wV, 1)

        CH = [(0, 512), (512, 512), (1024, 512), (1536, NK - 1536)]
        PSf = PS[:, :, :].rearrange("p b n -> p (b n)")
        scores_ps = PSf[:, 0:NK]
        pv_ps = PS[:, 7, 0:2 * CD + 1]
        HGR = [(0, 4, 4, 0), (4, 8, 5, 0), (8, 12, 6, 0), (12, 13, 4, 256)]

        def cx_of(par):
            return CX[:, par * 3 * 1602:(par + 1) * 3 * 1602].rearrange("p (s n) -> p s n", s=3)

        def cr_of(par):
            return CR[:, par * KT * 386:(par + 1) * KT * 386].rearrange("p (t n) -> p t n", t=KT)

        PASSES = 5

        def scores(pe, L, b, u, par, first, n):
            cx = cx_of(par)
            if n == 0 and isinstance(u, int) and u == 0:
                pe.wait_ge(L.wA, 2 * L.heads)
                pe.wait_ge(L.wV, 2 * L.heads)
            if n == 0 and first:
                pe.wait_ge(L.prep, 6 * (b + 1))
            if n == 0 and not (isinstance(u, int) and u == 0):
                pe.wait_ge(L.exp, 2 * u)
            q, hr, c = [(L.qa, 0, 0), (L.qa, 0, 1), (L.qa, 1, 0), (L.qb, 0, 2), (L.qb, 1, 2)][n]
            for o, w in CH:
                i = pe.matmul(PSf[:, o:o + w], q[:, u, hr, :], cx[:, c, o:o + w],
                              start=(n == 0), stop=(n == PASSES - 1))
            if n == PASSES - 1:
                i.then_inc(L.scores, 1)

        def transposes(pe, L, u, parity, k):
            pr = Pr[:, parity * 1602:parity * 1602 + NK]
            lo, hi, bank, col = HGR[k]
            for t in range(lo, hi):
                w = min(P, NK - t * P)
                i = pe.transpose(PS[0:w, bank, col + (t - lo) * P:col + (t - lo + 1) * P],
                                 pr[:, t * P:t * P + w], ident[:, :])
            i.then_inc(L.tr, 1)

        def turn_result(pe, L, u):
            pe.wait_ge(L.on, u + 1)
            pe.transpose(PS[:, 4, 0:P], On[:, 0:C0], ident[:, :])
            pe.transpose(PS[0:C1, 4, P:2 * P], On[:, C0:CD], ident[:, :]).then_inc(L.otr, 1)

        pt = PT[:, :].rearrange("p (s t q) -> p s t q", s=2, t=KT)

        def attend(pe, L, u, par, k):
            cr = cr_of(par)
            lo, hi, _, _ = HGR[k]
            pe.wait_ge(L.rest, 4 * u + k + 1)
            for t in range(lo, hi):
                w = min(P, NK - t * P)
                pe.matmul(pv_ps, pt[0:w, 0, t, :], cr[0:w, t, 0:2 * CD + 1], start=(t == 0), stop=False)
                i = pe.matmul(pv_ps[:, 0:CD + 1], pt[0:w, 1, t, :], cr[0:w, t, 0:CD + 1],
                              start=False, stop=(t == KT - 1))
            if k == 3:
                i.then_inc(L.pv, 1)

        def turn_most(pe, L, u, parity, prev):
            if prev:
                pe.wait_ge(L.rest, 4 * u)
                pe.wait_ge(L.oT, u - 1)
            pe.wait_ge(L.exp, 2 * u + 1)
            transposes(pe, L, u, parity, 0)
            transposes(pe, L, u, parity, 1)
            pe.wait_ge(L.exp, 2 * u + 2)
            transposes(pe, L, u, parity, 2)

        def turn_last(pe, L, u, parity, prev):
            pe.wait_ge(L.rest, 4 * u + 1)
            if prev:
                turn_result(pe, L, u - 1)
            transposes(pe, L, u, parity, 3)

        def unit_scalar_exp(s, L, u, parity):
            s.wait_ge(L.nmax, u + 1)
            if not isinstance(u, int) or u > 1:
                s.wait_ge(L.tr, 4 * (u - 1))
            for lo, hi in ((0, 1024), (1024, NK)):
                s.activation(Pr[:, parity * 1602 + lo:parity * 1602 + hi], PSf[:, lo:hi], ACT.Exp,
                             bias=nmax[:, parity:parity + 1]).then_inc(L.exp, 1)

        def unit_scalar_heads(s, L, u):
            if not isinstance(u, int) or u > 0:
                s.wait_ge(L.pv, u)
            for k, (lo, hi, bank, col) in enumerate(HGR):
                s.wait_ge(L.tr, 4 * u + k + 1)
                w = P if k < 3 else KL
                s.copy(pt[0:w, 0, lo:hi, :], PS[0:w, bank, col:col + (hi - lo) * P].rearrange("p (t q) -> p t q", q=P))\
                    .then_inc(L.head, 1)

        def unit_vector_max(v, L, u, parity):
            v.wait_ge(L.scores, u + 1)
            v.tensor_reduce(nmax[:, parity:parity + 1], scores_ps, AXX, ALU.max, negate=True).then_inc(L.nmax, 1)

        def unit_vector_rests(v, L, u):
            for k, (lo, hi, bank, col) in enumerate(HGR):
                v.wait_ge(L.head, 4 * u + k + 1)
                w = P if k < 3 else KL
                v.tensor_tensor(pt[0:w, 1, lo:hi, :], PS[0:w, bank, col:col + (hi - lo) * P].rearrange("p (t q) -> p t q", q=P),
                                pt[0:w, 0, lo:hi, :], ALU.subtract).then_inc(L.rest, 1)

        def store_result(v, L, u):
            v.wait_ge(L.otr, u + 1)
            v.tensor_copy(L.oa[:, u, :], PS[:, 4, 0:P])
            v.tensor_copy(L.ob[:, u, :], PS[0:C1, 4, P:2 * P]).then_inc(L.oT, 1)

        def normalise(v, L, u):
            v.wait_ge(L.pv, u + 1)
            v.reciprocal(rden, pv_ps[:, CD:CD + 1]).then_inc(L.yx, 1)
            if not isinstance(u, int) or u > 0:
                v.wait_ge(L.otr, u)
            v.wait_ge(L.yx, 2 * u + 1)
            v.tensor_scalar(On[:, :], pv_ps[:, CD + 1:], rden, None, ALU.mult).then_inc(L.yx, 1)
            v.wait_ge(L.yx, 2 * u + 2)
            v.scalar_tensor_tensor(out=On[:, :], in0=pv_ps[:, 0:CD], scalar=rden, in1=On[:, :],
                                   op0=ALU.mult, op1=ALU.add).then_inc(L.on, 1)

        PAIRS = B // 2

        def over_batch_pairs(eng, first, body):
            with eng.Fori(first, PAIRS - 1) as i:
                body(i * 2, False)
            body(B - 2, True)

        def units_tensor(pe, L):
            n = L.np
            for p in range(PASSES):
                scores(pe, L, 0, 0, 0, True, p)
            turn_most(pe, L, 0, 0, False)

            def pair(b, last, start=False):
                for s_ in range(2 * n):
                    u, x = b * n + s_, s_ + 1
                    prev = not (start and s_ == 0)
                    more = s_ < 2 * n - 1 or not last
                    for p in range(PASSES):
                        if more:
                            scores(pe, L, b + x // n, b * n + x, (x // n) % 2, x % n == 0, p)
                        if p == 0:
                            turn_last(pe, L, u, s_ % 2, prev)
                    if prev:
                        pe.wait_ge(L.on, u)
                    for k in range(4):
                        attend(pe, L, u, s_ // n, k)
                    if more:
                        turn_most(pe, L, u + 1, x % 2, prev)
            pair(0, False, True)
            over_batch_pairs(pe, 1, pair)
            pe.wait_ge(L.oT, B * n - 1)
            turn_result(pe, L, B * n - 1)

        def units_scalar(s, L):
            n = L.np
            unit_scalar_exp(s, L, 0, 0)

            def pair(b, last):
                for s_ in range(2 * n):
                    u = b * n + s_
                    unit_scalar_heads(s, L, u)
                    if s_ < 2 * n - 1 or not last:
                        unit_scalar_exp(s, L, u + 1, (s_ + 1) % 2)
            pair(0, False)
            over_batch_pairs(s, 1, pair)

        def units_vector(v, L):
            n = L.np
            unit_vector_max(v, L, 0, 0)

            def pair(b, last, start=False):
                for s_ in range(2 * n):
                    u = b * n + s_
                    unit_vector_rests(v, L, u)
                    if not (start and s_ == 0):
                        store_result(v, L, u - 1)
                    if s_ < 2 * n - 1 or not last:
                        unit_vector_max(v, L, u + 1, (s_ + 1) % 2)
                    normalise(v, L, u)
            pair(0, False, True)
            over_batch_pairs(v, 1, pair)
            store_result(v, L, B * n - 1)

        def project_tensor(pe, L):
            pe.wait_ge(L.oT, B * L.np)
            pe.wait_ge(L.wvo, 48)
            for j in range(L.np):
                if j >= 2:
                    pe.wait_ge(L.ao, j - 1)
                for h in range(2):
                    c = j * P + h * 64
                    o = PS[h * 64:h * 64 + 64, j % 2, :].rearrange("p (b q) -> p b q", b=B)
                    pe.matmul(o, L.wv[:, 0, c:c + 64], L.oa5[:, :, j, h, :], start=True, stop=False)
                    i = pe.matmul(o, L.wv[0:C1, 1, c:c + 64], L.ob5[:, :, j, h, :], start=False, stop=True)
                i.then_inc(L.av, 1)
            for t in range(NT):
                for j in range(L.np):
                    pe.wait_ge(L.ao, j + 1)
                    i = pe.matmul(PS[:, 2 + t, 0:D], L.xq[:, j, t * P:(t + 1) * P], L.wo[:, j, :],
                                  start=(j == 0), stop=(j == L.np - 1))
                i.then_inc(L.y, 1)

        def project_scalar(s, L):
            for j in range(L.np):
                s.wait_ge(L.av, j + 1)
                s.copy(L.xq[:, j, :], PS[:, j % 2, :]).then_inc(L.ao, 1)

        def project_vector(v, L):
            v.wait_ge(L.bias, 16)
            for t in range(NT):
                v.wait_ge(L.y, t + 1)
                vlink(v, v.tensor_tensor(X[:, t, :], PS[:, 2 + t, 0:D], X[:, t, :], ALU.add))
                vlink(v, v.tensor_tensor(X[:, t, :], X[:, t, :], bias_row[:, :], ALU.add))

        L0 = Cross("l0x", 8, 0)
        L1 = Cross("l1x", 16, B)
        s_out = sem("s_out")
        x_done = sem("x_done")

        def cross_loads_qk(sp, L, w):
            sp.dma_start(L.wq, w["wq"].rearrange("(k p) n -> p k n", p=P)).then_inc(L.wqk, 16)
            wk = w["wkT"].rearrange("(j p) c -> p j c", p=P)
            sp.dma_start(L.wk[:, :, 0:CD], wk).then_inc(L.wqk, 16)
            sp.dma_start(L.wk[:, :, CD:256], wk[:, :, C0:CD]).then_inc(L.wqk, 16)

        def cross_loads_vo(sp, L, w):
            sp.dma_start(L.wv[:, 0, :], w["wv"][0:C0, :]).then_inc(L.wvo, 16)
            sp.dma_start(L.wv[0:C1, 1, :], w["wv"][C0:CD, :]).then_inc(L.wvo, 16)
            sp.dma_start(L.wo, w["wo"].rearrange("(j p) n -> p j n", p=P)).then_inc(L.wvo, 16)


        QT = A[:, 0:2 * T].rearrange("p (f n) -> p f n", f=2)
        KB = A[:, 2 * T:6 * T].rearrange("p (f e n) -> p f e n", f=2, e=2)
        OT = A[:, 6 * T:8 * T].rearrange("p (f n) -> p f n", f=2)
        rt1 = Pr[:, 0:T]
        rt2 = Pr[:, T:2 * T]
        Sm = Pr[:, 0:4 * T]
        PTs = QB[:, 0:4 * T].rearrange("p (g t q) -> p g t q", g=4, t=NT)
        Vb = QB[:, 4 * T:8 * T].rearrange("p (b d) -> p b d", b=B)
        smx = small[:, 128:160]
        ssm = small[:, 160:192]

        class Self:

            def __init__(self, n, rope, w):
                self.wl = sem(f"{n}_wl")
                self.p = sem(f"{n}_p")
                self.pe = sem(f"{n}_pe")
                self.v = sem(f"{n}_v")
                self.ve = sem(f"{n}_ve")
                self.kb = sem(f"{n}_kb")
                self.s = sem(f"{n}_s")
                self.m = sem(f"{n}_m")
                self.ex = sem(f"{n}_ex")
                self.pn = sem(f"{n}_pn")
                self.t = sem(f"{n}_t")
                self.te = sem(f"{n}_te")
                self.o = sem(f"{n}_o")
                self.oe = sem(f"{n}_oe")
                self.y = sem(f"{n}_y")
                self.bias = sem(f"{n}_bias")
                self.n, self.rope, self.w = n, rope, w

        WA = QA[:, 4096:4096 + 6 * 512].rearrange("p (w k n) -> p w k n", w=6, k=2)
        WB = WQK[:, 0:6 * D].rearrange("p (k w n) -> p w k n", k=2, w=3)
        SA = Self("l0a", True, WA)
        SB = Self("l1a", False, WB)
        bq_c = small[:, 64:68]

        def self_tensor(pe, L):
            pe.wait_ge(L.wl, 16 * (6 if L.rope else 2))
            np_ = 4 if L.rope else 2
            for w in range(np_):
                for f in range(2):
                    n = 2 * w + f
                    if n >= 4:
                        pe.wait_ge(L.pe, n - 3)
                    for k in range(2):
                        i = pe.matmul(PS[:, n % 4, :], L.w[:, w, k, f * P:(f + 1) * P], xnT[:, k, :],
                                      start=(k == 0), stop=(k == 1))
                    i.then_inc(L.p, 1)
            for b in range(B):
                if b % 2 == 0 and b >= 4:
                    pe.wait_ge(L.ve, b // 2 - 1)
                for o in range(2):
                    for k in range(2):
                        i = pe.matmul(PS[64 * o:64 * o + 64, 4 + b // 2 % 2, (b % 2) * D:(b % 2 + 1) * D],
                                      xnT[:, k, b * S:(b + 1) * S], L.w[:, np_, k, :],
                                      start=(k == 0), stop=(k == 1))
                if b % 2:
                    i.then_inc(L.v, 1)
            pe.wait_ge(L.pe, 2 * np_)
            for f in range(2):
                pe.wait_ge(L.kb, 2 * (f + 1))
                if f:
                    pe.wait_ge(L.m, f)
                for b in range(B):
                    for g in range(4):
                        i = pe.matmul(PS[64 * (b % 2):64 * (b % 2) + 64, g, (b // 2) * P:(b // 2 + 1) * P]
                                      .rearrange("p (e n) -> p e n", e=2),
                                      QT[32 * g:32 * g + 32, f, b * S:(b + 1) * S],
                                      KB[32 * g:32 * g + 32, f, :, b * S:(b + 1) * S], start=True, stop=True)
                i.then_inc(L.s, 1)
                pe.wait_ge(L.pn, f + 1)
                if f == 0:
                    pe.wait_ge(L.ve, 4)
                for g in range(4):
                    n = 4 * f + g
                    if n >= 2:
                        pe.wait_ge(L.te, n - 1)
                    for t in range(NT):
                        i = pe.transpose(PS[:, 4 + n % 2, t * P:(t + 1) * P],
                                         Sm[:, (g * NT + t) * P:(g * NT + t + 1) * P], ident[:, :])
                    i.then_inc(L.t, 1)
                for g in range(4):
                    pe.wait_ge(L.te, 4 * f + g + 1)
                    for b in range(B):
                        i = pe.matmul(PS[32 * g:32 * g + 32, 6 + f, b * S:(b + 1) * S],
                                      Vb[:, b, f * P + 32 * g:f * P + 32 * g + 32],
                                      PTs[:, g, b // 2, (b % 2) * S:(b % 2 + 1) * S], start=True, stop=True)
                i.then_inc(L.o, 1)
            for t in range(NT):
                pe.wait_ge(L.oe, 2)
                for f in range(2):
                    if L.rope:
                        i = pe.matmul(PS[:, t, 0:D], OT[:, f, t * P:(t + 1) * P], L.w[:, 5, f, :],
                                      start=(f == 0), stop=(f == 1))
                    else:
                        i = pe.transpose(PS[:, t, f * P:(f + 1) * P], OT[:, f, t * P:(t + 1) * P], ident[:, :])
                i.then_inc(L.y, 1)

        def self_scalar(s, L):
            if not L.rope:
                for n in range(4):
                    s.wait_ge(L.p, n + 1)
                    if n == 0:
                        s.wait_ge(L.wl, 32)
                    dst = QT[:, n, :] if n < 2 else Pr[:, 1024 + (n - 2) * T:1024 + (n - 1) * T]
                    s.activation(dst, PS[:, n % 4, :], ACT.Identity, bias=bq_c[:, n:n + 1]).then_inc(L.pe, 1)
            for f in range(2):
                s.wait_ge(L.ex, 2 * f + 1)
                s.activation(Sm, Sm, ACT.Exp).then_inc(L.ex, 1)
                for g in range(4):
                    s.wait_ge(L.t, 4 * f + g + 1)
                    if g == 0 and f:
                        s.wait_ge(L.o, f)
                    s.copy(PTs[:, g, :, :], PS[:, 4 + (4 * f + g) % 2, :].rearrange("p (t q) -> p t q", t=NT))\
                        .then_inc(L.te, 1)
                s.wait_ge(L.o, f + 1)
                s.copy(OT[:, f, :], PS[:, 6 + f, :]).then_inc(L.oe, 1)

        def by_batch(ap):
            return ap.rearrange("p (b q) -> p b q", b=B)

        def over(ap, shape, axis):
            return ap.unsqueeze(axis).to_broadcast(shape)

        def self_vector(v, L):
            if L.rope:
                v.wait_ge(s_const, 16 * 6)
                for w in range(2):
                    for f in range(2):
                        v.wait_ge(L.p, 4 * w + f + 1)
                        v.tensor_tensor(by_batch(rt1), by_batch(PS[:, f, :]), over(cosT[:, :], [P, B, S], 1),
                                        ALU.mult).then_inc(L.pe, 1)
                        v.wait_ge(L.p, 4 * w + f + 3)
                        vlink(v, v.tensor_tensor(by_batch(rt2), by_batch(PS[:, 2 + f, :]),
                                                 over(sinT[:, :], [P, B, S], 1), ALU.mult))
                        if w == 0:
                            vlink(v, v.tensor_tensor(QT[:, f, :], rt1, rt2, ALU.add))
                        else:
                            vlink(v, v.tensor_tensor(rt1, rt1, rt2, ALU.add))
                            for e in range(2):
                                i = v.tensor_scalar(KB[:, f, e, :], rt1, eo[:, e:e + 1], None, ALU.mult)
                                i.then_inc(L.kb, 1)
                            vlink(v, v.memset(small[:, 500:501], 0.0))
                    v.memset(small[:, 501:502], 0.0).then_inc(L.pe, 2)
            else:
                v.wait_ge(L.pe, 4)
                for f in range(2):
                    for e in range(2):
                        v.tensor_scalar(KB[:, f, e, :], Pr[:, 1024 + f * T:1024 + (f + 1) * T], eo[:, e:e + 1],
                                        None, ALU.mult).then_inc(L.kb, 1)
                v.wait_ge(L.bias, 16)
                vlink(v, v.tensor_tensor(bias_row[:, :], bias_row[:, :], vmask[:, :], ALU.mult))
            for n in range(4):
                v.wait_ge(L.v, n + 1)
                vv = PS[:, 4 + n % 2, :].rearrange("p (b d) -> p b d", b=2)
                i = v.tensor_tensor(Vb[:, 2 * n:2 * n + 2, :], vv, over(vmask[:, :], [P, 2, D], 1), ALU.mult)
                if not L.rope:
                    vlink(v, i)
                    i = v.tensor_tensor(Vb[:, 2 * n:2 * n + 2, :], Vb[:, 2 * n:2 * n + 2, :],
                                        over(bias_row[:, :], [P, 2, D], 1), ALU.add)
                i.then_inc(L.ve, 1)
            S3 = Sm.rearrange("p (g k) -> p g k", k=S)
            for f in range(2):
                v.wait_ge(L.s, f + 1)
                if f:
                    v.wait_ge(L.t, 4)
                sp3 = PSf[:, 0:4 * T].rearrange("p (g k) -> p g k", k=S)
                if L.rope:
                    i = v.scalar_tensor_tensor(out=S3, in0=sp3, scalar=0.25, in1=over(cmask[:, :], [P, 32, S], 1),
                                               op0=ALU.mult, op1=ALU.add)
                else:
                    i = v.tensor_scalar(S3, sp3, 0.25, None, ALU.mult)
                i.then_inc(L.m, 1)
                v.wait_ge(L.m, f + 1)
                vlink(v, v.tensor_reduce(smx, S3, AXX, ALU.max))
                v.tensor_tensor(S3, S3, over(smx, [P, 32, S], 2), ALU.subtract).then_inc(L.ex, 1)
                v.wait_ge(L.ex, 2 * f + 2)
                vlink(v, v.tensor_reduce(ssm, S3, AXX, ALU.add))
                vlink(v, v.reciprocal(ssm, ssm))
                v.tensor_tensor(S3, S3, over(ssm, [P, 32, S], 2), ALU.mult).then_inc(L.pn, 1)
            for t in range(NT):
                v.wait_ge(L.y, t + 1)
                vlink(v, v.tensor_tensor(X[:, t, :], PS[:, t, 0:D], X[:, t, :], ALU.add))

        W1 = QB[:, 4096:6144].rearrange("p (k n) -> p k n", k=2)
        W2 = QB[:, 6144:8192].rearrange("p (f n) -> p f n", f=8)
        NF = FF // P
        fb = QA[:, 0:8 * T].rearrange("p (i n) -> p i n", i=8)
        for k in ("f_w", "f_bias", "f_b1", "f_h", "f_a", "f_v", "f_g", "f_n", "f_u", "f_o"):
            LN[k] = sem(k)
        STEP = ROUND * 64

        def ffn_tensor(pe):
            pe.wait_ge(LN["f_w"], 48)
            def up(f):
                if f >= 2:
                    pe.wait_ge(LN["f_a"], f - 1)
                for k in range(2):
                    i = pe.matmul(PS[:, f % 2, :], W1[:, k, f * P:(f + 1) * P], xnT[:, k, :],
                                  start=(k == 0), stop=(k == 1))
                i.then_inc(LN["f_h"], 1)
            up(0)
            for f in range(NF):
                if f + 1 < NF:
                    up(f + 1)
                pe.wait_ge(LN["f_n"], f + 1)
                for t in range(NT):
                    i = pe.matmul(PS[:, 2 + t, 0:D], fb[:, 6 + f % 2, t * P:(t + 1) * P], W2[:, f, :],
                                  start=(f == 0), stop=(f == NF - 1))
                i.then_inc(LN["f_u"], 1)

        def ffn_scalar(s):
            s.wait_ge(LN["f_b1"], 1)
            for f in range(NF):
                s.wait_ge(LN["f_h"], f + 1)
                if f >= 1:
                    s.wait_ge(LN["f_n"], f)
                s.activation(fb[:, 0, :], PS[:, f % 2, :], ACT.Identity, bias=b1_c[:, f:f + 1], scale=256.0)\
                    .then_inc(LN["f_a"], 1)
                s.wait_ge(LN["f_v"], f + 1)
                s.activation(fb[:, 3, :], fb[:, 2, :], ACT.Gelu, bias=gel0, scale=2.0 ** -8)
                s.activation(fb[:, 4, :], fb[:, 2, :], ACT.Gelu, bias=gel1, scale=2.0 ** -8).then_inc(LN["f_g"], 1)

        def ffn_vector(v):
            v.wait_ge(LN["f_w"], 48)
            v.tensor_scalar(b1_c, b1_c, 256.0, None, ALU.mult).then_inc(LN["f_b1"], 1)
            v.wait_ge(LN["f_bias"], 16)
            vlink(v, v.tensor_scalar(bias_row[:, :], bias_row[:, :], 256.0, None, ALU.mult))
            for f in range(NF):
                v.wait_ge(LN["f_a"], f + 1)
                vlink(v, v.tensor_scalar(fb[:, 0, :], fb[:, 0, :], ROUND, ROUND, ALU.add, ALU.subtract))
                vlink(v, v.tensor_scalar(fb[:, 1, :], fb[:, 0, :], -1024.0, 1024.0, ALU.max, ALU.min))
                v.tensor_scalar(fb[:, 2, :], fb[:, 1, :], -31.5, STEP, ALU.add, ALU.add).then_inc(LN["f_v"], 1)
                v.wait_ge(LN["f_v"], f + 1)
                vlink(v, v.scalar_tensor_tensor(out=fb[:, 1, :], in0=fb[:, 2, :], scalar=STEP, in1=fb[:, 1, :],
                                                op0=ALU.subtract, op1=ALU.subtract))
                v.wait_ge(LN["f_g"], f + 1)
                vlink(v, v.tensor_tensor(fb[:, 4, :], fb[:, 3, :], fb[:, 4, :], ALU.subtract))
                vlink(v, v.scalar_tensor_tensor(out=fb[:, 4, :], in0=fb[:, 4, :], scalar=4.0, in1=fb[:, 1, :],
                                                op0=ALU.mult, op1=ALU.mult))
                vlink(v, v.scalar_tensor_tensor(out=fb[:, 4, :], in0=fb[:, 3, :], scalar=256.0, in1=fb[:, 4, :],
                                                op0=ALU.mult, op1=ALU.add))
                vlink(v, v.tensor_scalar(fb[:, 4, :], fb[:, 4, :], ROUND, ROUND + 1024.0, ALU.add, ALU.subtract))
                if f >= 2:
                    v.wait_ge(LN["f_u"], f - 1)
                v.scalar_tensor_tensor(out=fb[:, 6 + f % 2, :], in0=fb[:, 0, :], scalar=1024.0, in1=fb[:, 4, :],
                                       op0=ALU.max, op1=ALU.add).then_inc(LN["f_n"], 1)
            v.wait_ge(LN["f_u"], NF)
            for t in range(NT):
                z = fb[:, 0, 0:D]
                vlink(v, v.tensor_tensor(z, PS[:, 2 + t, 0:D], bias_row[:, :], ALU.add))
                vlink(v, v.tensor_scalar(z, z, ROUND, ROUND, ALU.add, ALU.subtract))
                vlink(v, v.scalar_tensor_tensor(out=X[:, t, :], in0=z, scalar=1.0 / 256, in1=X[:, t, :],
                                                op0=ALU.mult, op1=ALU.add))

        NS = 8
        slot = QA[:, 0:NS * 768].rearrange("p (s w) -> p s w", s=NS)
        wsh = WQK[:, 1536:3584].rearrange("p (k n) -> p k n", k=2)
        wdn = rawR[:, 0:4 * D].rearrange("p (c n) -> p c n", c=4)
        wrt = rawR[:, 1024:1024 + 2 * 65].rearrange("p (k n) -> p k n", k=2)
        tri = rawR[:, 1280:1280 + 2 * P].rearrange("p (i n) -> p i n", i=2)
        Y = QB[:, 0:NT * D].rearrange("p (t d) -> p t d", t=NT)
        hsh = QB[:, 1024:1024 + 4 * T].rearrange("p (c n) -> p c n", c=4)
        sg = QB[:, 3072:3072 + 2 * T].rearrange("p (i n) -> p i n", i=2)
        hE = QB[:, 4096:4096 + 2 * T].rearrange("p (i n) -> p i n", i=2)
        lg = QB[:, 5120:5120 + NT * E].rearrange("p (t e) -> p t e", t=NT)
        sel = QB[:, 5376:5376 + NT * E].rearrange("p (t e) -> p t e", t=NT)
        wt = QB[:, 5632:5632 + NT * E].rearrange("p (t e) -> p t e", t=NT)
        sgm = small[:, 200:204]
        rm = small[:, 204:208]
        rs = small[:, 208:212]
        top = small[:, 216:248].rearrange("p (t k) -> p t k", t=NT)
        for k in ("m_w", "m_wx", "m_r", "m_rm", "m_re", "m_sel", "m_pos", "m_sh", "m_sg", "m_hs", "m_ys", "m_wt",
                  "e_gu", "e_sg", "e_h", "e_y", "e_acc"):
            LN[k] = sem(k)
        e_w = [sem(f"e_w{n}") for n in range(NS)]

        def router_tensor(pe):
            pe.wait_ge(LN["m_w"], 64)
            for t in range(NT):
                for k in range(2):
                    i = pe.matmul(PS[:, 0, t * P:t * P + 65], xnT[:, k, t * P:(t + 1) * P], wrt[:, k, :],
                                  start=(k == 0), stop=(k == 1))
            i.then_inc(LN["m_r"], 1)
            for c in range(4):
                if c >= 1:
                    pe.wait_ge(LN["m_hs"], c)
                for h in range(2):
                    for k in range(2):
                        i = pe.matmul(PS[:, 2 + h, :], wsh[:, k, h * ISH + c * P:h * ISH + (c + 1) * P], xnT[:, k, :],
                                      start=(k == 0), stop=(k == 1))
                i.then_inc(LN["m_sh"], 1)
            pe.wait_ge(LN["m_hs"], 4)
            for t in range(NT):
                for c in range(4):
                    i = pe.matmul(PS[:, 4 + t, 0:D], hsh[:, c, t * P:(t + 1) * P], wdn[:, c, :],
                                  start=(c == 0), stop=(c == 3))
                i.then_inc(LN["m_ys"], 1)
            pe.wait_ge(LN["m_sel"], 1)
            for t in range(NT):
                for s_ in range(t + 1):
                    i = pe.matmul(PS[:, 1, t * P:t * P + E], tri[:, 0 if s_ == t else 1, :], sel[:, s_, :],
                                  start=(s_ == 0), stop=(s_ == t))
            i.then_inc(LN["m_pos"], 1)

        def router_scalar(s):
            s.wait_ge(LN["m_rm"], 1)
            for t in range(NT):
                i = s.activation(lg[:, t, :], PS[:, 0, t * P:t * P + E], ACT.Exp, bias=rm[:, t:t + 1])
            i.then_inc(LN["m_re"], 1)
            s.activation(sgm, PS[:, 0, :].rearrange("p (t e) -> p t e", t=NT)[:, :, E], ACT.Sigmoid)\
                .then_inc(LN["m_re"], 1)
            for c in range(4):
                s.wait_ge(LN["m_sh"], c + 1)
                if c >= 2:
                    s.wait_ge(LN["m_hs"], c - 1)
                s.activation(sg[:, c % 2, :], PS[:, 2, :], ACT.Silu).then_inc(LN["m_sg"], 1)

        def router_vector(v):
            v.wait_ge(LN["m_r"], 1)
            lp = PS[:, 0, :].rearrange("p (t e) -> p t e", t=NT)[:, :, 0:E]
            v.tensor_reduce(rm, lp, AXX, ALU.max, negate=True).then_inc(LN["m_rm"], 1)
            for c in range(4):
                v.wait_ge(LN["m_sg"], c + 1)
                v.tensor_tensor(hsh[:, c, :], PS[:, 3, :], sg[:, c % 2, :], ALU.mult).then_inc(LN["m_hs"], 1)
            v.wait_ge(LN["m_re"], 1)
            vlink(v, v.tensor_reduce(rs, lg, AXX, ALU.add))
            vlink(v, v.reciprocal(rs, rs))
            vlink(v, v.tensor_tensor(lg, lg, over(rs, [P, NT, E], 2), ALU.mult))
            for t in range(NT):
                i = v.max(top[:, t, :], lg[:, t, :])
            vlink(v, i)
            for t in range(NT):
                i = v.match_replace(sel[:, t, :], top[:, t, :], lg[:, t, :], -1.0)
            vlink(v, i)
            v.tensor_scalar(sel, sel, 0.0, None, ALU.is_lt).then_inc(LN["m_sel"], 1)
            vlink(v, v.tensor_reduce(rs, top, AXX, ALU.add))
            vlink(v, v.reciprocal(rs, rs))
            v.wait_ge(LN["m_sel"], 1)
            vlink(v, v.tensor_tensor(wt, lg, sel, ALU.mult))
            vlink(v, v.tensor_tensor(wt, wt, over(rs, [P, NT, E], 2), ALU.mult))
            v.wait_ge(LN["m_pos"], 1)
            v.scalar_tensor_tensor(out=wt, in0=PS[:, 1, :].rearrange("p (t e) -> p t e", t=NT)[:, :, 0:E],
                                   scalar=float(CAPACITY), in1=wt, op0=ALU.is_lt, op1=ALU.mult).then_inc(LN["m_wt"], 1)
            v.wait_ge(LN["m_re"], 2)
            for t in range(NT):
                v.wait_ge(LN["m_ys"], t + 1)
                v.tensor_scalar(Y[:, t, :], PS[:, 4 + t, 0:D], sgm[:, t:t + 1], None, ALU.mult)\
                    .then_inc(LN["e_acc"], 1)
            v.wait_ge(LN["m_wt"], 1)

        def expert_gate_up(pe, e, n, cycle):
            w = slot[:, n, 0:512].rearrange("p (k f) -> p k f", k=2)
            pe.wait_ge(e_w[n], 32 * (cycle + 1))
            if not isinstance(e, int) or e > 1:
                pe.wait_ge(LN["e_h"], e - 1)
            for h in range(2):
                for k in range(2):
                    i = pe.matmul(PS[:, 2 * (n % 2) + h, :], w[:, k, h * P:(h + 1) * P], xnT[:, k, :],
                                  start=(k == 0), stop=(k == 1))
            i.then_inc(LN["e_gu"], 1)

        def expert_down(pe, e, n):
            pe.wait_ge(LN["e_h"], e + 1)
            pe.wait_ge(LN["e_acc"], 4 * e - 4 + 4 if not isinstance(e, int) else max(4, 4 * e))
            for t in range(NT):
                i = pe.matmul(PS[:, 4 + 2 * (n % 2) + t // 2, (t % 2) * D:(t % 2 + 1) * D],
                              hE[:, n % 2, t * P:(t + 1) * P], slot[:, n, 512:768], start=True, stop=True)
                if t % 2:
                    i.then_inc(LN["e_y"], 1)

        def experts(eng, first, rest):
            first()

            def cycle(c, last):
                for n in range(NS):
                    rest(c, n, c * NS + n, n < NS - 1 or not last)
            cycle(0, False)
            with eng.Fori(1, E // NS - 1) as c:
                cycle(c, False)
            cycle(E // NS - 1, True)

        def experts_tensor(pe):
            pe.wait_ge(LN["m_hs"], 4)
            pe.wait_ge(LN["m_wt"], 1)

            def rest(c, n, e, more):
                if more:
                    expert_gate_up(pe, e + 1, (n + 1) % NS, c + (n + 1) // NS)
                expert_down(pe, e, n)
            experts(pe, lambda: expert_gate_up(pe, 0, 0, 0), rest)

        def experts_scalar(s):
            def rest(c, n, e, more):
                s.wait_ge(LN["e_gu"], e + 1)
                if not isinstance(e, int) or e > 1:
                    s.wait_ge(LN["e_h"], e - 1)
                s.activation(sg[:, n % 2, :], PS[:, 2 * (n % 2), :], ACT.Silu).then_inc(LN["e_sg"], 1)
            experts(s, lambda: None, rest)

        def experts_vector(v):
            def act(e, n):
                v.wait_ge(LN["e_sg"], e + 1)
                if not isinstance(e, int) or e > 1:
                    v.wait_ge(LN["e_y"], 2 * (e - 1))
                v.tensor_tensor(hE[:, n % 2, :], PS[:, 2 * (n % 2) + 1, :], sg[:, n % 2, :], ALU.mult)\
                    .then_inc(LN["e_h"], 1)

            def rest(c, n, e, more):
                if more:
                    act(e + 1, (n + 1) % NS)
                v.wait_ge(LN["e_acc"], 4 * e + 4)
                for t in range(NT):
                    if t % 2 == 0:
                        v.wait_ge(LN["e_y"], 2 * e + t // 2 + 1)
                    v.scalar_tensor_tensor(out=Y[:, t, :],
                                           in0=PS[:, 4 + 2 * (n % 2) + t // 2, (t % 2) * D:(t % 2 + 1) * D],
                                           scalar=wt[:, t, bass.ds(e, 1)] if not isinstance(e, int) else wt[:, t, e:e + 1],
                                           in1=Y[:, t, :], op0=ALU.mult, op1=ALU.add).then_inc(LN["e_acc"], 1)
            experts(v, lambda: act(0, 0), rest)
            v.wait_ge(LN["e_acc"], 4 * E + 4)
            for t in range(NT):
                vlink(v, v.tensor_tensor(X[:, t, :], X[:, t, :], Y[:, t, :], ALU.add))

        def experts_sync(sp):
            def rest(c, n, e, more):
                if not isinstance(e, int) or e >= NS:
                    sp.wait_ge(LN["e_y"], 2 * (e - NS) + 2)
                gu = a["L1_ffn_expert_gate_up_w"]
                dn = a["L1_ffn_expert_down_w"]
                ge = gu[bass.ds(e, 1)] if not isinstance(e, int) else gu[e:e + 1]
                de = dn[bass.ds(e, 1)] if not isinstance(e, int) else dn[e:e + 1]
                sp.dma_start(slot[:, n, 0:512].rearrange("p (k f) -> p k f", k=2),
                             ge.rearrange("o (k p) f -> p (o k) f", p=P)).then_inc(e_w[n], 16)
                sp.dma_start(slot[:, n, 512:768], de.rearrange("o p f -> p (o f)")).then_inc(e_w[n], 16)
            experts(sp, lambda: None, rest)

        gam = PT[:, 0:512].bitcast(F32)
        bet = PT[:, 512:1024].bitcast(F32)
        eo = small[:, 70:72]
        vmask = sb("vmask", D)
        s_gb = sem("s_gb")

        block = ctx.enter_context(nc.Block())

        def row(ap):
            return ap.rearrange("(o n) -> o n", o=1).to_broadcast([P, D])

        @block.sync
        def _(sp):
            sp.dma_start(X, a["x"].rearrange("(t p) d -> p t d", p=P)).then_inc(s_x, 16)
            for dst, n in ((ident[:, :], "ident"), (cosT[:, :], "cos"), (sinT[:, :], "sin"), (cmask[:, :], "cmask"),
                           (eo, "eo"), (vmask[:, :], "vmask")):
                sp.dma_start(dst, a[n]).then_inc(s_const, 16)
            w0 = {k: a["L0_xattn_" + n] for k, n in (("wq", "Wq"), ("wkT", "WkT"), ("wv", "Wv"), ("wo", "Wout"))}
            w1 = {k: a["L1_xattn_" + n] for k, n in (("wq", "Wq"), ("wkT", "WkT"), ("wv", "Wv"), ("wo", "Wo"))}
            cross_loads_qk(sp, L0, w0)
            cross_loads_vo(sp, L0, w0)
            sp.dma_start(bias_row[:, :], row(a["L0_xattn_bout"])).then_inc(L0.bias, 16)
            for n, k in enumerate(("PQT", "PQsT", "PKT", "PKsT", "PVT", "POT")):
                sp.dma_start(WA[:, n, :, :], a["L0_attn_" + k].rearrange("(k p) n -> p k n", p=P)).then_inc(SA.wl, 16)
            sp.dma_start(W1, a["L0_ffn_w1"].rearrange("(k p) n -> p k n", p=P)).then_inc(LN["f_w"], 16)
            sp.dma_start(W2, a["L0_ffn_w2"].rearrange("(f p) n -> p f n", p=P)).then_inc(LN["f_w"], 16)
            sp.dma_start(b1_c, a["L0_ffn_b1_cols"]).then_inc(LN["f_w"], 16)
            sp.dma_start(bq_c, a["L1_attn_b_qk_cols"]).then_inc(SB.wl, 16)
            sp.wait_ge(s_memset, 5)
            raw_loads(sp, L0)
            if PHASES > 3:
                sp.wait_ge(L0.w, 2 * L0.heads)
                cross_loads_qk(sp, L1, w1)
            sp.wait_ge(L0.y, NT)
            if PHASES > 3:
                cross_loads_vo(sp, L1, w1)
            if PHASES > 2:
                sp.wait_ge(x_done, 1)
                sp.dma_start(bias_row[:, :], row(a["L0_ffn_b2"])).then_inc(LN["f_bias"], 16)
            if PHASES > 3:
                sp.wait_ge(x_done, 3)
                sp.dma_start(bias_row[:, :], row(a["L1_xattn_bo"])).then_inc(L1.bias, 16)
                raw_loads(sp, L1)
            if PHASES > 4:
                sp.wait_ge(L1.w, 2 * L1.heads)
                sp.dma_start(WQK[:, 0:6 * D].rearrange("p (k n) -> p k n", k=2),
                             a["L1_attn_w_qkvT"].rearrange("(k p) n -> p k n", p=P)).then_inc(SB.wl, 16)
                if PHASES > 5:
                    sp.dma_start(wsh, a["L1_ffn_shared_gate_up_w"].rearrange("(k p) n -> p k n", p=P)).then_inc(LN["m_w"], 16)
                    sp.wait_ge(L1.prep, 6 * B)
                    sp.dma_start(wdn, a["L1_ffn_shared_down_w"].rearrange("(c p) n -> p c n", p=P)).then_inc(LN["m_w"], 16)
                    sp.dma_start(wrt, a["L1_ffn_gates"].rearrange("(k p) n -> p k n", p=P)).then_inc(LN["m_w"], 16)
                    sp.dma_start(tri, a["tri"].rearrange("p (i n) -> p i n", i=2)).then_inc(LN["m_w"], 16)
                sp.wait_ge(L1.pv, B * L1.np)
                sp.wait_ge(L1.rest, 4 * B * L1.np)
                sp.dma_start(gam, row(a["L1_attn_ln_gamma"])).then_inc(s_gb, 16)
                sp.dma_start(bet, row(a["L1_attn_ln_beta"])).then_inc(s_gb, 16)
                sp.wait_ge(x_done, 4)
                sp.dma_start(bias_row[:, :], row(a["L1_attn_b_qkv"][2 * D:3 * D])).then_inc(SB.bias, 16)
            if PHASES > 5:
                experts_sync(sp)
            sp.wait_ge(x_done, PHASES)
            sp.dma_start(out.rearrange("(t p) d -> p t d", p=P), X).then_inc(s_out, 16)
            sp.wait_ge(s_out, 16)

        @block.gpsimd
        def _(g):
            g.memset(CR[:, :].rearrange("p (t n) -> p t n", n=386)[:, :, CD:CD + 1], 1.0).then_inc(s_memset, 1)
            g.memset(rawR[:, (KT - 1) * CD:], 0.0).then_inc(s_memset, 1)
            split_context(g, L0)
            if PHASES > 3:
                split_context(g, L1)

        @block.scalar
        def _(s):
            s.wait_ge(s_memset, 5)
            for n in range(PHASES):
                ln_scalar(s, ("l0x", "l0a", "l0f", "l1x", "l1a", "l1m")[n], 2 if n == 4 else 1)
                if n in (0, 3):
                    L = (L0, L1)[n // 3]
                    queries_scalar(s, L)
                    units_scalar(s, L)
                    project_scalar(s, L)
                elif n in (1, 4):
                    self_scalar(s, (SA, SB)[n // 3])
                elif n == 2:
                    ffn_scalar(s)
                else:
                    router_scalar(s)
                    experts_scalar(s)

        @block.vector
        def _(v):
            v.memset(eps_c, EPS).then_inc(s_memset, 1)
            v.memset(gel0, -STEP / 256).then_inc(s_memset, 1)
            v.memset(gel1, -STEP / 256 + 0.25).then_inc(s_memset, 1)
            v.wait_ge(s_x, 16)
            for n in range(PHASES):
                ln_vector(v, ("l0x", "l0a", "l0f", "l1x", "l1a", "l1m")[n], (gam, bet, s_gb) if n == 4 else None)
                if n in (0, 3):
                    L = (L0, L1)[n // 3]
                    queries_vector(v, L)
                    units_vector(v, L)
                    project_vector(v, L)
                elif n in (1, 4):
                    self_vector(v, (SA, SB)[n // 3])
                elif n == 2:
                    ffn_vector(v)
                else:
                    router_vector(v)
                    experts_vector(v)
                v.memset(small[:, 505:506], 0.0).then_inc(x_done, 1)

        @block.tensor
        def _(pe):
            for n in range(PHASES):
                ln_tensor(pe, ("l0x", "l0a", "l0f", "l1x", "l1a", "l1m")[n])
                if n in (0, 3):
                    L = (L0, L1)[n // 3]
                    queries_tensor(pe, L)
                    units_tensor(pe, L)
                    project_tensor(pe, L)
                elif n in (1, 4):
                    self_tensor(pe, (SA, SB)[n // 3])
                elif n == 2:
                    ffn_tensor(pe)
                else:
                    router_tensor(pe)
                    experts_tensor(pe)


def kernel(**inputs):
    import concourse.bacc as bacc
    from concourse.bass_utils import run_bass_kernel_spmd as run

    i = {k: np.asarray(v) for k, v in inputs.items()}
    cos, sin = rope_tables()
    arrays = {
        "x": i["x"].reshape(T, D),
        "ctx": i["ctx_768"],
        "ctxT": i["ctx_768"].transpose(0, 2, 1),
        "L0_xattn_WkT": i["L0_xattn_Wk"].T,
        "L1_xattn_WkT": i["L1_xattn_Wk"].T,
        "ident": np.eye(P, dtype=np.float32),
        "cos": cos,
        "sin": sin,
        "cmask": np.where(np.arange(S)[None, :] <= (np.arange(P) % S)[:, None], 0.0, -1e30).astype(np.float32),
    }
    swap = np.arange(D) ^ 1
    for n, k in (("PQT", "P_Q"), ("PKT", "P_K"), ("PVT", "P_V"), ("POT", "P_O")):
        arrays["L0_attn_" + n] = i["L0_attn_" + k].T
    arrays["L0_attn_PQsT"] = i["L0_attn_P_Q"][swap].T
    arrays["L0_attn_PKsT"] = i["L0_attn_P_K"][swap].T
    arrays["L0_ffn_b1_cols"] = i["L0_ffn_b1"].reshape(-1, P).T
    arrays["L1_attn_b_qk_cols"] = i["L1_attn_b_qkv"][:2 * D].reshape(-1, P).T
    arrays["L1_ffn_gates"] = np.concatenate([i["L1_ffn_gate_w"], i["L1_ffn_shared_gate_w"]], 1)
    arrays["L1_attn_w_qkvT"] = i["L1_attn_w_qkv"].T
    part, col = np.arange(P), np.arange(D)
    arrays["eo"] = np.stack([part // DK % 2 == 0, part // DK % 2 == 1], 1).astype(np.float32)
    arrays["vmask"] = (col[None, :] // DK % 2 == part[:, None] // S).astype(np.float32)
    arrays["tri"] = np.concatenate([part[:, None] < part[None, :], np.ones((P, P), bool)], 1).astype(np.float32)
    for k in i:
        if k not in ("x", "ctx_768", "L0_xattn_Wk", "L1_xattn_Wk", "L1_attn_w_qkv", "L0_ffn_b1", "L1_ffn_gate_w", "L1_ffn_shared_gate_w") and "_attn_P" not in k:
            arrays[k] = i[k]
    arrays = {k: np.ascontiguousarray(v) for k, v in arrays.items()}
    nc = bacc.Bacc("TRN2", target_bir_lowering=False, num_devices=1)
    a = {k: nc.dram_tensor(k + "_dram", v.shape, F32, kind="ExternalInput").ap() for k, v in arrays.items()}
    out = nc.dram_tensor("out_dram", (T, D), F32, kind="ExternalOutput").ap()
    perceiver(nc, a, out)
    r = run(nc, [{k + "_dram": v for k, v in arrays.items()}], core_ids=[0])
    return r.results[0]["out_dram"].reshape(B, S, D)
```

```python
from contextlib import ExitStack

import numpy as np

import concourse.bass as bass
from concourse import mybir

F32 = mybir.dt.float32
F16 = mybir.dt.float16
BF16 = mybir.dt.bfloat16
ALU = mybir.AluOpType
ACT = mybir.ActivationFunctionType
AXX = mybir.AxisListType.X

P = 128
B, S, D = 8, 64, 256
T = B * S
NT = T // P
NK = 1601
CD = 192
C0, C1 = 128, 64
KT = (NK + P - 1) // P
KL = NK - (KT - 1) * P
NH = 16
DK = D // NH
FF = 1024
E, IE, ISH = 64, 128, 512
TOPK, CAPACITY = 8, 128
EPS = 1e-5
ROUND = 1.5 * 2.0 ** 23
PHASES = 6


def rope_tables():
    freq = np.float32(10000.0) ** (-np.arange(0, DK, 2, dtype=np.float32) / np.float32(DK))
    ang = np.arange(S, dtype=np.float32)[:, None] * freq.astype(np.float32)[None, :]
    cos, sin = np.cos(ang).astype(np.float32), np.sin(ang).astype(np.float32)
    c = np.zeros((DK, S), np.float32)
    s = np.zeros((DK, S), np.float32)
    c[0::2], c[1::2] = cos.T, cos.T
    s[0::2], s[1::2] = -sin.T, sin.T
    return np.tile(c, (P // DK, 1)), np.tile(s, (P // DK, 1))


def perceiver(nc, a, out):
    with ExitStack() as ctx:
        def sb(name, floats, dt=F32):
            return ctx.enter_context(nc.sbuf_tensor(name, [P, floats], dt))

        def sem(name):
            return ctx.enter_context(nc.semaphore(name))

        X_ = sb("X", NT * D)
        X = X_[:, :].rearrange("p (t d) -> p t d", t=NT)
        xnT_ = sb("xnT", 2 * T)
        xnT = xnT_[:, :].rearrange("p (k n) -> p k n", k=2)
        QA = sb("QA", 8 * B * P)
        QB = sb("QB", 8 * B * P)
        A = sb("A", 8 * T)
        CX = sb("CX", 2 * 3 * 1602, F16)
        CR = sb("CR", 2 * KT * 386, F16)
        raw0 = sb("raw0", 1602)
        raw1 = sb("raw1", 1602)
        rawR = sb("rawR", KT * CD)
        Pr = sb("Pr", 2 * 1602)
        PT = sb("PT", 2 * KT * P, F16)
        On = sb("On", CD)
        WVO = sb("WVO", 4096)
        WQK = sb("WQK", 4096)
        bias_rows = sb("bias_rows", 3 * D)
        ident = sb("ident", P)
        cosT = sb("cosT", S)
        sinT = sb("sinT", S)
        cmask = sb("cmask", S)
        mask16 = sb("mask16", S, BF16)
        one16 = sb("one16", P, BF16)
        small = sb("small", 512)
        PS = ctx.enter_context(nc.psum_tensor("PS", [P, 8, 512], F32))

        XN = Pr[:, 0:NT * D].rearrange("p (t d) -> p t d", t=NT)
        stats = small[:, 0:24].rearrange("p (t s) -> p t s", t=NT)
        mv = small[:, 24:32].rearrange("p (t s) -> p t s", t=NT)
        std = small[:, 32:36]
        rstd = small[:, 36:40]
        bias_x0, bias_f, bias_x1 = (bias_rows[:, i * D:(i + 1) * D] for i in range(3))
        eps_c = small[:, 40:41]
        nmax = small[:, 42:44]
        rden = small[:, 44:45]
        b1_c = small[:, 48:56]
        gel0 = small[:, 56:57]
        gel1 = small[:, 57:58]

        s_ident = sem("s_ident")
        s_const = sem("s_const")
        s_x = sem("s_x")
        s_memset = sem("s_memset")
        vch = sem("vch")
        ach = sem("ach")
        gch = sem("gch")
        count = {"v": 0, "a": 0, "g": 0}

        def vmark(ins):
            count["v"] += 1
            ins.then_inc(vch, 1)
            return count["v"]

        def vlink(eng, ins):
            count["v"] += 1
            ins.then_inc(vch, 1)
            eng.wait_ge(vch, count["v"])

        def glink(eng, ins):
            count["g"] += 1
            ins.then_inc(gch, 1)
            eng.wait_ge(gch, count["g"])

        LN = {k: sem(f"ln_{k}") for k in ("var", "std", "xn", "T", "xnT")}
        NORMS = {n: (NT * (i + (i > 4)), NT * i) for i, n in enumerate(("l0x", "l0a", "l0f", "l1x", "l1a", "l1m"))}

        def ln_steps(rounds):
            return [[(k, n - k) for k in range(rounds + 1) if 0 <= n - k < NT] for n in range(NT + rounds)]

        def ln_variance_count(rounds):
            order = [kt for step in ln_steps(rounds) for kt in step if kt[0] < rounds]
            return {kt: n + 1 for n, kt in enumerate(order)}

        def ln_vector(v, n, finish=None, affine=None):
            z, (before, _) = LN, NORMS[n]
            rounds = 2 if affine else 1
            count_of = ln_variance_count(rounds)

            def moments(t, src):
                vlink(v, v.bn_stats(stats[:, t, :], src))
                v.bn_aggr(mv[:, t, :], stats[:, t, :]).then_inc(z["var"], 1)

            for k, t in [kt for step in ln_steps(rounds) for kt in step]:
                if k == 0:
                    if finish:
                        vlink(v, finish(v, t))
                    moments(t, X[:, t, :])
                    continue
                v.wait_ge(z["std"], before + count_of[k - 1, t])
                vlink(v, v.reciprocal(rstd[:, t:t + 1], std[:, t:t + 1]))
                if k < rounds:
                    vlink(v, v.tensor_scalar(XN[:, t, :], X[:, t, :], mv[:, t, 0:1], rstd[:, t:t + 1],
                                             ALU.subtract, ALU.mult))
                    moments(t, XN[:, t, :])
                elif affine:
                    gamma, beta, landed = affine
                    v.wait_ge(landed, 32)
                    vlink(v, v.scalar_tensor_tensor(out=XN[:, t, :], in0=XN[:, t, :], scalar=mv[:, t, 0:1],
                                                    in1=gamma, op0=ALU.subtract, op1=ALU.mult))
                    v.scalar_tensor_tensor(out=XN[:, t, :], in0=XN[:, t, :], scalar=rstd[:, t:t + 1], in1=beta,
                                           op0=ALU.mult, op1=ALU.add).then_inc(z["xn"], 1)
                else:
                    v.tensor_scalar(XN[:, t, :], X[:, t, :], mv[:, t, 0:1], rstd[:, t:t + 1],
                                    ALU.subtract, ALU.mult).then_inc(z["xn"], 1)

        def ln_scalar(s, n, rounds=1):
            z, (before, tiles) = LN, NORMS[n]
            count_of = ln_variance_count(rounds)

            def store(t):
                s.wait_ge(z["T"], tiles + t + 1)
                s.copy(xnT[:, :, t * P:(t + 1) * P],
                       PS[:, 6 + t % 2, 0:2 * P].rearrange("p (k n) -> p k n", k=2)).then_inc(z["xnT"], 1)

            for m, step in enumerate(ln_steps(rounds)):
                for k, t in step:
                    if k < rounds:
                        s.wait_ge(z["var"], before + count_of[k, t])
                        s.activation(std[:, t:t + 1], mv[:, t, 1:2], ACT.Sqrt, bias=eps_c).then_inc(z["std"], 1)
                if m > rounds:
                    store(m - rounds - 1)
            store(NT - 1)

        def ln_tensor(pe, n):
            z, tiles = LN, NORMS[n][1]
            if n == "l0x":
                pe.wait_ge(s_ident, 16)
            for t in range(NT):
                pe.wait_ge(z["xn"], tiles + t + 1)
                if t >= 2:
                    pe.wait_ge(z["xnT"], tiles + t - 1)
                for k in range(2):
                    i = pe.transpose(PS[:, 6 + t % 2, k * P:(k + 1) * P], XN[:, t, k * P:(k + 1) * P], ident[:, :])
                i.then_inc(z["T"], 1)
            pe.wait_ge(z["xnT"], tiles + NT)

        class Cross:

            def __init__(self, n, heads, g0):
                self.wqk = sem(f"{n}_wqk")
                self.wvo = sem(f"{n}_wvo")
                self.bias = sem(f"{n}_bias")
                self.q = sem(f"{n}_q")
                self.qT = sem(f"{n}_qT")
                self.w = sem(f"{n}_w")
                self.wA = sem(f"{n}_wA")
                self.wV = sem(f"{n}_wV")
                self.scores = sem(f"{n}_scores")
                self.nmax = sem(f"{n}_nmax")
                self.exp = sem(f"{n}_exp")
                self.tr = sem(f"{n}_tr")
                self.head = sem(f"{n}_head")
                self.rest = sem(f"{n}_rest")
                self.pv = sem(f"{n}_pv")
                self.on = sem(f"{n}_on")
                self.otr = sem(f"{n}_otr")
                self.oT = sem(f"{n}_oT")
                self.av = sem(f"{n}_av")
                self.ao = sem(f"{n}_ao")
                self.y = sem(f"{n}_y")
                self.yx = sem(f"{n}_yx")
                self.raw = sem(f"{n}_raw")
                self.cast = sem(f"{n}_cast")
                self.prep = sem(f"{n}_prep")
                self.n, self.heads, self.np, self.g0 = n, heads, heads // 2, g0
                self.inner = heads * 64
                self.wq = WQK[:, 0:2 * self.inner].rearrange("p (k n) -> p k n", k=2)
                self.wk = WQK[:, 2 * self.inner:2 * self.inner + self.np * 256].rearrange("p (j c) -> p j c", c=256)
                self.wv = WVO[:, 0:2 * self.inner].rearrange("p (k n) -> p k n", k=2)
                self.wo = WVO[:, 2 * self.inner:2 * self.inner + self.np * D].rearrange("p (j n) -> p j n", n=D)
                self.xq = A[:, 0:self.np * T].rearrange("p (j n) -> p j n", j=self.np)
                nu = B * self.np
                self.qa = QA[:, 0:nu * P].bitcast(F16).rearrange("p (u s c) -> p u s c", s=2, c=P)
                self.qb = QB[:, 0:nu * P].bitcast(F16).rearrange("p (u s c) -> p u s c", s=2, c=P)
                self.qa6 = self.qa.rearrange("p (b j) s (h q) -> p b j s h q", b=B, h=2)
                self.qb6 = self.qb.rearrange("p (b j) s (h q) -> p b j s h q", b=B, h=2)
                self.oa = QA[:, 0:nu * P].rearrange("p (u c) -> p u c", c=P)
                self.ob = QB[0:C1, 0:nu * P].rearrange("p (u c) -> p u c", c=P)
                self.oa5 = self.oa.rearrange("p (b j) (h q) -> p b j h q", b=B, h=2)
                self.ob5 = self.ob.rearrange("p (b j) (h q) -> p b j h q", b=B, h=2)

        def raw_loads(sp, L, batches):
            for b in batches:
                g = L.g0 + b
                if g:
                    sp.wait_ge(L.prep if b else L0.prep, 3 * (b or B))
                sp.dma_start(raw0[:, 0:NK], a["ctxT"][b, 0:C0, :]).then_inc(L.raw, 16)
                sp.dma_start(raw1[0:C1, 0:NK], a["ctxT"][b, C0:CD, :]).then_inc(L.raw, 16)
                sp.dma_start(raw1[C1:P, 0:NK], a["ctxT"][b, C0:CD, :]).then_inc(L.raw, 16)
                sp.dma_start(rawR[:, 0:(KT - 1) * CD].rearrange("p (t c) -> p t c", c=CD),
                             a["ctx"][b, 0:(KT - 1) * P, :].rearrange("(t p) c -> p t c", p=P)).then_inc(L.raw, 16)
                sp.dma_start(rawR[0:KL, (KT - 1) * CD:], a["ctx"][b, (KT - 1) * P:, :]).then_inc(L.raw, 16)

        def cx_of(par):
            return CX[:, par * 3 * 1602:(par + 1) * 3 * 1602].rearrange("p (s n) -> p s n", s=3)

        def cr_of(par):
            return CR[:, par * KT * 386:(par + 1) * KT * 386].rearrange("p (t n) -> p t n", t=KT)

        def context_head(v, L, b, par, n):
            cx, cr = cx_of(par), cr_of(par)
            if n == 0:
                v.wait_ge(L.raw, 80 * (b + 1))
                if not isinstance(b, int) or b >= 2:
                    v.wait_ge(L.pv, L.np * (b - 1))
                elif L.g0:
                    v.wait_ge(L0.pv, L0.np * (B - 1 + b))
            if n == 0:
                i = v.tensor_copy(cx[:, 0, 0:NK], raw0[:, 0:NK])
            elif n == 1:
                i = v.tensor_copy(cx[:, 2, 0:NK], raw1[:, 0:NK])
            else:
                i = v.tensor_copy(cr[:, :, 0:CD], rawR[:, :].rearrange("p (t c) -> p t c", c=CD))
            i.then_inc(L.cast, 1)

        def context_rests(g_, L, batches):
            for b in batches:
                cx, cr = cx_of((L.g0 + b) % 2), cr_of((L.g0 + b) % 2)
                if b or L.g0:
                    g_.wait_ge(L.prep if b else L0.prep, 3 * (b or B))
                g_.wait_ge(L.cast, 3 * b + 1)
                g_.tensor_tensor(cx[:, 1, 0:NK], raw0[:, 0:NK], cx[:, 0, 0:NK], ALU.subtract).then_inc(L.prep, 1)
                g_.wait_ge(L.prep, 3 * b + 1)
                g_.wait_ge(L.cast, 3 * b + 2)
                g_.tensor_tensor(cx[C1:P, 2, 0:NK], raw1[C1:P, 0:NK], cx[C1:P, 2, 0:NK], ALU.subtract)\
                    .then_inc(L.prep, 1)
                g_.wait_ge(L.prep, 3 * b + 2)
                g_.wait_ge(L.cast, 3 * b + 3)
                g_.tensor_tensor(cr[:, :, CD + 1:2 * CD + 1], rawR[:, :].rearrange("p (t c) -> p t c", c=CD),
                                 cr[:, :, 0:CD], ALU.subtract).then_inc(L.prep, 1)

        def queries_tensor(pe, L):
            pe.wait_ge(L.wqk, 48)
            for j in range(L.np):
                if j >= 2:
                    pe.wait_ge(L.qT, j - 1)
                for k in range(2):
                    i = pe.matmul(PS[:, j % 2, :], L.wq[:, k, j * P:(j + 1) * P], xnT[:, k, :],
                                  start=(k == 0), stop=(k == 1))
                i.then_inc(L.q, 1)
            for h in range(L.heads):
                j, o = h // 2, 64 * (h % 2)
                pe.wait_ge(L.qT, L.np)
                if h >= 2:
                    pe.wait_ge(L.wA, 2 * (h - 1))
                    pe.wait_ge(L.wV, 2 * (h - 1))
                for c in range(2):
                    i = pe.matmul(PS[:, 2 + 2 * (h % 2) + c, :], L.wk[o:o + 64, j, c * P:(c + 1) * P],
                                  L.xq[o:o + 64, j, :], start=True, stop=True)
                    i.then_inc(L.w, 1)

        def queries_scalar(s, L):
            for j in range(L.np):
                s.wait_ge(L.q, j + 1)
                s.activation(L.xq[:, j, :], PS[:, j % 2, :], ACT.Copy, scale=0.125).then_inc(L.qT, 1)
            for h in range(L.heads):
                for c, q6 in ((0, L.qa6), (1, L.qb6)):
                    s.wait_ge(L.w, 2 * h + c + 1)
                    s.copy(q6[:, :, h // 2, 0, h % 2, :],
                           PS[:, 2 + 2 * (h % 2) + c, :].rearrange("p (b q) -> p b q", b=B)).then_inc(L.wA, 1)

        def queries_vector(v, L):
            for h in range(L.heads):
                for c, q6 in ((0, L.qa6), (1, L.qb6)):
                    v.wait_ge(L.wA, 2 * h + c + 1)
                    v.tensor_tensor(q6[:, :, h // 2, 1, h % 2, :],
                                    PS[:, 2 + 2 * (h % 2) + c, :].rearrange("p (b q) -> p b q", b=B),
                                    q6[:, :, h // 2, 0, h % 2, :], ALU.subtract).then_inc(L.wV, 1)

        CH = [(0, 512), (512, 512), (1024, 512), (1536, NK - 1536)]
        PSf = PS[:, :, :].rearrange("p b n -> p (b n)")
        scores_ps = PSf[:, 0:NK]
        pv_ps = PS[:, 7, 0:2 * CD + 1]
        HGR = [(0, 4, 4, 0), (4, 8, 5, 0), (8, 12, 6, 0), (12, 13, 4, 256)]

        PASSES = 5

        def scores(pe, L, b, u, par, first, n):
            cx = cx_of(par)
            if n == 0 and isinstance(u, int) and u == 0:
                pe.wait_ge(L.wA, 2 * L.heads)
                pe.wait_ge(L.wV, 2 * L.heads)
            if n == 0 and first:
                pe.wait_ge(L.prep, 3 * (b + 1))
            if n == 0 and not (isinstance(u, int) and u == 0):
                pe.wait_ge(L.exp, 2 * u)
            q, hr, c = [(L.qa, 0, 0), (L.qa, 0, 1), (L.qa, 1, 0), (L.qb, 0, 2), (L.qb, 1, 2)][n]
            for o, w in CH:
                i = pe.matmul(PSf[:, o:o + w], q[:, u, hr, :], cx[:, c, o:o + w],
                              start=(n == 0), stop=(n == PASSES - 1))
            if n == PASSES - 1:
                i.then_inc(L.scores, 1)

        def transposes(pe, L, u, parity, k):
            pr = Pr[:, parity * 1602:parity * 1602 + NK]
            lo, hi, bank, col = HGR[k]
            for t in range(lo, hi):
                w = min(P, NK - t * P)
                i = pe.transpose(PS[0:w, bank, col + (t - lo) * P:col + (t - lo + 1) * P],
                                 pr[:, t * P:t * P + w], ident[:, :])
            i.then_inc(L.tr, 1)

        def turn_result(pe, L, u):
            pe.wait_ge(L.on, u + 1)
            pe.transpose(PS[:, 4, 0:P], On[:, 0:C0], ident[:, :])
            pe.transpose(PS[0:C1, 4, P:2 * P], On[:, C0:CD], ident[:, :]).then_inc(L.otr, 1)

        pt = PT[:, :].rearrange("p (s t q) -> p s t q", s=2, t=KT)

        def attend(pe, L, u, par, k):
            cr = cr_of(par)
            lo, hi, _, _ = HGR[k]
            pe.wait_ge(L.rest, 4 * u + k + 1)
            for t in range(lo, hi):
                w = min(P, NK - t * P)
                pe.matmul(pv_ps, pt[0:w, 0, t, :], cr[0:w, t, 0:2 * CD + 1], start=(t == 0), stop=False)
                i = pe.matmul(pv_ps[:, 0:CD + 1], pt[0:w, 1, t, :], cr[0:w, t, 0:CD + 1],
                              start=False, stop=(t == KT - 1))
            if k == 3:
                i.then_inc(L.pv, 1)

        def turn_most(pe, L, u, parity, prev):
            if prev:
                pe.wait_ge(L.rest, 4 * u)
                pe.wait_ge(L.oT, u - 1)
            pe.wait_ge(L.exp, 2 * u + 1)
            transposes(pe, L, u, parity, 0)
            transposes(pe, L, u, parity, 1)
            pe.wait_ge(L.exp, 2 * u + 2)
            transposes(pe, L, u, parity, 2)

        def turn_last(pe, L, u, parity, prev):
            pe.wait_ge(L.rest, 4 * u + 1)
            if prev:
                turn_result(pe, L, u - 1)
            transposes(pe, L, u, parity, 3)

        def unit_scalar_exp(s, L, u, parity):
            s.wait_ge(L.nmax, u + 1)
            if not isinstance(u, int) or u > 1:
                s.wait_ge(L.tr, 4 * (u - 1))
            for lo, hi in ((0, 1024), (1024, NK)):
                s.activation(Pr[:, parity * 1602 + lo:parity * 1602 + hi], PSf[:, lo:hi], ACT.Exp,
                             bias=nmax[:, parity:parity + 1]).then_inc(L.exp, 1)

        def unit_scalar_heads(s, L, u):
            if not isinstance(u, int) or u > 0:
                s.wait_ge(L.pv, u)
            for k, (lo, hi, bank, col) in enumerate(HGR):
                s.wait_ge(L.tr, 4 * u + k + 1)
                w = P if k < 3 else KL
                s.copy(pt[0:w, 0, lo:hi, :], PS[0:w, bank, col:col + (hi - lo) * P].rearrange("p (t q) -> p t q", q=P))\
                    .then_inc(L.head, 1)

        def unit_vector_max(v, L, u, parity):
            v.wait_ge(L.scores, u + 1)
            v.tensor_reduce(nmax[:, parity:parity + 1], scores_ps, AXX, ALU.max, negate=True).then_inc(L.nmax, 1)

        def unit_vector_rests(v, L, u):
            for k, (lo, hi, bank, col) in enumerate(HGR):
                v.wait_ge(L.head, 4 * u + k + 1)
                w = P if k < 3 else KL
                v.tensor_tensor(pt[0:w, 1, lo:hi, :], PS[0:w, bank, col:col + (hi - lo) * P].rearrange("p (t q) -> p t q", q=P),
                                pt[0:w, 0, lo:hi, :], ALU.subtract).then_inc(L.rest, 1)

        def store_result(v, L, u):
            v.wait_ge(L.otr, u + 1)
            v.tensor_copy(L.oa[:, u, :], PS[:, 4, 0:P])
            v.tensor_copy(L.ob[:, u, :], PS[0:C1, 4, P:2 * P]).then_inc(L.oT, 1)

        def normalise(v, L, u):
            v.wait_ge(L.pv, u + 1)
            v.reciprocal(rden, pv_ps[:, CD:CD + 1]).then_inc(L.yx, 1)
            if not isinstance(u, int) or u > 0:
                v.wait_ge(L.otr, u)
            v.wait_ge(L.yx, 2 * u + 1)
            v.tensor_scalar(On[:, :], pv_ps[:, CD + 1:], rden, None, ALU.mult).then_inc(L.yx, 1)
            v.wait_ge(L.yx, 2 * u + 2)
            v.scalar_tensor_tensor(out=On[:, :], in0=pv_ps[:, 0:CD], scalar=rden, in1=On[:, :],
                                   op0=ALU.mult, op1=ALU.add).then_inc(L.on, 1)

        PAIRS = B // 2

        def over_batch_pairs(eng, first, body):
            with eng.Fori(first, PAIRS - 1) as i:
                body(i * 2, False)
            body(B - 2, True)

        def units_tensor(pe, L):
            n = L.np
            for p in range(PASSES):
                scores(pe, L, 0, 0, 0, True, p)
            turn_most(pe, L, 0, 0, False)

            def pair(b, last, start=False):
                for s_ in range(2 * n):
                    u, x = b * n + s_, s_ + 1
                    prev = not (start and s_ == 0)
                    more = s_ < 2 * n - 1 or not last
                    for p in range(PASSES):
                        if more:
                            scores(pe, L, b + x // n, b * n + x, (x // n) % 2, x % n == 0, p)
                        if p == 0:
                            turn_last(pe, L, u, s_ % 2, prev)
                    if prev:
                        pe.wait_ge(L.on, u)
                    for k in range(4):
                        attend(pe, L, u, s_ // n, k)
                    if more:
                        turn_most(pe, L, u + 1, x % 2, prev)
            pair(0, False, True)
            over_batch_pairs(pe, 1, pair)
            pe.wait_ge(L.oT, B * n - 1)
            turn_result(pe, L, B * n - 1)

        def units_scalar(s, L):
            n = L.np
            unit_scalar_exp(s, L, 0, 0)

            def pair(b, last):
                for s_ in range(2 * n):
                    u = b * n + s_
                    unit_scalar_heads(s, L, u)
                    if s_ < 2 * n - 1 or not last:
                        unit_scalar_exp(s, L, u + 1, (s_ + 1) % 2)
            pair(0, False)
            over_batch_pairs(s, 1, pair)

        def units_vector(v, L):
            n = L.np
            unit_vector_max(v, L, 0, 0)

            def pair(b, last, start=False):
                for s_ in range(2 * n):
                    u = b * n + s_
                    unit_vector_rests(v, L, u)
                    if not (start and s_ == 0):
                        store_result(v, L, u - 1)
                    if s_ < 2 * n - 1 or not last:
                        unit_vector_max(v, L, u + 1, (s_ + 1) % 2)
                    for part in {0: (0, 1), 1: (2,)}.get(s_ % n, ()):
                        if s_ < n or not last:
                            context_head(v, L, b + s_ // n + 1, (s_ // n + 1) % 2, part)
                        elif L is L0 and PHASES > 3:
                            context_head(v, L1, 0, 0, part)
                    normalise(v, L, u)
            pair(0, False, True)
            over_batch_pairs(v, 1, pair)
            store_result(v, L, B * n - 1)

        def project_tensor(pe, L):
            pe.wait_ge(L.oT, B * L.np)
            pe.wait_ge(L.wvo, 48)
            for j in range(L.np):
                if j >= 2:
                    pe.wait_ge(L.ao, j - 1)
                for h in range(2):
                    c = j * P + h * 64
                    o = PS[h * 64:h * 64 + 64, j % 2, :].rearrange("p (b q) -> p b q", b=B)
                    pe.matmul(o, L.wv[:, 0, c:c + 64], L.oa5[:, :, j, h, :], start=True, stop=False)
                    i = pe.matmul(o, L.wv[0:C1, 1, c:c + 64], L.ob5[:, :, j, h, :], start=False, stop=True)
                i.then_inc(L.av, 1)
            for t in range(NT):
                for j in range(L.np):
                    pe.wait_ge(L.ao, j + 1)
                    i = pe.matmul(PS[:, 2 + t, 0:D], L.xq[:, j, t * P:(t + 1) * P], L.wo[:, j, :],
                                  start=(j == 0), stop=(j == L.np - 1))
                i.then_inc(L.y, 1)

        def project_scalar(s, L):
            for j in range(L.np):
                s.wait_ge(L.av, j + 1)
                s.copy(L.xq[:, j, :], PS[:, j % 2, :]).then_inc(L.ao, 1)

        def project_vector(v, L):
            v.wait_ge(L.bias, 16)
            row_ = bias_x1 if L.g0 else bias_x0
            for t in range(NT):
                i = v.tensor_tensor(X[:, t, :], X[:, t, :], row_, ALU.add)
            vlink(v, i)

        def project_finish(L):
            def finish(v, t):
                v.wait_ge(L.y, t + 1)
                return v.tensor_tensor(X[:, t, :], PS[:, 2 + t, 0:D], X[:, t, :], ALU.add)
            return finish

        L0 = Cross("l0x", 8, 0)
        L1 = Cross("l1x", 16, B)
        s_out = sem("s_out")
        x_done = sem("x_done")

        def cross_loads_qk(sp, L, w):
            sp.dma_start(L.wq, w["wq"].rearrange("(k p) n -> p k n", p=P)).then_inc(L.wqk, 16)
            wk = w["wkT"].rearrange("(j p) c -> p j c", p=P)
            sp.dma_start(L.wk[:, :, 0:CD], wk).then_inc(L.wqk, 16)
            sp.dma_start(L.wk[:, :, CD:256], wk[:, :, C0:CD]).then_inc(L.wqk, 16)

        def cross_loads_vo(sp, L, w):
            sp.dma_start(L.wv[:, 0, :], w["wv"][0:C0, :]).then_inc(L.wvo, 16)
            sp.dma_start(L.wv[0:C1, 1, :], w["wv"][C0:CD, :]).then_inc(L.wvo, 16)
            sp.dma_start(L.wo, w["wo"].rearrange("(j p) n -> p j n", p=P)).then_inc(L.wvo, 16)


        QT = A[:, 0:2 * T].rearrange("p (f n) -> p f n", f=2)
        KB = A[:, 2 * T:6 * T].rearrange("p (f e n) -> p f e n", f=2, e=2)
        OT = A[:, 6 * T:8 * T].rearrange("p (f n) -> p f n", f=2)
        blk = Pr[:, 0:6 * T].rearrange("p (i n) -> p i n", i=6)
        PTs = QB[:, 0:4 * T].rearrange("p (g t q) -> p g t q", g=4, t=NT)
        Vb_ = QB[:, 4 * T:8 * T]
        Vb = Vb_.rearrange("p (b d) -> p b d", b=B)
        smx = small[:, 128:160].rearrange("p (i h) -> p i h", i=4)
        ssm = small[:, 160:192].rearrange("p (i h) -> p i h", i=4)
        NG = 8

        class Self:

            def __init__(self, n, rope, w):
                self.wl = sem(f"{n}_wl")
                self.p = sem(f"{n}_p")
                self.pe = sem(f"{n}_pe")
                self.sum = sem(f"{n}_sum")
                self.v = sem(f"{n}_v")
                self.vz = sem(f"{n}_vz")
                self.ve = sem(f"{n}_ve")
                self.qt = sem(f"{n}_qt")
                self.kb = sem(f"{n}_kb")
                self.s = sem(f"{n}_s")
                self.m = sem(f"{n}_m")
                self.ex = sem(f"{n}_ex")
                self.rs = sem(f"{n}_rs")
                self.pn = sem(f"{n}_pn")
                self.t = sem(f"{n}_t")
                self.te = sem(f"{n}_te")
                self.o = sem(f"{n}_o")
                self.oe = sem(f"{n}_oe")
                self.y = sem(f"{n}_y")
                self.n, self.rope, self.w = n, rope, w

        WA = QA[:, 4096:4096 + 6 * 512].rearrange("p (w k n) -> p w k n", w=6, k=2)
        WB = WQK[:, 0:6 * D].rearrange("p (k w n) -> p w k n", k=2, w=3)
        SA = Self("l0a", True, WA)
        SB = Self("l1a", False, WB)
        b_c = small[:, 64:70]
        b_eo = small[:, 72:76].rearrange("p (e f) -> p e f", e=2)
        s_mask = sem("s_mask")

        def block_of(n):
            return blk[:, (n + 2) % 6, :]

        def self_tensor(pe, L):
            pe.wait_ge(L.wl, 16 * (6 if L.rope else 2))
            nw = 4 if L.rope else 2
            for f in range(2):
                for w in range(nw):
                    for k in range(2):
                        i = pe.matmul(PS[:, (4 * f if L.rope else 4 + 2 * f) + w, :], L.w[:, w, k, f * P:(f + 1) * P],
                                      xnT[:, k, :], start=(k == 0), stop=(k == 1))
                    i.then_inc(L.p, 1)

            def scores_of(n):
                f, g = n // 4, n % 4
                if f:
                    pe.wait_ge(L.m, g + 1)
                if L.rope:
                    pe.matmul(PS[:, g, :].rearrange("p (x k) -> p x k", k=S), one16[:, :],
                              mask16[:, :].unsqueeze(1).to_broadcast([P, 8, S]), start=True, stop=False,
                              skip_group_check=True)
                for b in range(B):
                    i = pe.matmul(PS[64 * (b % 2):64 * (b % 2) + 64, g, (b // 2) * P:(b // 2 + 1) * P]
                                  .rearrange("p (e n) -> p e n", e=2),
                                  QT[32 * g:32 * g + 32, f, b * S:(b + 1) * S],
                                  KB[32 * g:32 * g + 32, f, :, b * S:(b + 1) * S], start=not L.rope, stop=True,
                                  skip_group_check=True)
                i.then_inc(L.s, 1)

            def attend_of(n):
                f, g = n // 4, n % 4
                pe.wait_ge(L.te, n + 1)
                if n == 0:
                    pe.wait_ge(L.ve, 8)
                for b in range(B):
                    i = pe.matmul(PS[32 * g:32 * g + 32, 6 + f, b * S:(b + 1) * S],
                                  Vb[:, b, f * P + 32 * g:f * P + 32 * g + 32],
                                  PTs[:, g, b // 2, (b % 2) * S:(b % 2 + 1) * S], start=True, stop=True)
                i.then_inc(L.o, 1)

            if L.rope:
                pe.wait_ge(L.pe, 4)
                pe.wait_ge(s_mask, 2)
            pe.wait_ge(L.sum if L.rope else L.qt, 1)
            pe.wait_ge(L.kb, 2)
            for n in range(4):
                scores_of(n)
            if L.rope:
                pe.wait_ge(L.pe, 8)
            else:
                pe.wait_ge(L.qt, 2)
                pe.wait_ge(L.kb, 4)
            for t in range(NT):
                for k in range(2):
                    i = pe.matmul(PS[:, 6 + t // 2, (t % 2) * D:(t % 2 + 1) * D], xnT[:, k, t * P:(t + 1) * P],
                                  L.w[:, nw, k, :], start=(k == 0), stop=(k == 1))
                if t % 2:
                    i.then_inc(L.v, 1)
            pe.wait_ge(L.sum if L.rope else L.qt, 3 if L.rope else 2)
            pe.wait_ge(L.kb, 4)
            for n in range(NG):
                if n < 4:
                    scores_of(4 + n)
                pe.wait_ge(L.pn, n + 1)
                if n >= 2:
                    pe.wait_ge(L.te, n - 1)
                for t in range(NT):
                    i = pe.transpose(PS[:, 4 + n % 2, t * P:(t + 1) * P], block_of(n)[:, t * P:(t + 1) * P], ident[:, :])
                i.then_inc(L.t, 1)
                if n:
                    attend_of(n - 1)
            attend_of(NG - 1)
            pe.wait_ge(L.oe, 2)
            for t in range(NT):
                for f in range(2):
                    if L.rope:
                        i = pe.matmul(PS[:, t, 0:D], OT[:, f, t * P:(t + 1) * P], L.w[:, 5, f, :],
                                      start=(f == 0), stop=(f == 1))
                    else:
                        i = pe.transpose(PS[:, t, f * P:(f + 1) * P], OT[:, f, t * P:(t + 1) * P], ident[:, :])
                i.then_inc(L.y, 1)

        def self_scalar(s, L):
            for f in range(2):
                if L.rope:
                    s.wait_ge(L.sum, 2 * f + 2)
                    for e in range(2):
                        s.activation(KB[:, f, e, :], blk[:, 2 - 2 * f, :], ACT.Copy, scale=eo[:, e:e + 1])\
                            .then_inc(L.kb, 1)
                else:
                    s.wait_ge(L.p, 2 * f + 1)
                    s.wait_ge(L.wl, 32)
                    s.activation(QT[:, f, :], PS[:, 4 + 2 * f, :], ACT.Identity, bias=b_c[:, f:f + 1]).then_inc(L.qt, 1)

            def exponentials(n):
                s.wait_ge(L.m, n + 1)
                s.activation(block_of(n), block_of(n), ACT.Exp, scale=0.25).then_inc(L.ex, 1)

            def store_turned(n):
                s.wait_ge(L.t, n + 1)
                if n >= 4:
                    s.wait_ge(L.o, n - 3)
                s.copy(PTs[:, n % 4, :, :], PS[:, 4 + n % 2, :].rearrange("p (t q) -> p t q", t=NT)).then_inc(L.te, 1)

            def store_output(f):
                s.wait_ge(L.o, 4 * f + 4)
                if L.rope:
                    s.copy(OT[:, f, :], PS[:, 6 + f, :]).then_inc(L.oe, 1)
                else:
                    s.activation(OT[:, f, :], PS[:, 6 + f, :], ACT.Identity, bias=b_c[:, 4 + f:5 + f]).then_inc(L.oe, 1)

            for n in range(4):
                exponentials(n)
            s.wait_ge(L.vz, 1)
            for half in range(2):
                s.wait_ge(L.v, half + 1)
                for o in range(2):
                    for bb in range(2):
                        src = PS[64 * bb:64 * bb + 64, 6 + half, :].rearrange("p (t h o d) -> p t h o d", t=2, o=2, d=DK)
                        dst = Vb_[64 * o:64 * o + 64, half * 4 * D:(half + 1) * 4 * D]\
                            .rearrange("p (t b h o d) -> p t b h o d", t=2, b=2, o=2, d=DK)
                        s.copy(dst[:, :, bb, :, o, :], src[:, :, :, o, :]).then_inc(L.ve, 1)
            for n in range(4):
                store_turned(n)
                exponentials(4 + n)
            store_turned(4)
            store_turned(5)
            store_output(0)
            store_turned(6)
            store_turned(7)
            store_output(1)

        def by_batch(ap):
            return ap.rearrange("p (b q) -> p b q", b=B)

        def over(ap, shape, axis):
            return ap.unsqueeze(axis).to_broadcast(shape)

        PARTS = ((0, 1), (2, 3), (4, 5), (0, 1))

        def self_vector(v, L):
            if L.rope:
                v.wait_ge(s_const, 16 * 4)
                v.tensor_copy(mask16[:, :], cmask[:, :]).then_inc(s_mask, 1)
                v.tensor_copy(one16[:, :], ident[:, :]).then_inc(s_mask, 1)
                for n in range(4):
                    if n == 3:
                        v.wait_ge(L.sum, 1)
                    for i, table in enumerate((cosT, sinT)):
                        v.wait_ge(L.p, 2 * n + i + 1)
                        v.tensor_tensor(by_batch(blk[:, PARTS[n][i], :]), by_batch(PS[:, 2 * n + i, :]),
                                        over(table[:, :], [P, B, S], 1), ALU.mult).then_inc(L.pe, 1)
            else:
                v.wait_ge(L.wl, 32)
                for e in range(2):
                    i = v.tensor_scalar(b_eo[:, e, :], b_c[:, 2:4], eo[:, e:e + 1], None, ALU.mult)
                vlink(v, i)
                for f in range(2):
                    v.wait_ge(L.p, 2 * f + 2)
                    for e in range(2):
                        v.tensor_scalar(KB[:, f, e, :], PS[:, 5 + 2 * f, :], eo[:, e:e + 1], b_eo[:, e, f:f + 1],
                                        ALU.mult, ALU.add).then_inc(L.kb, 1)

            def less_maxima(n):
                sc = PS[:, n % 4, :].rearrange("p (h k) -> p h k", k=S)
                v.wait_ge(L.s, n + 1)
                vlink(v, v.tensor_reduce(smx[:, n % 4, :], sc, AXX, ALU.max))
                if L.rope and n == 2:
                    v.wait_ge(L.sum, 3)
                if n >= 6:
                    v.wait_ge(L.t, n - 5)
                v.tensor_tensor(block_of(n).rearrange("p (h k) -> p h k", k=S), sc,
                                over(smx[:, n % 4, :], [P, 8, S], 2), ALU.subtract).then_inc(L.m, 1)

            def sums(n):
                v.wait_ge(L.ex, n + 1)
                if n >= 4:
                    v.wait_ge(L.pn, n - 3)
                vlink(v, v.tensor_reduce(ssm[:, n % 4, :], block_of(n).rearrange("p (h k) -> p h k", k=S), AXX, ALU.add))
                v.reciprocal(ssm[:, n % 4, :], ssm[:, n % 4, :]).then_inc(L.rs, 1)

            for n in range(NG + 1):
                if n < NG:
                    less_maxima(n)
                if n:
                    sums(n - 1)

        def self_gpsimd(g, L, cross):
            g.wait_ge(cross.av, cross.np)
            g.memset(Vb_, 0.0).then_inc(L.vz, 1)
            if L.rope:
                for n in range(4):
                    g.wait_ge(L.pe, 2 * n + 2)
                    one, two = (blk[:, i, :] for i in PARTS[n])
                    i = g.tensor_tensor(one if n % 2 else QT[:, n // 2, :], one, two, ALU.add)
                    i.then_inc(L.sum, 1)
            for n in range(NG):
                g.wait_ge(L.rs, n + 1)
                p3 = block_of(n).rearrange("p (h k) -> p h k", k=S)
                g.tensor_tensor(p3, p3, over(ssm[:, n % 4, :], [P, 8, S], 2), ALU.mult).then_inc(L.pn, 1)

        def self_finish(L):
            def finish(v, t):
                v.wait_ge(L.y, t + 1)
                return v.tensor_tensor(X[:, t, :], PS[:, t, 0:D], X[:, t, :], ALU.add)
            return finish

        W1 = QB[:, 4096:6144].rearrange("p (k n) -> p k n", k=2)
        W2 = QB[:, 6144:8192].rearrange("p (f n) -> p f n", f=8)
        NF = FF // P
        fbuf = QA[:, 0:16 * T].rearrange("p (i n) -> p i n", i=16)
        F_C, F_B, F_G0, F_D, F_Y, F_O, F_N = (0, 3), (3, 2), (5, 2), (7, 2), (9, 1), (10, 2), (12, 4)

        def fb(f, place):
            first, copies = place
            return fbuf[:, first + f % copies, :]

        for k in ("f_w", "f_bias", "f_b1", "f_h", "f_a", "f_v", "f_g", "f_d", "f_n", "f_u", "f_o"):
            LN[k] = sem(k)
        STEP = ROUND * 64

        def ffn_tensor(pe):
            pe.wait_ge(LN["f_w"], 48)
            def up(f):
                if f >= 4:
                    pe.wait_ge(LN["f_a"], f - 3)
                for k in range(2):
                    i = pe.matmul(PS[:, (0, 1, 6, 7)[f % 4], :], W1[:, k, f * P:(f + 1) * P], xnT[:, k, :],
                                  start=(k == 0), stop=(k == 1))
                i.then_inc(LN["f_h"], 1)
            for f in range(NF + 3):
                if f < NF:
                    up(f)
                if f >= 3:
                    c = f - 3
                    pe.wait_ge(LN["f_n"], c + 1)
                    for t in range(NT):
                        i = pe.matmul(PS[:, 2 + t, 0:D], fb(c, F_O)[:, t * P:(t + 1) * P], W2[:, c, :],
                                      start=(c == 0), stop=(c == NF - 1))
                    i.then_inc(LN["f_u"], 1)

        def ffn_scalar(s):
            s.wait_ge(LN["f_b1"], 1)

            def hidden(f):
                s.wait_ge(LN["f_h"], f + 1)
                if f >= 4:
                    s.wait_ge(LN["f_n"], f - 3)
                s.activation(fb(f, F_N), PS[:, (0, 1, 6, 7)[f % 4], :], ACT.Identity, bias=b1_c[:, f:f + 1], scale=256.0)\
                    .then_inc(LN["f_a"], 1)
            hidden(0)
            for f in range(NF):
                if f + 1 < NF:
                    hidden(f + 1)
                s.wait_ge(LN["f_v"], f + 1)
                s.activation(fb(f, F_G0), fb(f, F_B), ACT.Gelu, bias=gel0, scale=2.0 ** -8)
                s.activation(fb(f, F_D), fb(f, F_B), ACT.Gelu, bias=gel1, scale=2.0 ** -8).then_inc(LN["f_g"], 1)

        def ffn_vector(v):
            v.wait_ge(LN["f_w"], 48)
            v.tensor_scalar(b1_c, b1_c, 256.0, None, ALU.mult).then_inc(LN["f_b1"], 1)
            v.wait_ge(LN["f_bias"], 16)
            vlink(v, v.tensor_scalar(bias_f, bias_f, 256.0, None, ALU.mult))
            for f in range(NF + 2):
                g = f - 2
                if f < NF:
                    v.wait_ge(LN["f_a"], f + 1)
                    rounded = vmark(v.tensor_scalar(fb(f, F_N), fb(f, F_N), ROUND, ROUND, ALU.add, ALU.subtract))
                if g >= 0:
                    v.wait_ge(LN["f_d"], g + 1)
                    product = vmark(v.scalar_tensor_tensor(out=fb(g, F_D), in0=fb(g, F_D), scalar=4.0,
                                                           in1=fb(g, F_C), op0=ALU.mult, op1=ALU.mult))
                if f < NF:
                    v.wait_ge(vch, rounded)
                    clamped = vmark(v.tensor_scalar(fb(f, F_C), fb(f, F_N), -1024.0, 1024.0, ALU.max, ALU.min))
                if g >= 0:
                    v.wait_ge(vch, product)
                    total = vmark(v.scalar_tensor_tensor(out=fb(g, F_Y), in0=fb(g, F_G0), scalar=256.0,
                                                         in1=fb(g, F_D), op0=ALU.mult, op1=ALU.add))
                if f < NF:
                    v.wait_ge(vch, clamped)
                    v.tensor_scalar(fb(f, F_B), fb(f, F_C), -31.5, STEP, ALU.add, ALU.add).then_inc(LN["f_v"], 1)
                if g >= 0:
                    v.wait_ge(vch, total)
                    less = vmark(v.tensor_scalar(fb(g, F_Y), fb(g, F_Y), ROUND, ROUND + 1024.0,
                                                 ALU.add, ALU.subtract))
                if f < NF:
                    v.wait_ge(LN["f_v"], f + 1)
                    vmark(v.scalar_tensor_tensor(out=fb(f, F_C), in0=fb(f, F_B), scalar=STEP, in1=fb(f, F_C),
                                                 op0=ALU.subtract, op1=ALU.subtract))
                if g >= 0:
                    v.wait_ge(vch, less)
                    if g >= 2:
                        v.wait_ge(LN["f_u"], g - 1)
                    v.scalar_tensor_tensor(out=fb(g, F_O), in0=fb(g, F_N), scalar=1024.0, in1=fb(g, F_Y),
                                           op0=ALU.max, op1=ALU.add).then_inc(LN["f_n"], 1)

        def ffn_gpsimd(g_):
            for f in range(NF):
                g_.wait_ge(LN["f_g"], f + 1)
                g_.tensor_tensor(fb(f, F_D), fb(f, F_G0), fb(f, F_D), ALU.subtract).then_inc(LN["f_d"], 1)

        def ffn_finish(v, t):
            v.wait_ge(LN["f_u"], NF)
            z = fbuf[:, t, 0:D]
            vlink(v, v.tensor_tensor(z, PS[:, 2 + t, 0:D], bias_f, ALU.add))
            vlink(v, v.tensor_scalar(z, z, ROUND, ROUND, ALU.add, ALU.subtract))
            return v.scalar_tensor_tensor(out=X[:, t, :], in0=z, scalar=1.0 / 256, in1=X[:, t, :],
                                          op0=ALU.mult, op1=ALU.add)

        NS = 8
        slot = QA[:, 0:NS * 768].rearrange("p (s w) -> p s w", s=NS)
        wsh = WQK[:, 1536:3584].rearrange("p (k n) -> p k n", k=2)
        wdn = rawR[:, 0:4 * D].rearrange("p (c n) -> p c n", c=4)
        wrt = rawR[:, 1024:1024 + 2 * 65].rearrange("p (k n) -> p k n", k=2)
        tri = rawR[:, 1280:1280 + 2 * P].rearrange("p (i n) -> p i n", i=2)
        hsh = QB[:, 1024:1024 + 4 * T].rearrange("p (c n) -> p c n", c=4)
        sg = QB[:, 3072:3072 + 2 * T].rearrange("p (i n) -> p i n", i=2)
        wthl = QB[:, 4096:4096 + NT * E].bitcast(F16).rearrange("p (t e s) -> p t e s", t=NT, s=2)
        posm = QB[:, 4352:4352 + NT * E].rearrange("p (t e) -> p t e", t=NT)
        xh = PT[:, 0:NT * D].rearrange("p (t d) -> p t d", t=NT)
        xl = PT[:, NT * D:2 * NT * D].rearrange("p (t d) -> p t d", t=NT)
        iota = rawR[:, 1536:1600].bitcast(F16)
        id16 = rawR[:, 1600:1664].bitcast(F16)
        hf = rawR[:, 1664:1920].rearrange("p (i n) -> p i n", i=2)
        oh = raw0[:, 0:512].bitcast(F16).rearrange("p (i t n) -> p i t n", i=2, t=NT)
        oht = raw0[:, 512:1536].bitcast(F16).rearrange("p (i n) -> p i n", i=4)
        xg = raw1[:, 0:512].bitcast(F16).rearrange("p (i s k n) -> p i s k n", i=2, s=2, k=2)
        sl = raw1[:, 512:768].rearrange("p (i n) -> p i n", i=2)
        hh = raw1[:, 768:1024].bitcast(F16).rearrange("p (i s n) -> p i s n", i=2, s=2)
        oo = raw1[:, 1024:1536].bitcast(F16).rearrange("p (i s n) -> p i s n", i=2, s=2)
        wh = Pr[:, 0:3072].bitcast(F16).rearrange("p (i s w) -> p i s w", i=4, s=2)
        wsl = small[:, 250:254]
        lg = QB[:, 5120:5120 + NT * E].rearrange("p (t e) -> p t e", t=NT)
        sel = QB[:, 5376:5376 + NT * E].rearrange("p (t e) -> p t e", t=NT)
        wt = QB[:, 5632:5632 + NT * E].rearrange("p (t e) -> p t e", t=NT)
        sgm = small[:, 200:204]
        rm = small[:, 204:208]
        rs = small[:, 208:212]
        top = small[:, 216:248].rearrange("p (t k) -> p t k", t=NT)
        for k in ("m_w", "m_r", "m_rm", "m_re", "m_sel", "m_pos", "m_sh", "m_sg", "m_hs", "m_ys", "m_yd", "m_wt", "m_xh",
                  "m_xl"):
            LN[k] = sem(k)
        e_oh = sem("e_oh")
        e_turn = sem("e_turn")
        e_oht = sem("e_oht")
        e_gather = sem("e_gather")
        e_xg = sem("e_xg")
        e_cast = sem("e_cast")
        e_split = sem("e_split")
        e_gu = sem("e_gu")
        e_silu = sem("e_silu")
        e_hf = sem("e_hf")
        e_hh = sem("e_hh")
        e_hl = sem("e_hl")
        e_out = sem("e_out")
        e_ohi = sem("e_ohi")
        e_ol = sem("e_ol")
        e_comb = sem("e_comb")
        e_w = [sem(f"e_w{n}") for n in range(NS)]

        SHB = (2, 4)

        def router_tensor(pe):
            pe.wait_ge(LN["m_w"], 96)
            for t in range(NT):
                for k in range(2):
                    i = pe.matmul(PS[:, 0, t * P:t * P + 65], xnT[:, k, t * P:(t + 1) * P], wrt[:, k, :],
                                  start=(k == 0), stop=(k == 1))
            i.then_inc(LN["m_r"], 1)
            for c in range(4):
                if c == 3:
                    pe.wait_ge(LN["m_sel"], 1)
                    for t in range(NT):
                        for s_ in range(t + 1):
                            i = pe.matmul(PS[:, 1, t * P:t * P + E], tri[:, 0 if s_ == t else 1, :], sel[:, s_, :],
                                          start=(s_ == 0), stop=(s_ == t))
                    i.then_inc(LN["m_pos"], 1)
                if c >= 2:
                    pe.wait_ge(LN["m_hs"], c - 1)
                for h in range(2):
                    for k in range(2):
                        i = pe.matmul(PS[:, SHB[c % 2] + h, :], wsh[:, k, h * ISH + c * P:h * ISH + (c + 1) * P],
                                      xnT[:, k, :], start=(k == 0), stop=(k == 1))
                i.then_inc(LN["m_sh"], 1)
            pe.wait_ge(LN["m_hs"], 4)
            for t in range(NT):
                for c in range(4):
                    i = pe.matmul(PS[:, 6 + t // 2, (t % 2) * D:(t % 2 + 1) * D], hsh[:, c, t * P:(t + 1) * P],
                                  wdn[:, c, :], start=(c == 0), stop=(c == 3))
                if t % 2:
                    i.then_inc(LN["m_ys"], 1)

        def router_scalar(s):
            s.wait_ge(LN["m_rm"], 1)
            for t in range(NT):
                i = s.activation(lg[:, t, :], PS[:, 0, t * P:t * P + E], ACT.Exp, bias=rm[:, t:t + 1])
            i.then_inc(LN["m_re"], 1)
            s.activation(sgm, PS[:, 0, :].rearrange("p (t e) -> p t e", t=NT)[:, :, E], ACT.Exp, scale=-1.0)\
                .then_inc(LN["m_re"], 1)
            for c in range(4):
                s.wait_ge(LN["m_sh"], c + 1)
                if c >= 2:
                    s.wait_ge(LN["m_hs"], c - 1)
                s.activation(sg[:, c % 2, :], PS[:, SHB[c % 2], :], ACT.Silu).then_inc(LN["m_sg"], 1)

        def router_vector(v):
            v.wait_ge(LN["m_r"], 1)
            lp = PS[:, 0, :].rearrange("p (t e) -> p t e", t=NT)[:, :, 0:E]
            v.tensor_reduce(rm, lp, AXX, ALU.max, negate=True).then_inc(LN["m_rm"], 1)
            v.tensor_copy(xh, XN).then_inc(LN["m_xh"], 1)

            def shared_hidden(c):
                v.wait_ge(LN["m_sg"], c + 1)
                v.tensor_tensor(hsh[:, c, :], PS[:, SHB[c % 2] + 1, :], sg[:, c % 2, :], ALU.mult)\
                    .then_inc(LN["m_hs"], 1)
            v.wait_ge(LN["m_re"], 1)
            vlink(v, v.tensor_reduce(rs, lg, AXX, ALU.add))
            vlink(v, v.reciprocal(rs, rs))
            vlink(v, v.tensor_tensor(lg, lg, over(rs, [P, NT, E], 2), ALU.mult))
            for t in range(NT):
                i = v.max(top[:, t, :], lg[:, t, :])
            vlink(v, i)
            for t in range(NT):
                i = v.match_replace(sel[:, t, :], top[:, t, :], lg[:, t, :], -1.0)
            vlink(v, i)
            v.tensor_scalar(sel, sel, 0.0, None, ALU.is_lt).then_inc(LN["m_sel"], 1)
            shared_hidden(0)
            vlink(v, v.tensor_reduce(rs, top, AXX, ALU.add))
            vlink(v, v.reciprocal(rs, rs))
            v.wait_ge(LN["m_sel"], 1)
            vlink(v, v.tensor_tensor(wt, lg, sel, ALU.mult))
            vlink(v, v.tensor_tensor(wt, wt, over(rs, [P, NT, E], 2), ALU.mult))
            shared_hidden(1)
            shared_hidden(2)
            v.wait_ge(LN["m_pos"], 1)
            pos = PS[:, 1, :].rearrange("p (t e) -> p t e", t=NT)[:, :, 0:E]
            vlink(v, v.scalar_tensor_tensor(out=sel, in0=pos, scalar=float(CAPACITY), in1=sel,
                                            op0=ALU.is_lt, op1=ALU.mult))
            vlink(v, v.scalar_tensor_tensor(out=posm, in0=pos, scalar=1.0, in1=sel, op0=ALU.add, op1=ALU.mult))
            v.tensor_scalar(posm, posm, -1.0, None, ALU.add).then_inc(LN["m_wt"], 1)
            vlink(v, v.tensor_tensor(wt, wt, sel, ALU.mult))
            vlink(v, v.tensor_copy(wthl[:, :, :, 0], wt))
            v.tensor_tensor(wthl[:, :, :, 1], wt, wthl[:, :, :, 0], ALU.subtract).then_inc(LN["m_wt"], 1)
            shared_hidden(3)
            v.wait_ge(LN["m_re"], 2)
            vlink(v, v.tensor_scalar(sgm, sgm, 1.0, None, ALU.add))
            vlink(v, v.reciprocal(sgm, sgm))

        def add_shared(v):
            for t in range(NT):
                v.wait_ge(LN["m_ys"], t // 2 + 1)
                v.scalar_tensor_tensor(out=X[:, t, :], in0=PS[:, 6 + t // 2, (t % 2) * D:(t % 2 + 1) * D],
                                       scalar=sgm[:, t:t + 1], in1=X[:, t, :], op0=ALU.mult, op1=ALU.add)\
                    .then_inc(LN["m_yd"], 1)

        def after(eng, sm, n):
            if not isinstance(n, int) or n > 0:
                eng.wait_ge(sm, n)

        def expert_turn_and_gather(pe, e, n):
            after(pe, e_oh, e + 1)
            after(pe, e_oht, e)
            ids = bass.ds(e, 1) if not isinstance(e, int) else slice(e, e + 1)
            for t in range(NT):
                pe.matmul(PS[:, 4, 256:258], oh[:, n % 2, t, :],
                          wthl[:, t, ids, :].rearrange("p e s -> p (e s)"), start=(t == 0), stop=(t == NT - 1))
            t16 = PS[:, 4, 0:256].bitcast(F16)
            for t in range(NT):
                i = pe.transpose(t16[:, t * P:(t + 1) * P], oh[:, n % 2, t, :], id16)
            i.then_inc(e_turn, 1)
            after(pe, e_xg, e - 1)
            for m, x in ((0, xh), (1, xl)):
                for k in range(2):
                    for t in range(NT):
                        i = pe.matmul(PS[:, n % 2, (2 * m + k) * P:(2 * m + k + 1) * P], x[:, t, k * P:(k + 1) * P],
                                      oh[:, n % 2, t, :], start=(t == 0), stop=(t == NT - 1))
            i.then_inc(e_gather, 1)

        def expert_gate_up(pe, e, n):
            w = wh[:, n % 4, :, 0:512].rearrange("p s (k f) -> p s k f", k=2)
            after(pe, e_xg, e + 1)
            after(pe, e_split, e + 1)
            after(pe, e_hf, e - 1)
            for h in range(2):
                for n_, (a_, b_, k) in enumerate([(a_, b_, k) for a_, b_ in ((0, 0), (0, 1), (1, 0)) for k in range(2)]):
                    i = pe.matmul(PS[:, 2 + n % 2, h * P:(h + 1) * P], w[:, a_, k, h * P:(h + 1) * P],
                                  xg[:, n % 2, b_, k, :], start=(n_ == 0), stop=(n_ == 5))
            i.then_inc(e_gu, 1)

        def expert_down(pe, e, n):
            after(pe, e_hl, e + 1)
            after(pe, e_ol, e)
            for n_, (a_, b_) in enumerate(((0, 0), (0, 1), (1, 0))):
                i = pe.matmul(PS[:, 5, 0:D], hh[:, n % 2, a_, :], wh[:, n % 4, b_, 512:768],
                              start=(n_ == 0), stop=(n_ == 2))
            i.then_inc(e_out, 1)

        def expert_combine(pe, e, n):
            after(pe, e_ol, e + 1)
            if isinstance(e, int) and e == 0:
                pe.wait_ge(LN["m_yd"], NT)
            for t in range(NT):
                for m in range(2):
                    i = pe.matmul(PS[:, 6 + t // 2, (t % 2) * D:(t % 2 + 1) * D], oht[:, n % 4, t * P:(t + 1) * P],
                                  oo[:, n % 2, m, :], start=(isinstance(e, int) and e == 0 and t % 2 == 0 and m == 0),
                                  stop=(isinstance(e, int) and e == E - 1), skip_group_check=True)
            i.then_inc(e_comb, 1)

        def experts(eng, step):
            for e in range(-3, NS):
                step(e, e % NS)
            with eng.Fori(1, E // NS - 1) as c:
                for n in range(NS):
                    step(c * NS + n, n)
            for n in range(NS):
                step(E - NS + n, n)

        def is_expert(e):
            return not isinstance(e, int) or 0 <= e < E

        def experts_tensor(pe):
            pe.wait_ge(LN["m_wt"], 2)
            pe.wait_ge(LN["m_xl"], 1)

            def step(e, n):
                if is_expert(e + 1):
                    expert_gate_up(pe, e + 1, (n + 1) % NS)
                if is_expert(e):
                    expert_down(pe, e, n)
                if is_expert(e + 2):
                    expert_turn_and_gather(pe, e + 2, (n + 2) % NS)
                if is_expert(e - 1):
                    expert_combine(pe, e - 1, (n - 1) % NS)
            experts(pe, step)
            expert_combine(pe, E - 1, NS - 1)

        def experts_scalar(s):
            s.wait_ge(LN["m_xl"], 1)

            def step(e, n):
                if is_expert(e + 1):
                    after(s, e_gu, e + 2)
                    after(s, e_hf, e)
                    s.activation(sl[:, (n + 1) % 2, :], PS[:, 2 + (n + 1) % 2, 0:P], ACT.Silu).then_inc(e_silu, 1)
                if is_expert(e):
                    after(s, e_out, e + 1)
                    after(s, e_comb, e - 1)
                    after(s, e_oht, e + 1)
                    s.activation(oo[:, n % 2, 0, :], PS[:, 5, 0:D], ACT.Copy, scale=wsl[:, n % 4:n % 4 + 1])\
                        .then_inc(e_ohi, 1)
                if is_expert(e + 3):
                    k = (n + 3) % NS
                    c = (e + 3 - k) // NS if isinstance(e, int) else None
                    s.wait_ge(e_w[k], 32 * (c + 1) if c is not None else (e + (3 - k + NS)) * (32 // NS))
                    after(s, e_out, e)
                    s.copy(wh[:, (n + 3) % 4, 0, :], slot[:, k, :]).then_inc(e_cast, 1)
                if is_expert(e + 2):
                    after(s, e_gather, e + 3)
                    after(s, e_gu, e + 1)
                    s.copy(xg[:, n % 2, :, :, :].rearrange("p s k n -> p (s k n)"), PS[:, n % 2, :]).then_inc(e_xg, 1)
            experts(s, step)

        def experts_vector(v):
            def step(e, n):
                if is_expert(e + 1):
                    m = (n + 1) % 2
                    after(v, e_silu, e + 2)
                    after(v, e_hl, e)
                    v.tensor_tensor(hf[:, m, :], PS[:, 2 + m, P:2 * P], sl[:, m, :], ALU.mult).then_inc(e_hf, 1)
                    after(v, e_out, e)
                    after(v, e_hf, e + 2)
                    v.tensor_copy(hh[:, m, 0, :], hf[:, m, :]).then_inc(e_hh, 1)
                    after(v, e_hh, e + 2)
                    v.tensor_tensor(hh[:, m, 1, :], hf[:, m, :], hh[:, m, 0, :], ALU.subtract).then_inc(e_hl, 1)
                if is_expert(e):
                    after(v, e_ohi, e + 1)
                    v.scalar_tensor_tensor(out=oo[:, n % 2, 1, :], in0=PS[:, 5, 0:D], scalar=wsl[:, n % 4:n % 4 + 1],
                                           in1=oo[:, n % 2, 0, :], op0=ALU.mult, op1=ALU.subtract).then_inc(e_ol, 1)
                if is_expert(e + 2):
                    k = (n + 2) % 4
                    after(v, e_turn, e + 3)
                    after(v, e_comb, e - 1)
                    v.tensor_reduce(wsl[:, k:k + 1], PS[:, 4, 256:258], AXX, ALU.add)
                    v.tensor_copy(oht[:, k, :], PS[:, 4, 0:256].bitcast(F16)).then_inc(e_oht, 1)
                if isinstance(e, int) and e == -1:
                    add_shared(v)
                if is_expert(e + 3):
                    after(v, e_gather, e + 2)
                    x = e + 3
                    for t in range(NT):
                        col = posm[:, t, bass.ds(x, 1)] if not isinstance(x, int) else posm[:, t, x:x + 1]
                        i = v.tensor_scalar(oh[:, (n + 3) % 2, t, :], iota, col, None, ALU.is_equal)
                    i.then_inc(e_oh, 1)
            experts(v, step)
            v.wait_ge(e_comb, E)
            for t in range(NT):
                v.tensor_tensor(X[:, t, :], PS[:, 6 + t // 2, (t % 2) * D:(t % 2 + 1) * D], X[:, t, :], ALU.add)\
                    .then_inc(x_done, 1)

        def experts_gpsimd(g):
            g.wait_ge(LN["m_xh"], 1)
            g.tensor_tensor(xl, XN, xh, ALU.subtract).then_inc(LN["m_xl"], 1)
            g.wait_ge(LN["m_xl"], 1)

            def step(e, n):
                if is_expert(e + 3):
                    after(g, e_cast, e + 4)
                    after(g, e_split, e + 3)
                    g.tensor_tensor(wh[:, (n + 3) % 4, 1, :], slot[:, (n + 3) % NS, :], wh[:, (n + 3) % 4, 0, :],
                                    ALU.subtract).then_inc(e_split, 1)
            experts(g, step)

        def experts_sync(sp):
            def load(e, n):
                after(sp, e_split, e - NS + 1)
                gu = a["L1_ffn_expert_gate_up_w"]
                dn = a["L1_ffn_expert_down_w"]
                ge = gu[bass.ds(e, 1)] if not isinstance(e, int) else gu[e:e + 1]
                de = dn[bass.ds(e, 1)] if not isinstance(e, int) else dn[e:e + 1]
                sp.dma_start(slot[:, n, 0:512].rearrange("p (k f) -> p k f", k=2),
                             ge.rearrange("o (k p) f -> p (o k) f", p=P)).then_inc(e_w[n], 16)
                sp.dma_start(slot[:, n, 512:768], de.rearrange("o p f -> p (o f)")).then_inc(e_w[n], 16)
            for n in range(NS):
                load(n, n)
            with sp.Fori(1, E // NS) as c:
                for n in range(NS):
                    load(c * NS + n, n)

        gam = PT[:, 0:512].bitcast(F32)
        bet = PT[:, 512:1024].bitcast(F32)
        eo = small[:, 70:72]
        s_gb = sem("s_gb")

        block = ctx.enter_context(nc.Block())

        def row(ap):
            return ap.rearrange("(o n) -> o n", o=1).to_broadcast([P, D])

        @block.sync
        def _(sp):
            sp.dma_start(X, a["x"].rearrange("(t p) d -> p t d", p=P)).then_inc(s_x, 16)
            sp.dma_start(ident[:, :], a["ident"]).then_inc(s_ident, 16)
            w0 = {k: a["L0_xattn_" + n] for k, n in (("wq", "Wq"), ("wkT", "WkT"), ("wv", "Wv"), ("wo", "Wout"))}
            w1 = {k: a["L1_xattn_" + n] for k, n in (("wq", "Wq"), ("wkT", "WkT"), ("wv", "Wv"), ("wo", "Wo"))}
            cross_loads_qk(sp, L0, w0)
            sp.wait_ge(s_memset, 5)
            raw_loads(sp, L0, [0])
            for dst, n in ((cosT[:, :], "cos"), (sinT[:, :], "sin"), (cmask[:, :], "cmask"),
                           (eo, "eo")):
                sp.dma_start(dst, a[n]).then_inc(s_const, 16)
            raw_loads(sp, L0, [1])
            cross_loads_vo(sp, L0, w0)
            sp.dma_start(bias_x0, row(a["L0_xattn_bout"])).then_inc(L0.bias, 16)
            sp.dma_start(bias_f, row(a["L0_ffn_b2"])).then_inc(LN["f_bias"], 16)
            sp.dma_start(bias_x1, row(a["L1_xattn_bo"])).then_inc(L1.bias, 16)
            for n, k in enumerate(("PQT", "PQsT", "PKT", "PKsT", "PVT", "POT")):
                sp.dma_start(WA[:, n, :, :], a["L0_attn_" + k].rearrange("(k p) n -> p k n", p=P)).then_inc(SA.wl, 16)
            sp.dma_start(W1, a["L0_ffn_w1"].rearrange("(k p) n -> p k n", p=P)).then_inc(LN["f_w"], 16)
            sp.dma_start(W2, a["L0_ffn_w2"].rearrange("(f p) n -> p f n", p=P)).then_inc(LN["f_w"], 16)
            sp.dma_start(b1_c, a["L0_ffn_b1_cols"]).then_inc(LN["f_w"], 16)
            sp.dma_start(b_c, a["L1_attn_b_cols"]).then_inc(SB.wl, 16)
            if PHASES > 3:
                sp.wait_ge(L0.w, 2 * L0.heads)
                cross_loads_qk(sp, L1, w1)
            raw_loads(sp, L0, range(2, B))
            if PHASES > 3:
                raw_loads(sp, L1, [0])
                sp.wait_ge(L0.y, NT)
                cross_loads_vo(sp, L1, w1)
            if PHASES > 3:
                raw_loads(sp, L1, range(1, B))
            if PHASES > 4:
                sp.wait_ge(L1.w, 2 * L1.heads)
                sp.dma_start(WQK[:, 0:6 * D].rearrange("p (k n) -> p k n", k=2),
                             a["L1_attn_w_qkvT"].rearrange("(k p) n -> p k n", p=P)).then_inc(SB.wl, 16)
                if PHASES > 5:
                    sp.dma_start(wsh, a["L1_ffn_shared_gate_up_w"].rearrange("(k p) n -> p k n", p=P)).then_inc(LN["m_w"], 16)
                    sp.wait_ge(L1.prep, 3 * B)
                    sp.dma_start(wdn, a["L1_ffn_shared_down_w"].rearrange("(c p) n -> p c n", p=P)).then_inc(LN["m_w"], 16)
                    sp.dma_start(wrt, a["L1_ffn_gates"].rearrange("(k p) n -> p k n", p=P)).then_inc(LN["m_w"], 16)
                    sp.dma_start(iota, a["iota16"]).then_inc(LN["m_w"], 16)
                    sp.dma_start(id16, a["id16"]).then_inc(LN["m_w"], 16)
                    sp.dma_start(tri, a["tri"].rearrange("p (i n) -> p i n", i=2)).then_inc(LN["m_w"], 16)
                sp.wait_ge(L1.pv, B * L1.np)
                sp.wait_ge(L1.rest, 4 * B * L1.np)
                sp.dma_start(gam, row(a["L1_attn_ln_gamma"])).then_inc(s_gb, 16)
                sp.dma_start(bet, row(a["L1_attn_ln_beta"])).then_inc(s_gb, 16)
            if PHASES > 5:
                sp.wait_ge(L1.av, L1.np)
                experts_sync(sp)
            sp.wait_ge(x_done, NT)
            sp.dma_start(out.rearrange("(t p) d -> p t d", p=P), X).then_inc(s_out, 16)
            sp.wait_ge(s_out, 16)

        @block.gpsimd
        def _(g):
            g.memset(CR[:, :].rearrange("p (t n) -> p t n", n=386)[:, :, CD:CD + 1], 1.0).then_inc(s_memset, 1)
            g.memset(rawR[:, (KT - 1) * CD:], 0.0).then_inc(s_memset, 1)
            context_rests(g, L0, range(B))
            if PHASES > 3:
                context_rests(g, L1, [0])
            if PHASES > 1:
                self_gpsimd(g, SA, L0)
            if PHASES > 2:
                ffn_gpsimd(g)
            if PHASES > 3:
                context_rests(g, L1, range(1, B))
            if PHASES > 4:
                self_gpsimd(g, SB, L1)
            if PHASES > 5:
                experts_gpsimd(g)

        @block.scalar
        def _(s):
            s.wait_ge(s_memset, 5)
            for n in range(PHASES):
                ln_scalar(s, ("l0x", "l0a", "l0f", "l1x", "l1a", "l1m")[n], 2 if n == 4 else 1)
                if n in (0, 3):
                    L = (L0, L1)[n // 3]
                    queries_scalar(s, L)
                    units_scalar(s, L)
                    project_scalar(s, L)
                elif n in (1, 4):
                    self_scalar(s, (SA, SB)[n // 3])
                elif n == 2:
                    ffn_scalar(s)
                else:
                    router_scalar(s)
                    experts_scalar(s)

        @block.vector
        def _(v):
            v.memset(eps_c, EPS).then_inc(s_memset, 1)
            v.memset(gel0, -STEP / 256).then_inc(s_memset, 1)
            v.memset(gel1, -STEP / 256 + 0.25).then_inc(s_memset, 1)
            v.wait_ge(s_x, 16)
            finish = None
            for n in range(PHASES):
                ln_vector(v, ("l0x", "l0a", "l0f", "l1x", "l1a", "l1m")[n], finish, (gam, bet, s_gb) if n == 4 else None)
                if n in (0, 3):
                    L = (L0, L1)[n // 3]
                    if n == 0:
                        for part in range(3):
                            context_head(v, L0, 0, 0, part)
                    queries_vector(v, L)
                    units_vector(v, L)
                    project_vector(v, L)
                    finish = project_finish(L)
                elif n in (1, 4):
                    self_vector(v, (SA, SB)[n // 3])
                    finish = self_finish((SA, SB)[n // 3])
                elif n == 2:
                    ffn_vector(v)
                    finish = ffn_finish
                else:
                    router_vector(v)
                    experts_vector(v)
            if PHASES < 6:
                for t in range(NT):
                    finish(v, t).then_inc(x_done, 1)

        @block.tensor
        def _(pe):
            for n in range(PHASES):
                ln_tensor(pe, ("l0x", "l0a", "l0f", "l1x", "l1a", "l1m")[n])
                if n in (0, 3):
                    L = (L0, L1)[n // 3]
                    queries_tensor(pe, L)
                    units_tensor(pe, L)
                    project_tensor(pe, L)
                elif n in (1, 4):
                    self_tensor(pe, (SA, SB)[n // 3])
                elif n == 2:
                    ffn_tensor(pe)
                else:
                    router_tensor(pe)
                    experts_tensor(pe)


def kernel(**inputs):
    import concourse.bacc as bacc
    from concourse.bass_utils import run_bass_kernel_spmd as run

    i = {k: np.asarray(v) for k, v in inputs.items()}
    cos, sin = rope_tables()
    arrays = {
        "x": i["x"].reshape(T, D),
        "ctx": i["ctx_768"],
        "ctxT": i["ctx_768"].transpose(0, 2, 1),
        "L0_xattn_WkT": i["L0_xattn_Wk"].T,
        "L1_xattn_WkT": i["L1_xattn_Wk"].T,
        "ident": np.eye(P, dtype=np.float32),
        "cos": cos,
        "sin": sin,
        "cmask": np.where(np.arange(S)[None, :] <= (np.arange(P) % S)[:, None], 0.0, -1e30).astype(np.float32),
    }
    swap = np.arange(D) ^ 1
    for n, k in (("PQT", "P_Q"), ("PKT", "P_K"), ("PVT", "P_V"), ("POT", "P_O")):
        arrays["L0_attn_" + n] = i["L0_attn_" + k].T
    arrays["L0_attn_PQsT"] = i["L0_attn_P_Q"][swap].T
    arrays["L0_attn_PKsT"] = i["L0_attn_P_K"][swap].T
    arrays["L0_ffn_b1_cols"] = i["L0_ffn_b1"].reshape(-1, P).T
    arrays["L1_attn_b_cols"] = i["L1_attn_b_qkv"].reshape(-1, P).T
    arrays["L1_ffn_gates"] = np.concatenate([i["L1_ffn_gate_w"], i["L1_ffn_shared_gate_w"]], 1)
    arrays["L1_attn_w_qkvT"] = i["L1_attn_w_qkv"].T
    part = np.arange(P)
    arrays["eo"] = np.stack([part // DK % 2 == 0, part // DK % 2 == 1], 1).astype(np.float32)
    arrays["iota16"] = np.broadcast_to(np.arange(P), (P, P)).astype(np.float16)
    arrays["id16"] = np.eye(P, dtype=np.float16)
    arrays["tri"] = np.concatenate([part[:, None] < part[None, :], np.ones((P, P), bool)], 1).astype(np.float32)
    for k in i:
        if k not in ("x", "ctx_768", "L0_xattn_Wk", "L1_xattn_Wk", "L1_attn_w_qkv", "L1_attn_b_qkv", "L0_ffn_b1", "L1_ffn_gate_w", "L1_ffn_shared_gate_w") and "_attn_P" not in k:
            arrays[k] = i[k]
    arrays = {k: np.ascontiguousarray(v) for k, v in arrays.items()}
    nc = bacc.Bacc("TRN2", target_bir_lowering=False, num_devices=1)
    a = {k: nc.dram_tensor(k + "_dram", v.shape, mybir.dt.from_np(v.dtype), kind="ExternalInput").ap() for k, v in arrays.items()}
    out = nc.dram_tensor("out_dram", (T, D), F32, kind="ExternalOutput").ap()
    perceiver(nc, a, out)
    r = run(nc, [{k + "_dram": v for k, v in arrays.items()}], core_ids=[0])
    return r.results[0]["out_dram"].reshape(B, S, D)
```

```python
from contextlib import ExitStack

import numpy as np

import concourse.bass as bass
from concourse import mybir

F32 = mybir.dt.float32
F16 = mybir.dt.float16
BF16 = mybir.dt.bfloat16
ALU = mybir.AluOpType
ACT = mybir.ActivationFunctionType
AXX = mybir.AxisListType.X

P = 128
B, S, D = 8, 64, 256
T = B * S
NT = T // P
NK = 1601
CD = 192
C0, C1 = 128, 64
KT = (NK + P - 1) // P
KL = NK - (KT - 1) * P
DK = D // 16
FF = 1024
E, ISH = 64, 512
CAPACITY = 128
EPS = 1e-5
ROUND = 1.5 * 2.0 ** 23


def rope_tables():
    freq = np.float32(10000.0) ** (-np.arange(0, DK, 2, dtype=np.float32) / np.float32(DK))
    ang = np.arange(S, dtype=np.float32)[:, None] * freq.astype(np.float32)[None, :]
    cos, sin = np.cos(ang).astype(np.float32), np.sin(ang).astype(np.float32)
    c = np.zeros((DK, S), np.float32)
    s = np.zeros((DK, S), np.float32)
    c[0::2], c[1::2] = cos.T, cos.T
    s[0::2], s[1::2] = -sin.T, sin.T
    return np.tile(c, (P // DK, 1)), np.tile(s, (P // DK, 1))


def perceiver(nc, a, out):
    with ExitStack() as ctx:
        def sb(name, floats, dt=F32):
            return ctx.enter_context(nc.sbuf_tensor(name, [P, floats], dt))

        def sem(name):
            return ctx.enter_context(nc.semaphore(name))

        X_ = sb("X", NT * D)
        X = X_[:, :].rearrange("p (t d) -> p t d", t=NT)
        xnT_ = sb("xnT", 2 * T)
        xnT = xnT_[:, :].rearrange("p (k n) -> p k n", k=2)
        QA = sb("QA", 8 * B * P)
        QB = sb("QB", 8 * B * P)
        A = sb("A", 8 * T)
        CX = sb("CX", 2 * 3 * 1602, F16)
        CR = sb("CR", 2 * KT * 386, F16)
        raw0 = sb("raw0", 1602)
        raw1 = sb("raw1", 1602)
        rawR = sb("rawR", KT * CD)
        Pr = sb("Pr", 2 * 1602)
        PT = sb("PT", 2 * KT * P, F16)
        On = sb("On", CD)
        WVO = sb("WVO", 4096)
        WQK = sb("WQK", 4096)
        bias_rows = sb("bias_rows", 3 * D)
        ident = sb("ident", P)
        cosT = sb("cosT", S)
        sinT = sb("sinT", S)
        cmask = sb("cmask", S)
        mask16 = sb("mask16", S, BF16)
        one16 = sb("one16", P, BF16)
        small = sb("small", 512)
        PS = ctx.enter_context(nc.psum_tensor("PS", [P, 8, 512], F32))

        XN = Pr[:, 0:NT * D].rearrange("p (t d) -> p t d", t=NT)
        stats = small[:, 0:24].rearrange("p (t s) -> p t s", t=NT)
        mv = small[:, 24:32].rearrange("p (t s) -> p t s", t=NT)
        std = small[:, 32:36]
        rstd = small[:, 36:40]
        bias_x0, bias_f, bias_x1 = (bias_rows[:, i * D:(i + 1) * D] for i in range(3))
        eps_c = small[:, 40:41]
        nmax = small[:, 42:44]
        rden = small[:, 44:45]
        b1_c = small[:, 48:56]
        gel0 = small[:, 56:57]
        gel1 = small[:, 57:58]
        nstep = small[:, 58:59]

        s_ident = sem("s_ident")
        s_const = sem("s_const")
        s_x = sem("s_x")
        s_bias = sem("s_bias")
        s_memset = sem("s_memset")
        vch = sem("vch")
        count = {"v": 0}

        def vmark(ins):
            count["v"] += 1
            ins.then_inc(vch, 1)
            return count["v"]

        def vlink(eng, ins):
            count["v"] += 1
            ins.then_inc(vch, 1)
            eng.wait_ge(vch, count["v"])

        LN = {k: sem(f"ln_{k}") for k in ("var", "std", "xn", "T", "xnT")}
        NORMS = {n: (NT * (i + (i > 4)), NT * i) for i, n in enumerate(("l0x", "l0a", "l0f", "l1x", "l1a", "l1m"))}

        def ln_steps(rounds):
            return [[(k, n - k) for k in range(rounds + 1) if 0 <= n - k < NT] for n in range(NT + rounds)]

        def ln_variance_count(rounds):
            order = [kt for step in ln_steps(rounds) for kt in step if kt[0] < rounds]
            return {kt: n + 1 for n, kt in enumerate(order)}

        def ln_vector(v, n, finish=None, affine=None):
            z, (before, _) = LN, NORMS[n]
            rounds = 2 if affine else 1
            count_of = ln_variance_count(rounds)
            if affine:
                gamma, beta, landed = affine
                v.wait_ge(landed, 32)

            def root(t, k):
                v.wait_ge(z["std"], before + count_of[k, t])
                return vmark(v.reciprocal(rstd[:, t:t + 1], std[:, t:t + 1]))

            for m in range(NT + rounds):
                t, u, w = (i if 0 <= i < NT else None for i in (m, m - 1, m - 2 if affine else -1))
                if t is not None:
                    t_done = vmark(finish(v, t)) if finish else None
                if w is not None:
                    w_done = root(w, 1)
                if t is not None:
                    if finish:
                        v.wait_ge(vch, t_done)
                    t_done = vmark(v.bn_stats(stats[:, t, :], X[:, t, :]))
                if u is not None:
                    u_done = root(u, 0)
                if t is not None:
                    v.wait_ge(vch, t_done)
                    v.bn_aggr(mv[:, t, :], stats[:, t, :]).then_inc(z["var"], 1)
                if u is not None:
                    v.wait_ge(vch, u_done)
                    i = v.tensor_scalar(XN[:, u, :], X[:, u, :], mv[:, u, 0:1], rstd[:, u:u + 1],
                                        ALU.subtract, ALU.mult)
                    if affine:
                        u_done = vmark(i)
                    else:
                        i.then_inc(z["xn"], 1)
                if w is not None:
                    v.wait_ge(vch, w_done)
                    w_done = vmark(v.scalar_tensor_tensor(out=XN[:, w, :], in0=XN[:, w, :], scalar=mv[:, w, 0:1],
                                                          in1=gamma, op0=ALU.subtract, op1=ALU.mult))
                if u is not None and affine:
                    v.wait_ge(vch, u_done)
                    u_done = vmark(v.bn_stats(stats[:, u, :], XN[:, u, :]))
                if w is not None:
                    v.wait_ge(vch, w_done)
                    v.scalar_tensor_tensor(out=XN[:, w, :], in0=XN[:, w, :], scalar=rstd[:, w:w + 1], in1=beta,
                                           op0=ALU.mult, op1=ALU.add).then_inc(z["xn"], 1)
                if u is not None and affine:
                    v.wait_ge(vch, u_done)
                    v.bn_aggr(mv[:, u, :], stats[:, u, :]).then_inc(z["var"], 1)

        def ln_scalar(s, n, rounds=1):
            z, (before, tiles) = LN, NORMS[n]
            count_of = ln_variance_count(rounds)

            def store(t):
                s.wait_ge(z["T"], tiles + t + 1)
                s.copy(xnT[:, :, t * P:(t + 1) * P],
                       PS[:, 6 + t % 2, 0:2 * P].rearrange("p (k n) -> p k n", k=2)).then_inc(z["xnT"], 1)

            for m, step in enumerate(ln_steps(rounds)):
                for k, t in step:
                    if k < rounds:
                        s.wait_ge(z["var"], before + count_of[k, t])
                        s.activation(std[:, t:t + 1], mv[:, t, 1:2], ACT.Sqrt, bias=eps_c).then_inc(z["std"], 1)
                if m > rounds:
                    store(m - rounds - 1)
            store(NT - 1)

        def ln_tensor(pe, n):
            z, tiles = LN, NORMS[n][1]
            if n == "l0x":
                pe.wait_ge(s_ident, 16)
            for t in range(NT):
                pe.wait_ge(z["xn"], tiles + t + 1)
                if t >= 2:
                    pe.wait_ge(z["xnT"], tiles + t - 1)
                for k in range(2):
                    i = pe.transpose(PS[:, 6 + t % 2, k * P:(k + 1) * P], XN[:, t, k * P:(k + 1) * P], ident[:, :])
                i.then_inc(z["T"], 1)
            pe.wait_ge(z["xnT"], tiles + NT)

        class Cross:

            def __init__(self, n, heads, g0):
                self.wqk = sem(f"{n}_wqk")
                self.wvo = sem(f"{n}_wvo")
                self.q = sem(f"{n}_q")
                self.qT = sem(f"{n}_qT")
                self.w = sem(f"{n}_w")
                self.wA = sem(f"{n}_wA")
                self.wV = sem(f"{n}_wV")
                self.scores = sem(f"{n}_scores")
                self.nmax = sem(f"{n}_nmax")
                self.exp = sem(f"{n}_exp")
                self.tr = sem(f"{n}_tr")
                self.head = sem(f"{n}_head")
                self.rest = sem(f"{n}_rest")
                self.pv = sem(f"{n}_pv")
                self.on = sem(f"{n}_on")
                self.otr = sem(f"{n}_otr")
                self.oT = sem(f"{n}_oT")
                self.oh = sem(f"{n}_oh")
                self.wvs = sem(f"{n}_wvs")
                self.av = sem(f"{n}_av")
                self.ao = sem(f"{n}_ao")
                self.y = sem(f"{n}_y")
                self.yx = sem(f"{n}_yx")
                self.raw = sem(f"{n}_raw")
                self.rows = sem(f"{n}_rows")
                self.cast = sem(f"{n}_cast")
                self.prep = sem(f"{n}_prep")
                self.n, self.heads, self.np, self.g0 = n, heads, heads // 2, g0
                self.inner = heads * 64
                self.wq = WQK[:, 0:2 * self.inner].rearrange("p (k n) -> p k n", k=2)
                self.wk = WQK[:, 2 * self.inner:2 * self.inner + self.np * 256].rearrange("p (j c) -> p j c", c=256)
                self.wv = WVO[:, 0:2 * self.inner].rearrange("p (k n) -> p k n", k=2)
                self.wo = WVO[:, 2 * self.inner:2 * self.inner + self.np * D].rearrange("p (j n) -> p j n", n=D)
                self.xq = A[:, 0:self.np * T].rearrange("p (j n) -> p j n", j=self.np)
                nu = B * self.np
                self.qa = QA[:, 0:nu * P].bitcast(F16).rearrange("p (u s c) -> p u s c", s=2, c=P)
                self.qb = QB[:, 0:nu * P].bitcast(F16).rearrange("p (u s c) -> p u s c", s=2, c=P)
                self.qa6 = self.qa.rearrange("p (b j) s (h q) -> p b j s h q", b=B, h=2)
                self.qb6 = self.qb.rearrange("p (b j) s (h q) -> p b j s h q", b=B, h=2)
                half = self.inner // 2
                if g0 == 0:
                    places = [WVO[:, 2048 + i * half:2048 + (i + 1) * half] for i in range(4)]
                else:
                    places = [raw[:, i * half:(i + 1) * half] for raw in (raw0, raw1) for i in range(2)]
                self.vh0, self.vl0, self.vh1, self.vl1 = (place.bitcast(F16) for place in places)

        SPLITS = 5
        ROWS = ((0, 5), (5, 9), (9, KT))

        def raw_loads(sp, L, batches):
            for b in batches:
                g = L.g0 + b
                if g:
                    sp.wait_ge(L.prep if b else L0.prep, SPLITS * (b or B))
                sp.dma_start(raw0[:, 0:NK], a["ctxT"][b, 0:C0, :]).then_inc(L.raw, 16)
                sp.dma_start(raw1[0:C1, 0:NK], a["ctxT"][b, C0:CD, :]).then_inc(L.raw, 16)
                sp.dma_start(raw1[C1:P, 0:NK], a["ctxT"][b, C0:CD, :]).then_inc(L.raw, 16)
                sp.dma_start(rawR[:, 0:(KT - 1) * CD].rearrange("p (t c) -> p t c", c=CD),
                             a["ctx"][b, 0:(KT - 1) * P, :].rearrange("(t p) c -> p t c", p=P)).then_inc(L.rows, 16)
                sp.dma_start(rawR[0:KL, (KT - 1) * CD:], a["ctx"][b, (KT - 1) * P:, :]).then_inc(L.rows, 16)

        def cx_of(par):
            return CX[:, par * 3 * 1602:(par + 1) * 3 * 1602].rearrange("p (s n) -> p s n", s=3)

        def cr_of(par):
            return CR[:, par * KT * 386:(par + 1) * KT * 386].rearrange("p (t n) -> p t n", t=KT)

        def context_head(v, L, b, par, n):
            cx, cr = cx_of(par), cr_of(par)
            if n == 0:
                v.wait_ge(L.raw, 48 * (b + 1))
                if not isinstance(b, int) or b >= 2:
                    v.wait_ge(L.pv, L.np * (b - 1))
                elif L.g0:
                    v.wait_ge(L0.pv, L0.np * (B - 1 + b))
            if n == 0:
                i = v.tensor_copy(cx[:, 0, 0:NK], raw0[:, 0:NK])
            elif n == 1:
                i = v.tensor_copy(cx[:, 2, 0:NK], raw1[:, 0:NK])
            else:
                lo, hi = ROWS[n - 2]
                if n == 2:
                    v.wait_ge(L.rows, 32 * (b + 1))
                i = v.tensor_copy(cr[:, lo:hi, 0:CD], rawR[:, lo * CD:hi * CD].rearrange("p (t c) -> p t c", c=CD))
            i.then_inc(L.cast, 1)

        def context_rests(g_, L, batches):
            for b in batches:
                cx, cr = cx_of((L.g0 + b) % 2), cr_of((L.g0 + b) % 2)
                if b or L.g0:
                    g_.wait_ge(L.prep if b else L0.prep, SPLITS * (b or B))
                g_.wait_ge(L.cast, SPLITS * b + 1)
                g_.tensor_tensor(cx[:, 1, 0:NK], raw0[:, 0:NK], cx[:, 0, 0:NK], ALU.subtract).then_inc(L.prep, 1)
                g_.wait_ge(L.prep, SPLITS * b + 1)
                g_.wait_ge(L.cast, SPLITS * b + 2)
                g_.tensor_tensor(cx[C1:P, 2, 0:NK], raw1[C1:P, 0:NK], cx[C1:P, 2, 0:NK], ALU.subtract)\
                    .then_inc(L.prep, 1)
                g_.wait_ge(L.prep, SPLITS * b + 2)
                for n, (lo, hi) in enumerate(ROWS):
                    g_.wait_ge(L.cast, SPLITS * b + 3 + n)
                    g_.tensor_tensor(cr[:, lo:hi, CD + 1:2 * CD + 1],
                                     rawR[:, lo * CD:hi * CD].rearrange("p (t c) -> p t c", c=CD),
                                     cr[:, lo:hi, 0:CD], ALU.subtract).then_inc(L.prep, 1)

        def q_bank(h, c):
            return PS[:, 4 + 2 * (h % 2) + c, :]

        EARLY = {0: 3, B: 5}

        def queries_tensor(pe, L):
            pe.wait_ge(L.wqk, 48)
            for j in range(L.np):
                if j >= 2:
                    pe.wait_ge(L.qT, j - 1)
                for k in range(2):
                    i = pe.matmul(PS[:, j % 2, :], L.wq[:, k, j * P:(j + 1) * P], xnT[:, k, :],
                                  start=(k == 0), stop=(k == 1))
                i.then_inc(L.q, 1)
            for h in range(L.heads):
                if h == L.heads - EARLY[L.g0]:
                    for p in range(PASSES):
                        scores(pe, L, 0, 0, 0, True, p)
                j, o = h // 2, 64 * (h % 2)
                pe.wait_ge(L.qT, j + 1)
                if h >= 2:
                    pe.wait_ge(L.wA, 2 * (h - 1))
                    pe.wait_ge(L.wV, 2 * (h - 1))
                for c in range(2):
                    i = pe.matmul(q_bank(h, c), L.wk[o:o + 64, j, c * P:(c + 1) * P],
                                  L.xq[o:o + 64, j, :], start=True, stop=True)
                    i.then_inc(L.w, 1)

        def queries_scalar(s, L):
            s.activation(small[:, 80:81], eps_c, ACT.Exp)
            for j in range(L.np):
                s.wait_ge(L.q, j + 1)
                s.activation(L.xq[:, j, :], PS[:, j % 2, :], ACT.Copy, scale=0.125).then_inc(L.qT, 1)
            for h in range(L.heads):
                for c, q6 in ((0, L.qa6), (1, L.qb6)):
                    s.wait_ge(L.w, 2 * h + c + 1)
                    s.copy(q6[:, :, h // 2, 0, h % 2, :],
                           q_bank(h, c).rearrange("p (b q) -> p b q", b=B)).then_inc(L.wA, 1)
                if h == L.heads - EARLY[L.g0]:
                    unit_scalar_exp(s, L, 0, 0)

        def queries_vector(v, L):
            for h in range(L.heads):
                for c, q6 in ((0, L.qa6), (1, L.qb6)):
                    v.wait_ge(L.wA, 2 * h + c + 1)
                    v.tensor_tensor(q6[:, :, h // 2, 1, h % 2, :],
                                    q_bank(h, c).rearrange("p (b q) -> p b q", b=B),
                                    q6[:, :, h // 2, 0, h % 2, :], ALU.subtract).then_inc(L.wV, 1)
                if h == L.heads - EARLY[L.g0] - 1:
                    unit_vector_max(v, L, 0, 0)

        CH = [(0, 512), (512, 512), (1024, 512), (1536, NK - 1536)]
        PSf = PS[:, :, :].rearrange("p b n -> p (b n)")
        scores_ps = PSf[:, 0:NK]
        pv_ps = PS[:, 7, 0:2 * CD + 1]
        HGR = [(0, 4, 4, 0), (4, 8, 5, 0), (8, 12, 6, 0), (12, 13, 4, 256)]

        PASSES = 5

        def scores(pe, L, b, u, par, first, n):
            cx = cx_of(par)
            if n == 0 and isinstance(u, int) and u == 0:
                pe.wait_ge(L.wA, 4)
                pe.wait_ge(L.wV, 4)
            if n == 0 and first:
                pe.wait_ge(L.prep, SPLITS * (b + 1))
            if n == 0 and not (isinstance(u, int) and u == 0):
                pe.wait_ge(L.exp, 2 * u)
            q, hr, c = [(L.qa, 0, 0), (L.qa, 0, 1), (L.qa, 1, 0), (L.qb, 0, 2), (L.qb, 1, 2)][n]
            for o, w in CH:
                i = pe.matmul(PSf[:, o:o + w], q[:, u, hr, :], cx[:, c, o:o + w],
                              start=(n == 0), stop=(n == PASSES - 1))
            if n == PASSES - 1:
                i.then_inc(L.scores, 1)

        def transposes(pe, L, u, parity, k):
            pr = Pr[:, parity * 1602:parity * 1602 + NK]
            lo, hi, bank, col = HGR[k]
            for t in range(lo, hi):
                w = min(P, NK - t * P)
                i = pe.transpose(PS[0:w, bank, col + (t - lo) * P:col + (t - lo + 1) * P],
                                 pr[:, t * P:t * P + w], ident[:, :])
            i.then_inc(L.tr, 1)

        def turn_result(pe, L, u):
            pe.wait_ge(L.on, u + 1)
            pe.transpose(PS[:, 4, 0:P], On[:, 0:C0], ident[:, :])
            pe.transpose(PS[0:C1, 4, P:2 * P], On[:, C0:CD], ident[:, :]).then_inc(L.otr, 1)

        pt = PT[:, :].rearrange("p (s t q) -> p s t q", s=2, t=KT)

        def attend(pe, L, u, par, k):
            cr = cr_of(par)
            lo, hi, _, _ = HGR[k]
            pe.wait_ge(L.rest, 4 * u + k + 1)
            for t in range(lo, hi):
                w = min(P, NK - t * P)
                pe.matmul(pv_ps, pt[0:w, 0, t, :], cr[0:w, t, 0:2 * CD + 1], start=(t == 0), stop=False)
                i = pe.matmul(pv_ps[:, 0:CD + 1], pt[0:w, 1, t, :], cr[0:w, t, 0:CD + 1],
                              start=False, stop=(t == KT - 1))
            if k == 3:
                i.then_inc(L.pv, 1)

        def turn_most(pe, L, u, parity, prev):
            if prev:
                pe.wait_ge(L.oT, u - 1)
            pe.wait_ge(L.exp, 2 * u + 1)
            transposes(pe, L, u, parity, 0)
            transposes(pe, L, u, parity, 1)
            pe.wait_ge(L.exp, 2 * u + 2)
            if not prev and isinstance(u, int) and u == 0:
                pe.wait_ge(L.wA, 2 * L.heads)
                pe.wait_ge(L.wV, 2 * L.heads)
            transposes(pe, L, u, parity, 2)

        def turn_last(pe, L, u, parity, prev):
            pe.wait_ge(L.rest, 4 * u + 1)
            if prev:
                turn_result(pe, L, u - 1)
            transposes(pe, L, u, parity, 3)

        def unit_scalar_exp(s, L, u, parity):
            s.wait_ge(L.nmax, u + 1)
            if not isinstance(u, int) or u > 1:
                s.wait_ge(L.tr, 4 * (u - 1))
            for lo, hi in ((0, 1024), (1024, NK)):
                s.activation(Pr[:, parity * 1602 + lo:parity * 1602 + hi], PSf[:, lo:hi], ACT.Exp,
                             bias=nmax[:, parity:parity + 1]).then_inc(L.exp, 1)

        def unit_scalar_heads(s, L, u):
            if not isinstance(u, int) or u > 0:
                s.wait_ge(L.pv, u)
            for k, (lo, hi, bank, col) in enumerate(HGR):
                s.wait_ge(L.tr, 4 * u + k + 1)
                w = P if k < 3 else KL
                s.copy(pt[0:w, 0, lo:hi, :], PS[0:w, bank, col:col + (hi - lo) * P].rearrange("p (t q) -> p t q", q=P))\
                    .then_inc(L.head, 1)

        def unit_vector_max(v, L, u, parity):
            v.wait_ge(L.scores, u + 1)
            v.tensor_reduce(nmax[:, parity:parity + 1], scores_ps, AXX, ALU.max, negate=True).then_inc(L.nmax, 1)

        def unit_vector_rests(v, L, u):
            for k, (lo, hi, bank, col) in enumerate(HGR):
                v.wait_ge(L.head, 4 * u + k + 1)
                w = P if k < 3 else KL
                v.tensor_tensor(pt[0:w, 1, lo:hi, :], PS[0:w, bank, col:col + (hi - lo) * P].rearrange("p (t q) -> p t q", q=P),
                                pt[0:w, 0, lo:hi, :], ALU.subtract).then_inc(L.rest, 1)

        def store_head(v, L, u):
            v.wait_ge(L.otr, u + 1)
            v.tensor_copy(L.qa[:, u, 0, :], PS[:, 4, 0:P])
            v.tensor_copy(L.qb[0:C1, u, 0, :], PS[0:C1, 4, P:2 * P]).then_inc(L.oh, 1)

        def store_rest(v, L, u):
            v.wait_ge(L.oh, u + 1)
            v.tensor_tensor(L.qa[:, u, 1, :], PS[:, 4, 0:P], L.qa[:, u, 0, :], ALU.subtract)
            v.tensor_tensor(L.qb[C1:P, u, 0, :], PS[0:C1, 4, P:2 * P], L.qb[0:C1, u, 0, :], ALU.subtract)\
                .then_inc(L.oT, 1)

        def normalise(v, L, u):
            v.wait_ge(L.pv, u + 1)
            v.reciprocal(rden, pv_ps[:, CD:CD + 1]).then_inc(L.yx, 1)
            if not isinstance(u, int) or u > 0:
                v.wait_ge(L.otr, u)
            v.wait_ge(L.yx, 2 * u + 1)
            v.tensor_scalar(On[:, :], pv_ps[:, CD + 1:], rden, None, ALU.mult).then_inc(L.yx, 1)
            v.wait_ge(L.yx, 2 * u + 2)
            v.scalar_tensor_tensor(out=On[:, :], in0=pv_ps[:, 0:CD], scalar=rden, in1=On[:, :],
                                   op0=ALU.mult, op1=ALU.add).then_inc(L.on, 1)

        PAIRS = B // 2

        def over_batch_pairs(eng, first, body):
            with eng.Fori(first, PAIRS - 1) as i:
                body(i * 2, False)
            body(B - 2, True)

        def units_tensor(pe, L):
            n = L.np
            pe.wait_ge(L.wA, 2 * L.heads - 2)
            pe.wait_ge(L.wV, 2 * L.heads - 2)
            turn_most(pe, L, 0, 0, False)

            def pair(b, last, start=False):
                for s_ in range(2 * n):
                    u, x = b * n + s_, s_ + 1
                    prev = not (start and s_ == 0)
                    more = s_ < 2 * n - 1 or not last
                    for p in range(PASSES):
                        if more:
                            scores(pe, L, b + x // n, b * n + x, (x // n) % 2, x % n == 0, p)
                        if p == 1:
                            turn_last(pe, L, u, s_ % 2, prev)
                    if prev:
                        pe.wait_ge(L.on, u)
                    for k in range(4):
                        attend(pe, L, u, s_ // n, k)
                    if more:
                        turn_most(pe, L, u + 1, x % 2, prev)
            pair(0, False, True)
            over_batch_pairs(pe, 1, pair)

        def units_scalar(s, L):
            n = L.np

            def pair(b, last):
                for s_ in range(2 * n):
                    u = b * n + s_
                    unit_scalar_heads(s, L, u)
                    if s_ < 2 * n - 1 or not last:
                        unit_scalar_exp(s, L, u + 1, (s_ + 1) % 2)
            pair(0, False)
            over_batch_pairs(s, 1, pair)

        CONTEXT_AT = {4: {(0, 0): (0,), (0, 1): (1,), (1, 0): (2,), (2, 0): (3,), (2, 1): (4,)},
                      8: {(n, 0): (n,) for n in range(SPLITS)}}

        def units_vector(v, L):
            n = L.np

            def pair(b, last, start=False):
                for s_ in range(2 * n):
                    u = b * n + s_
                    unit_vector_rests(v, L, u)
                    if not (start and s_ == 0):
                        store_head(v, L, u - 1)
                    for place in range(2):
                        for part in CONTEXT_AT[n].get((s_ % n, place), ()):
                            if s_ < n or not last:
                                context_head(v, L, b + s_ // n + 1, (s_ // n + 1) % 2, part)
                            elif L is L0:
                                context_head(v, L1, 0, 0, part)
                        if place == 0 and (s_ < 2 * n - 1 or not last):
                            unit_vector_max(v, L, u + 1, (s_ + 1) % 2)
                        if place == 0 and not (start and s_ == 0):
                            store_rest(v, L, u - 1)
                    normalise(v, L, u)
            pair(0, False, True)
            over_batch_pairs(v, 1, pair)
            store_head(v, L, B * n - 1)
            store_rest(v, L, B * n - 1)

        def project_tensor(pe, L):
            pe.wait_ge(L.wvo, 64)
            pe.wait_ge(L.wvs, 4)
            pe.wait_ge(L.oT, B * L.np - 1)
            for j in range(L.np):
                if j == 1:
                    turn_result(pe, L, B * L.np - 1)
                if j == L.np - 1:
                    pe.wait_ge(L.oT, B * L.np)
                if j >= 2:
                    pe.wait_ge(L.ao, j - 1)
                for n in range(5):
                    for h in range(2):
                        c = slice(j * P + h * 64, j * P + h * 64 + 64)
                        head, rest = L.qa6[:, :, j, 0, h, :], L.qa6[:, :, j, 1, h, :]
                        both = L.qb6[:, :, j, 0, h, :]
                        w, x = ((L.vh0[:, c], head), (L.vh0[:, c], rest), (L.vl0[:, c], head),
                                (L.vh1[:, c], both), (L.vl1[0:C1, c], both[0:C1]))[n]
                        i = pe.matmul(PS[h * 64:h * 64 + 64, j % 2, :].rearrange("p (b q) -> p b q", b=B), w, x,
                                      start=(n == 0), stop=(n == 4))
                i.then_inc(L.av, 1)
            for t in range(NT):
                for j in range(L.np):
                    pe.wait_ge(L.ao, j + 1)
                    i = pe.matmul(PS[:, 2 + t, 0:D], L.xq[:, j, t * P:(t + 1) * P], L.wo[:, j, :],
                                  start=(j == 0), stop=(j == L.np - 1))
                i.then_inc(L.y, 1)

        def split_values(g_, L):
            g_.wait_ge(L.wvo, 64)
            if L.g0:
                g_.wait_ge(L.prep, SPLITS * B)
            g_.tensor_copy(L.vh0, L.wv[:, 0, :]).then_inc(L.wvs, 1)
            g_.tensor_copy(L.vh1, L.wv[:, 1, :]).then_inc(L.wvs, 1)
            g_.wait_ge(L.wvs, 2)
            g_.tensor_tensor(L.vl0, L.wv[:, 0, :], L.vh0, ALU.subtract).then_inc(L.wvs, 1)
            g_.tensor_tensor(L.vl1, L.wv[:, 1, :], L.vh1, ALU.subtract).then_inc(L.wvs, 1)

        def project_scalar(s, L):
            for j in range(L.np):
                s.wait_ge(L.av, j + 1)
                s.copy(L.xq[:, j, :], PS[:, j % 2, :]).then_inc(L.ao, 1)

        def project_vector(v, L):
            v.wait_ge(s_bias, 48)
            row_ = bias_x1 if L.g0 else bias_x0
            for t in range(NT):
                i = v.tensor_tensor(X[:, t, :], X[:, t, :], row_, ALU.add)
            vlink(v, i)

        def project_finish(L):
            def finish(v, t):
                v.wait_ge(L.y, t + 1)
                return v.tensor_tensor(X[:, t, :], PS[:, 2 + t, 0:D], X[:, t, :], ALU.add)
            return finish

        def cross_tensor(pe, L):
            queries_tensor(pe, L)
            units_tensor(pe, L)
            project_tensor(pe, L)

        def cross_scalar(s, L):
            queries_scalar(s, L)
            units_scalar(s, L)
            project_scalar(s, L)

        def cross_vector(v, L):
            queries_vector(v, L)
            units_vector(v, L)
            project_vector(v, L)

        L0 = Cross("l0x", 8, 0)
        L1 = Cross("l1x", 16, B)
        s_out = sem("s_out")
        x_done = sem("x_done")

        def cross_loads_qk(sp, L, w):
            sp.dma_start(L.wq, w["wq"].rearrange("(k p) n -> p k n", p=P)).then_inc(L.wqk, 16)
            wk = w["wkT"].rearrange("(j p) c -> p j c", p=P)
            sp.dma_start(L.wk[:, :, 0:CD], wk).then_inc(L.wqk, 16)
            sp.dma_start(L.wk[:, :, CD:256], wk[:, :, C0:CD]).then_inc(L.wqk, 16)

        def cross_loads_vo(sp, L, w):
            sp.dma_start(L.wv[:, 0, :], w["wv"][0:C0, :]).then_inc(L.wvo, 16)
            sp.dma_start(L.wv[0:C1, 1, :], w["wv"][C0:CD, :]).then_inc(L.wvo, 16)
            sp.dma_start(L.wv[C1:P, 1, :], w["wv"][C0:CD, :]).then_inc(L.wvo, 16)
            sp.dma_start(L.wo, w["wo"].rearrange("(j p) n -> p j n", p=P)).then_inc(L.wvo, 16)


        QT = A[:, 0:2 * T].rearrange("p (f n) -> p f n", f=2)
        KB = A[:, 2 * T:6 * T].rearrange("p (f e n) -> p f e n", f=2, e=2)
        OT = A[:, 6 * T:8 * T].rearrange("p (f n) -> p f n", f=2)
        blk = Pr[:, 0:6 * T].rearrange("p (i n) -> p i n", i=6)
        PTs = QB[:, 0:4 * T].rearrange("p (g t q) -> p g t q", g=4, t=NT)
        Vb_ = QB[:, 4 * T:8 * T]
        Vb = Vb_.rearrange("p (b d) -> p b d", b=B)
        smx = small[:, 128:160].rearrange("p (i h) -> p i h", i=4)
        ssm = small[:, 160:192].rearrange("p (i h) -> p i h", i=4)
        NG = 8

        class Self:

            def __init__(self, n, rope, w):
                self.wl = sem(f"{n}_wl")
                self.p = sem(f"{n}_p")
                self.pe = sem(f"{n}_pe")
                if rope:
                    self.sum = sem(f"{n}_sum")
                self.v = sem(f"{n}_v")
                self.vz = sem(f"{n}_vz")
                self.ve = sem(f"{n}_ve")
                if not rope:
                    self.qt = sem(f"{n}_qt")
                self.kb = sem(f"{n}_kb")
                self.s = sem(f"{n}_s")
                self.m = sem(f"{n}_m")
                self.ex = sem(f"{n}_ex")
                self.rs = sem(f"{n}_rs")
                self.pn = sem(f"{n}_pn")
                self.t = sem(f"{n}_t")
                self.te = sem(f"{n}_te")
                self.o = sem(f"{n}_o")
                self.oe = sem(f"{n}_oe")
                self.y = sem(f"{n}_y")
                self.n, self.rope, self.w = n, rope, w

        WA = QA[:, 4096:4096 + 6 * 512].rearrange("p (w k n) -> p w k n", w=6, k=2)
        WB = WQK[:, 0:6 * D].rearrange("p (k w n) -> p w k n", k=2, w=3)
        SA = Self("l0a", True, WA)
        SB = Self("l1a", False, WB)
        b_c = small[:, 64:70]
        b_eo = small[:, 72:76].rearrange("p (e f) -> p e f", e=2)
        s_mask = sem("s_mask")

        def block_of(n):
            return blk[:, (n + 2) % 6, :]

        def self_tensor(pe, L):
            pe.wait_ge(L.wl, 16 * (6 if L.rope else 2))
            nw = 4 if L.rope else 2
            for f in range(2):
                for w in range(nw):
                    for k in range(2):
                        i = pe.matmul(PS[:, (4 * f if L.rope else 4 + 2 * f) + w, :], L.w[:, w, k, f * P:(f + 1) * P],
                                      xnT[:, k, :], start=(k == 0), stop=(k == 1))
                    i.then_inc(L.p, 1)

            def scores_of(n):
                f, g = n // 4, n % 4
                if f:
                    pe.wait_ge(L.m, g + 1)
                if L.rope:
                    pe.matmul(PS[:, g, :].rearrange("p (x k) -> p x k", k=S), one16[:, :],
                              mask16[:, :].unsqueeze(1).to_broadcast([P, 8, S]), start=True, stop=False,
                              skip_group_check=True)
                for b in range(B):
                    i = pe.matmul(PS[64 * (b % 2):64 * (b % 2) + 64, g, (b // 2) * P:(b // 2 + 1) * P]
                                  .rearrange("p (e n) -> p e n", e=2),
                                  QT[32 * g:32 * g + 32, f, b * S:(b + 1) * S],
                                  KB[32 * g:32 * g + 32, f, :, b * S:(b + 1) * S], start=not L.rope, stop=True,
                                  skip_group_check=True)
                i.then_inc(L.s, 1)

            def attend_of(n):
                f, g = n // 4, n % 4
                pe.wait_ge(L.te, n + 1)
                if n == 0:
                    pe.wait_ge(L.ve, 8)
                for b in range(B):
                    i = pe.matmul(PS[32 * g:32 * g + 32, 6 + f, b * S:(b + 1) * S],
                                  Vb[:, b, f * P + 32 * g:f * P + 32 * g + 32],
                                  PTs[:, g, b // 2, (b % 2) * S:(b % 2 + 1) * S], start=True, stop=True)
                i.then_inc(L.o, 1)

            if L.rope:
                pe.wait_ge(L.pe, 4)
                pe.wait_ge(s_mask, 2)
            pe.wait_ge(L.sum if L.rope else L.qt, 1)
            pe.wait_ge(L.kb, 2)
            for n in range(4):
                scores_of(n)
            if L.rope:
                pe.wait_ge(L.pe, 8)
            else:
                pe.wait_ge(L.qt, 2)
                pe.wait_ge(L.kb, 4)
            for t in range(NT):
                for k in range(2):
                    i = pe.matmul(PS[:, 6 + t // 2, (t % 2) * D:(t % 2 + 1) * D], xnT[:, k, t * P:(t + 1) * P],
                                  L.w[:, nw, k, :], start=(k == 0), stop=(k == 1))
                if t % 2:
                    i.then_inc(L.v, 1)
            pe.wait_ge(L.sum if L.rope else L.qt, 3 if L.rope else 2)
            pe.wait_ge(L.kb, 4)
            for n in range(NG):
                if n < 4:
                    scores_of(4 + n)
                pe.wait_ge(L.pn, n + 1)
                if n >= 2:
                    pe.wait_ge(L.te, n - 1)
                for t in range(NT):
                    i = pe.transpose(PS[:, 4 + n % 2, t * P:(t + 1) * P], block_of(n)[:, t * P:(t + 1) * P], ident[:, :])
                i.then_inc(L.t, 1)
                if n:
                    attend_of(n - 1)
            attend_of(NG - 1)
            pe.wait_ge(L.oe, 2)
            for t in range(NT):
                for f in range(2):
                    if L.rope:
                        i = pe.matmul(PS[:, t, 0:D], OT[:, f, t * P:(t + 1) * P], L.w[:, 5, f, :],
                                      start=(f == 0), stop=(f == 1))
                    else:
                        i = pe.transpose(PS[:, t, f * P:(f + 1) * P], OT[:, f, t * P:(t + 1) * P], ident[:, :])
                i.then_inc(L.y, 1)

        def self_scalar(s, L):
            for f in range(2):
                if L.rope:
                    s.wait_ge(L.sum, 2 * f + 2)
                    for e in range(2):
                        s.activation(KB[:, f, e, :], blk[:, 2 - 2 * f, :], ACT.Copy, scale=eo[:, e:e + 1])\
                            .then_inc(L.kb, 1)
                else:
                    s.wait_ge(L.p, 2 * f + 1)
                    s.wait_ge(L.wl, 32)
                    s.activation(QT[:, f, :], PS[:, 4 + 2 * f, :], ACT.Identity, bias=b_c[:, f:f + 1]).then_inc(L.qt, 1)

            def exponentials(n):
                s.wait_ge(L.m, n + 1)
                s.activation(block_of(n), block_of(n), ACT.Exp, scale=0.25).then_inc(L.ex, 1)

            def store_turned(n):
                s.wait_ge(L.t, n + 1)
                if n >= 4:
                    s.wait_ge(L.o, n - 3)
                s.copy(PTs[:, n % 4, :, :], PS[:, 4 + n % 2, :].rearrange("p (t q) -> p t q", t=NT)).then_inc(L.te, 1)

            def store_output(f):
                s.wait_ge(L.o, 4 * f + 4)
                if L.rope:
                    s.copy(OT[:, f, :], PS[:, 6 + f, :]).then_inc(L.oe, 1)
                else:
                    s.activation(OT[:, f, :], PS[:, 6 + f, :], ACT.Identity, bias=b_c[:, 4 + f:5 + f]).then_inc(L.oe, 1)

            for n in range(4):
                exponentials(n)
            s.wait_ge(L.vz, 1)
            for half in range(2):
                s.wait_ge(L.v, half + 1)
                for o in range(2):
                    for bb in range(2):
                        src = PS[64 * bb:64 * bb + 64, 6 + half, :].rearrange("p (t h o d) -> p t h o d", t=2, o=2, d=DK)
                        dst = Vb_[64 * o:64 * o + 64, half * 4 * D:(half + 1) * 4 * D]\
                            .rearrange("p (t b h o d) -> p t b h o d", t=2, b=2, o=2, d=DK)
                        s.copy(dst[:, :, bb, :, o, :], src[:, :, :, o, :]).then_inc(L.ve, 1)
            for n in range(4):
                store_turned(n)
                exponentials(4 + n)
            store_turned(4)
            store_turned(5)
            store_output(0)
            store_turned(6)
            store_turned(7)
            store_output(1)

        def by_batch(ap):
            return ap.rearrange("p (b q) -> p b q", b=B)

        def over(ap, shape, axis):
            return ap.unsqueeze(axis).to_broadcast(shape)

        PARTS = ((0, 1), (2, 3), (4, 5), (0, 1))

        def self_vector(v, L):
            if L.rope:
                v.wait_ge(s_const, 16 * 4)
                v.tensor_copy(mask16[:, :], cmask[:, :]).then_inc(s_mask, 1)
                v.tensor_copy(one16[:, :], ident[:, :]).then_inc(s_mask, 1)
                for n in range(4):
                    if n == 3:
                        v.wait_ge(L.sum, 1)
                    for i, table in enumerate((cosT, sinT)):
                        v.wait_ge(L.p, 2 * n + i + 1)
                        v.tensor_tensor(by_batch(blk[:, PARTS[n][i], :]), by_batch(PS[:, 2 * n + i, :]),
                                        over(table[:, :], [P, B, S], 1), ALU.mult).then_inc(L.pe, 1)
            else:
                v.wait_ge(L.wl, 32)
                for e in range(2):
                    i = v.tensor_scalar(b_eo[:, e, :], b_c[:, 2:4], eo[:, e:e + 1], None, ALU.mult)
                vlink(v, i)
                for f in range(2):
                    v.wait_ge(L.p, 2 * f + 2)
                    for e in range(2):
                        v.tensor_scalar(KB[:, f, e, :], PS[:, 5 + 2 * f, :], eo[:, e:e + 1], b_eo[:, e, f:f + 1],
                                        ALU.mult, ALU.add).then_inc(L.kb, 1)

            def less_maxima(n):
                sc = PS[:, n % 4, :].rearrange("p (h k) -> p h k", k=S)
                v.wait_ge(L.s, n + 1)
                vlink(v, v.tensor_reduce(smx[:, n % 4, :], sc, AXX, ALU.max))
                if L.rope and n == 2:
                    v.wait_ge(L.sum, 3)
                if n >= 6:
                    v.wait_ge(L.t, n - 5)
                v.tensor_tensor(block_of(n).rearrange("p (h k) -> p h k", k=S), sc,
                                over(smx[:, n % 4, :], [P, 8, S], 2), ALU.subtract).then_inc(L.m, 1)

            def sums(n):
                v.wait_ge(L.ex, n + 1)
                if n >= 4:
                    v.wait_ge(L.pn, n - 3)
                vlink(v, v.tensor_reduce(ssm[:, n % 4, :], block_of(n).rearrange("p (h k) -> p h k", k=S), AXX, ALU.add))
                v.reciprocal(ssm[:, n % 4, :], ssm[:, n % 4, :]).then_inc(L.rs, 1)

            for n in range(NG + 1):
                if n < NG:
                    less_maxima(n)
                if n:
                    sums(n - 1)

        def self_gpsimd(g, L, cross):
            g.wait_ge(cross.av, cross.np)
            g.memset(Vb_, 0.0).then_inc(L.vz, 1)
            if L.rope:
                for n in range(4):
                    g.wait_ge(L.pe, 2 * n + 2)
                    one, two = (blk[:, i, :] for i in PARTS[n])
                    i = g.tensor_tensor(one if n % 2 else QT[:, n // 2, :], one, two, ALU.add)
                    i.then_inc(L.sum, 1)
            for n in range(NG):
                g.wait_ge(L.rs, n + 1)
                p3 = block_of(n).rearrange("p (h k) -> p h k", k=S)
                g.tensor_tensor(p3, p3, over(ssm[:, n % 4, :], [P, 8, S], 2), ALU.mult).then_inc(L.pn, 1)

        def self_finish(L):
            def finish(v, t):
                v.wait_ge(L.y, t + 1)
                return v.tensor_tensor(X[:, t, :], PS[:, t, 0:D], X[:, t, :], ALU.add)
            return finish

        W1 = QB[:, 4096:6144].rearrange("p (k n) -> p k n", k=2)
        W2 = QB[:, 6144:8192].rearrange("p (f n) -> p f n", f=8)
        NF = FF // P
        fbuf = QA[:, 0:16 * T].rearrange("p (i n) -> p i n", i=16)
        F_C, F_B, F_G0, F_D, F_Y, F_O, F_N, F_E = (0, 3), (3, 2), (5, 2), (7, 2), (9, 1), (10, 2), (12, 3), (15, 1)

        def fb(f, place):
            first, copies = place
            return fbuf[:, first + f % copies, :]

        for k in ("f_w", "f_b1", "f_h", "f_a", "f_v", "f_g", "f_d", "f_n", "f_u", "f_x", "f_e"):
            LN[k] = sem(k)
        STEP = ROUND * 64

        def ffn_tensor(pe):
            pe.wait_ge(LN["f_w"], 48)
            def up(f):
                if f >= 4:
                    pe.wait_ge(LN["f_a"], f - 3)
                for k in range(2):
                    i = pe.matmul(PS[:, (0, 1, 6, 7)[f % 4], :], W1[:, k, f * P:(f + 1) * P], xnT[:, k, :],
                                  start=(k == 0), stop=(k == 1))
                i.then_inc(LN["f_h"], 1)
            for f in range(NF + 3):
                if f < NF:
                    up(f)
                if f >= 3:
                    c = f - 3
                    pe.wait_ge(LN["f_n"], c + 1)
                    for t in range(NT):
                        i = pe.matmul(PS[:, 2 + t, 0:D], fb(c, F_O)[:, t * P:(t + 1) * P], W2[:, c, :],
                                      start=(c == 0), stop=(c == NF - 1))
                        if c == NF - 1 or t == NT - 1:
                            i.then_inc(LN["f_u"], 1)

        def ffn_scalar(s):
            s.wait_ge(LN["f_b1"], 1)

            def hidden(f):
                s.wait_ge(LN["f_h"], f + 1)
                if f >= 3:
                    s.wait_ge(LN["f_n"], f - 2)
                s.activation(fb(f, F_N), PS[:, (0, 1, 6, 7)[f % 4], :], ACT.Identity, bias=b1_c[:, f:f + 1], scale=256.0)\
                    .then_inc(LN["f_a"], 1)
            hidden(0)
            for f in range(NF):
                if f + 1 < NF:
                    hidden(f + 1)
                s.wait_ge(LN["f_v"], f + 1)
                if f:
                    s.wait_ge(LN["f_e"], f)
                s.activation(fb(f, F_E), fb(f, F_B), ACT.Identity, bias=nstep).then_inc(LN["f_x"], 1)
                s.activation(fb(f, F_G0), fb(f, F_B), ACT.Gelu, bias=gel0, scale=2.0 ** -8)
                s.activation(fb(f, F_D), fb(f, F_B), ACT.Gelu, bias=gel1, scale=2.0 ** -8).then_inc(LN["f_g"], 1)

        def ffn_vector(v):
            v.wait_ge(LN["f_w"], 48)
            v.tensor_scalar(b1_c, b1_c, 256.0, None, ALU.mult).then_inc(LN["f_b1"], 1)
            v.wait_ge(s_bias, 48)
            vlink(v, v.tensor_scalar(bias_f, bias_f, 256.0, None, ALU.mult))
            for f in range(NF + 2):
                g = f - 2
                if f < NF:
                    v.wait_ge(LN["f_a"], f + 1)
                    rounded = vmark(v.tensor_scalar(fb(f, F_N), fb(f, F_N), ROUND, ROUND, ALU.add, ALU.subtract))
                if g >= 0:
                    v.wait_ge(LN["f_d"], g + 1)
                    product = vmark(v.scalar_tensor_tensor(out=fb(g, F_D), in0=fb(g, F_D), scalar=4.0,
                                                           in1=fb(g, F_C), op0=ALU.mult, op1=ALU.mult))
                if f < NF:
                    v.wait_ge(vch, rounded)
                    clamped = vmark(v.tensor_scalar(fb(f, F_C), fb(f, F_N), -1024.0, 1024.0, ALU.max, ALU.min))
                if g >= 0:
                    v.wait_ge(vch, product)
                    total = vmark(v.scalar_tensor_tensor(out=fb(g, F_Y), in0=fb(g, F_G0), scalar=256.0,
                                                         in1=fb(g, F_D), op0=ALU.mult, op1=ALU.add))
                if f < NF:
                    v.wait_ge(vch, clamped)
                    v.tensor_scalar(fb(f, F_B), fb(f, F_C), -31.5, STEP, ALU.add, ALU.add).then_inc(LN["f_v"], 1)
                if g >= 0:
                    v.wait_ge(vch, total)
                    less = vmark(v.tensor_scalar(fb(g, F_Y), fb(g, F_Y), ROUND, ROUND + 1024.0,
                                                 ALU.add, ALU.subtract))
                if g >= 0:
                    v.wait_ge(vch, less)
                    if g >= 2:
                        v.wait_ge(LN["f_u"], g - 1)
                    v.scalar_tensor_tensor(out=fb(g, F_O), in0=fb(g, F_N), scalar=1024.0, in1=fb(g, F_Y),
                                           op0=ALU.max, op1=ALU.add).then_inc(LN["f_n"], 1)

        def ffn_gpsimd(g_):
            for f in range(NF):
                g_.wait_ge(LN["f_x"], f + 1)
                g_.tensor_tensor(fb(f, F_C), fb(f, F_E), fb(f, F_C), ALU.subtract).then_inc(LN["f_e"], 1)
                g_.wait_ge(LN["f_g"], f + 1)
                g_.tensor_tensor(fb(f, F_D), fb(f, F_G0), fb(f, F_D), ALU.subtract).then_inc(LN["f_d"], 1)

        def ffn_finish(v, t):
            v.wait_ge(LN["f_u"], NF + t)
            z = fbuf[:, t, 0:D]
            vlink(v, v.tensor_tensor(z, PS[:, 2 + t, 0:D], bias_f, ALU.add))
            vlink(v, v.tensor_scalar(z, z, ROUND, ROUND, ALU.add, ALU.subtract))
            return v.scalar_tensor_tensor(out=X[:, t, :], in0=z, scalar=1.0 / 256, in1=X[:, t, :],
                                          op0=ALU.mult, op1=ALU.add)

        NS = 8
        slot = QA[:, 0:NS * 768].rearrange("p (s w) -> p s w", s=NS)
        wsh = WQK[:, 1536:3584].rearrange("p (k n) -> p k n", k=2)
        wdn = rawR[:, 0:4 * D].rearrange("p (c n) -> p c n", c=4)
        wrt = rawR[:, 1024:1024 + 2 * 65].rearrange("p (k n) -> p k n", k=2)
        tri = rawR[:, 1280:1280 + 2 * P].rearrange("p (i n) -> p i n", i=2)
        hsh = QB[:, 1024:1024 + 4 * T].rearrange("p (c n) -> p c n", c=4)
        sg = QB[:, 3072:3072 + 2 * T].rearrange("p (i n) -> p i n", i=2)
        wthl = QB[:, 4096:4096 + NT * E].bitcast(F16).rearrange("p (t e s) -> p t e s", t=NT, s=2)
        posm = QB[:, 4352:4352 + NT * E].rearrange("p (t e) -> p t e", t=NT)
        xh = PT[:, 0:NT * D].rearrange("p (t d) -> p t d", t=NT)
        xl = PT[:, NT * D:2 * NT * D].rearrange("p (t d) -> p t d", t=NT)
        iota = rawR[:, 1536:1600].bitcast(F16)
        id16 = rawR[:, 1600:1664].bitcast(F16)
        hf = rawR[:, 1664:1920].rearrange("p (i n) -> p i n", i=2)
        oh = raw0[:, 0:512].bitcast(F16).rearrange("p (i t n) -> p i t n", i=2, t=NT)
        oht = raw0[:, 512:1536].bitcast(F16).rearrange("p (i n) -> p i n", i=4)
        xg = raw1[:, 0:512].bitcast(F16).rearrange("p (i s k n) -> p i s k n", i=2, s=2, k=2)
        sl = raw1[:, 512:768].rearrange("p (i n) -> p i n", i=2)
        hh = raw1[:, 768:1024].bitcast(F16).rearrange("p (i s n) -> p i s n", i=2, s=2)
        oo = raw1[:, 1024:1536].bitcast(F16).rearrange("p (i s n) -> p i s n", i=2, s=2)
        wh = Pr[:, 0:3072].bitcast(F16).rearrange("p (i s w) -> p i s w", i=4, s=2)
        wsl = small[:, 250:254]
        lg = QB[:, 5120:5120 + NT * E].rearrange("p (t e) -> p t e", t=NT)
        sel = QB[:, 5376:5376 + NT * E].rearrange("p (t e) -> p t e", t=NT)
        wt = QB[:, 5632:5632 + NT * E].rearrange("p (t e) -> p t e", t=NT)
        sgm = small[:, 200:204]
        rm = small[:, 204:208]
        rs = small[:, 208:212]
        top = small[:, 216:248].rearrange("p (t k) -> p t k", t=NT)
        for k in ("m_w", "m_r", "m_rm", "m_re", "m_sel", "m_pos", "m_sh", "m_sg", "m_hs", "m_ys", "m_yd", "m_wt", "m_xh",
                  "m_xl"):
            LN[k] = sem(k)
        e_oh = sem("e_oh")
        e_turn = sem("e_turn")
        e_oht = sem("e_oht")
        e_gather = sem("e_gather")
        e_xg = sem("e_xg")
        e_cast = sem("e_cast")
        e_split = sem("e_split")
        e_gu = sem("e_gu")
        e_silu = sem("e_silu")
        e_hf = sem("e_hf")
        e_hh = sem("e_hh")
        e_hl = sem("e_hl")
        e_out = sem("e_out")
        e_ohi = sem("e_ohi")
        e_ol = sem("e_ol")
        e_comb = sem("e_comb")
        e_w = [sem(f"e_w{n}") for n in range(NS)]

        SHB = (2, 4)

        def router_tensor(pe):
            pe.wait_ge(LN["m_w"], 96)
            for t in range(NT):
                for k in range(2):
                    i = pe.matmul(PS[:, 0, t * P:t * P + 65], xnT[:, k, t * P:(t + 1) * P], wrt[:, k, :],
                                  start=(k == 0), stop=(k == 1))
            i.then_inc(LN["m_r"], 1)
            for c in range(4):
                if c == 3:
                    pe.wait_ge(LN["m_sel"], 1)
                    for t in range(NT):
                        for s_ in range(t + 1):
                            i = pe.matmul(PS[:, 1, t * P:t * P + E], tri[:, 0 if s_ == t else 1, :], sel[:, s_, :],
                                          start=(s_ == 0), stop=(s_ == t))
                    i.then_inc(LN["m_pos"], 1)
                if c >= 2:
                    pe.wait_ge(LN["m_hs"], c - 1)
                for h in range(2):
                    for k in range(2):
                        i = pe.matmul(PS[:, SHB[c % 2] + h, :], wsh[:, k, h * ISH + c * P:h * ISH + (c + 1) * P],
                                      xnT[:, k, :], start=(k == 0), stop=(k == 1))
                i.then_inc(LN["m_sh"], 1)
            pe.wait_ge(LN["m_hs"], 4)
            for t in range(NT):
                for c in range(4):
                    i = pe.matmul(PS[:, 6 + t // 2, (t % 2) * D:(t % 2 + 1) * D], hsh[:, c, t * P:(t + 1) * P],
                                  wdn[:, c, :], start=(c == 0), stop=(c == 3))
                if t % 2:
                    i.then_inc(LN["m_ys"], 1)

        def router_scalar(s):
            s.wait_ge(LN["m_rm"], 1)
            for t in range(NT):
                i = s.activation(lg[:, t, :], PS[:, 0, t * P:t * P + E], ACT.Exp, bias=rm[:, t:t + 1])
            i.then_inc(LN["m_re"], 1)
            s.activation(sgm, PS[:, 0, :].rearrange("p (t e) -> p t e", t=NT)[:, :, E], ACT.Exp, scale=-1.0)\
                .then_inc(LN["m_re"], 1)
            for c in range(4):
                s.wait_ge(LN["m_sh"], c + 1)
                if c >= 2:
                    s.wait_ge(LN["m_hs"], c - 1)
                s.activation(sg[:, c % 2, :], PS[:, SHB[c % 2], :], ACT.Silu).then_inc(LN["m_sg"], 1)

        def router_vector(v):
            v.wait_ge(LN["m_r"], 1)
            lp = PS[:, 0, :].rearrange("p (t e) -> p t e", t=NT)[:, :, 0:E]
            v.tensor_reduce(rm, lp, AXX, ALU.max, negate=True).then_inc(LN["m_rm"], 1)
            v.tensor_copy(xh, XN).then_inc(LN["m_xh"], 1)

            def shared_hidden(c):
                v.wait_ge(LN["m_sg"], c + 1)
                v.tensor_tensor(hsh[:, c, :], PS[:, SHB[c % 2] + 1, :], sg[:, c % 2, :], ALU.mult)\
                    .then_inc(LN["m_hs"], 1)
            v.wait_ge(LN["m_re"], 1)
            vlink(v, v.tensor_reduce(rs, lg, AXX, ALU.add))
            vlink(v, v.reciprocal(rs, rs))
            vlink(v, v.tensor_tensor(lg, lg, over(rs, [P, NT, E], 2), ALU.mult))
            for t in range(NT):
                i = v.max(top[:, t, :], lg[:, t, :])
            vlink(v, i)
            for t in range(NT):
                i = v.match_replace(sel[:, t, :], top[:, t, :], lg[:, t, :], -1.0)
            vlink(v, i)
            v.tensor_scalar(sel, sel, 0.0, None, ALU.is_lt).then_inc(LN["m_sel"], 1)
            shared_hidden(0)
            vlink(v, v.tensor_reduce(rs, top, AXX, ALU.add))
            vlink(v, v.reciprocal(rs, rs))
            v.wait_ge(LN["m_sel"], 1)
            vlink(v, v.tensor_tensor(wt, lg, sel, ALU.mult))
            vlink(v, v.tensor_tensor(wt, wt, over(rs, [P, NT, E], 2), ALU.mult))
            shared_hidden(1)
            shared_hidden(2)
            v.wait_ge(LN["m_pos"], 1)
            pos = PS[:, 1, :].rearrange("p (t e) -> p t e", t=NT)[:, :, 0:E]
            vlink(v, v.scalar_tensor_tensor(out=sel, in0=pos, scalar=float(CAPACITY), in1=sel,
                                            op0=ALU.is_lt, op1=ALU.mult))
            vlink(v, v.scalar_tensor_tensor(out=posm, in0=pos, scalar=1.0, in1=sel, op0=ALU.add, op1=ALU.mult))
            v.tensor_scalar(posm, posm, -1.0, None, ALU.add).then_inc(LN["m_wt"], 1)
            vlink(v, v.tensor_tensor(wt, wt, sel, ALU.mult))
            vlink(v, v.tensor_copy(wthl[:, :, :, 0], wt))
            v.tensor_tensor(wthl[:, :, :, 1], wt, wthl[:, :, :, 0], ALU.subtract).then_inc(LN["m_wt"], 1)
            shared_hidden(3)
            v.wait_ge(LN["m_re"], 2)
            vlink(v, v.tensor_scalar(sgm, sgm, 1.0, None, ALU.add))
            vlink(v, v.reciprocal(sgm, sgm))

        def add_shared(v):
            for t in range(NT):
                v.wait_ge(LN["m_ys"], t // 2 + 1)
                v.scalar_tensor_tensor(out=X[:, t, :], in0=PS[:, 6 + t // 2, (t % 2) * D:(t % 2 + 1) * D],
                                       scalar=sgm[:, t:t + 1], in1=X[:, t, :], op0=ALU.mult, op1=ALU.add)\
                    .then_inc(LN["m_yd"], 1)

        def after(eng, sm, n):
            if not isinstance(n, int) or n > 0:
                eng.wait_ge(sm, n)

        def expert_turn_and_gather(pe, e, n):
            after(pe, e_oh, e + 1)
            after(pe, e_oht, e)
            ids = bass.ds(e, 1) if not isinstance(e, int) else slice(e, e + 1)
            for t in range(NT):
                pe.matmul(PS[:, 4, 256:258], oh[:, n % 2, t, :],
                          wthl[:, t, ids, :].rearrange("p e s -> p (e s)"), start=(t == 0), stop=(t == NT - 1))
            t16 = PS[:, 4, 0:256].bitcast(F16)
            for t in range(NT):
                i = pe.transpose(t16[:, t * P:(t + 1) * P], oh[:, n % 2, t, :], id16)
            i.then_inc(e_turn, 1)
            after(pe, e_xg, e - 1)
            for m, x in ((0, xh), (1, xl)):
                for k in range(2):
                    for t in range(NT):
                        i = pe.matmul(PS[:, n % 2, (2 * m + k) * P:(2 * m + k + 1) * P], x[:, t, k * P:(k + 1) * P],
                                      oh[:, n % 2, t, :], start=(t == 0), stop=(t == NT - 1))
            i.then_inc(e_gather, 1)

        def expert_gate_up(pe, e, n):
            w = wh[:, n % 4, :, 0:512].rearrange("p s (k f) -> p s k f", k=2)
            after(pe, e_xg, e + 1)
            after(pe, e_split, e + 1)
            after(pe, e_hf, e - 1)
            for h in range(2):
                for n_, (a_, b_, k) in enumerate([(a_, b_, k) for a_, b_ in ((0, 0), (0, 1), (1, 0)) for k in range(2)]):
                    i = pe.matmul(PS[:, 2 + n % 2, h * P:(h + 1) * P], w[:, a_, k, h * P:(h + 1) * P],
                                  xg[:, n % 2, b_, k, :], start=(n_ == 0), stop=(n_ == 5))
            i.then_inc(e_gu, 1)

        def expert_down(pe, e, n):
            after(pe, e_hl, e + 1)
            after(pe, e_ol, e)
            for n_, (a_, b_) in enumerate(((0, 0), (0, 1), (1, 0))):
                i = pe.matmul(PS[:, 5, 0:D], hh[:, n % 2, a_, :], wh[:, n % 4, b_, 512:768],
                              start=(n_ == 0), stop=(n_ == 2))
            i.then_inc(e_out, 1)

        def expert_combine(pe, e, n):
            after(pe, e_ol, e + 1)
            if isinstance(e, int) and e == 0:
                pe.wait_ge(LN["m_yd"], NT)
            for t in range(NT):
                for m in range(2):
                    i = pe.matmul(PS[:, 6 + t // 2, (t % 2) * D:(t % 2 + 1) * D], oht[:, n % 4, t * P:(t + 1) * P],
                                  oo[:, n % 2, m, :], start=(isinstance(e, int) and e == 0 and t % 2 == 0 and m == 0),
                                  stop=(isinstance(e, int) and e == E - 1), skip_group_check=True)
            i.then_inc(e_comb, 1)

        def experts(eng, step):
            for e in range(-3, NS):
                step(e, e % NS)
            with eng.Fori(1, E // NS - 1) as c:
                for n in range(NS):
                    step(c * NS + n, n)
            for n in range(NS):
                step(E - NS + n, n)

        def is_expert(e):
            return not isinstance(e, int) or 0 <= e < E

        def experts_tensor(pe):
            pe.wait_ge(LN["m_wt"], 2)
            pe.wait_ge(LN["m_xl"], 1)

            def step(e, n):
                if is_expert(e + 1):
                    expert_gate_up(pe, e + 1, (n + 1) % NS)
                if is_expert(e):
                    expert_down(pe, e, n)
                if is_expert(e + 2):
                    expert_turn_and_gather(pe, e + 2, (n + 2) % NS)
                if is_expert(e - 1):
                    expert_combine(pe, e - 1, (n - 1) % NS)
            experts(pe, step)
            expert_combine(pe, E - 1, NS - 1)

        def experts_scalar(s):
            s.wait_ge(LN["m_xl"], 1)

            def step(e, n):
                if is_expert(e + 1):
                    after(s, e_gu, e + 2)
                    after(s, e_hf, e)
                    s.activation(sl[:, (n + 1) % 2, :], PS[:, 2 + (n + 1) % 2, 0:P], ACT.Silu).then_inc(e_silu, 1)
                if is_expert(e):
                    after(s, e_out, e + 1)
                    after(s, e_comb, e - 1)
                    after(s, e_oht, e + 1)
                    s.activation(oo[:, n % 2, 0, :], PS[:, 5, 0:D], ACT.Copy, scale=wsl[:, n % 4:n % 4 + 1])\
                        .then_inc(e_ohi, 1)
                if is_expert(e + 3):
                    k = (n + 3) % NS
                    c = (e + 3 - k) // NS if isinstance(e, int) else None
                    s.wait_ge(e_w[k], 32 * (c + 1) if c is not None else (e + (3 - k + NS)) * (32 // NS))
                    after(s, e_out, e)
                    s.copy(wh[:, (n + 3) % 4, 0, :], slot[:, k, :]).then_inc(e_cast, 1)
                if is_expert(e + 2):
                    after(s, e_gather, e + 3)
                    after(s, e_gu, e + 1)
                    s.copy(xg[:, n % 2, :, :, :].rearrange("p s k n -> p (s k n)"), PS[:, n % 2, :]).then_inc(e_xg, 1)
            experts(s, step)

        def experts_vector(v):
            def step(e, n):
                if is_expert(e + 1):
                    m = (n + 1) % 2
                    after(v, e_silu, e + 2)
                    after(v, e_hl, e)
                    v.tensor_tensor(hf[:, m, :], PS[:, 2 + m, P:2 * P], sl[:, m, :], ALU.mult).then_inc(e_hf, 1)
                    after(v, e_out, e)
                    after(v, e_hf, e + 2)
                    v.tensor_copy(hh[:, m, 0, :], hf[:, m, :]).then_inc(e_hh, 1)
                    after(v, e_hh, e + 2)
                    v.tensor_tensor(hh[:, m, 1, :], hf[:, m, :], hh[:, m, 0, :], ALU.subtract).then_inc(e_hl, 1)
                if is_expert(e):
                    after(v, e_ohi, e + 1)
                    v.scalar_tensor_tensor(out=oo[:, n % 2, 1, :], in0=PS[:, 5, 0:D], scalar=wsl[:, n % 4:n % 4 + 1],
                                           in1=oo[:, n % 2, 0, :], op0=ALU.mult, op1=ALU.subtract).then_inc(e_ol, 1)
                if is_expert(e + 2):
                    k = (n + 2) % 4
                    after(v, e_turn, e + 3)
                    after(v, e_comb, e - 1)
                    v.tensor_reduce(wsl[:, k:k + 1], PS[:, 4, 256:258], AXX, ALU.add)
                    v.tensor_copy(oht[:, k, :], PS[:, 4, 0:256].bitcast(F16)).then_inc(e_oht, 1)
                if isinstance(e, int) and e == -1:
                    add_shared(v)
                if is_expert(e + 3):
                    after(v, e_gather, e + 2)
                    x = e + 3
                    for t in range(NT):
                        col = posm[:, t, bass.ds(x, 1)] if not isinstance(x, int) else posm[:, t, x:x + 1]
                        i = v.tensor_scalar(oh[:, (n + 3) % 2, t, :], iota, col, None, ALU.is_equal)
                    i.then_inc(e_oh, 1)
            experts(v, step)
            v.wait_ge(e_comb, E)
            for t in range(NT):
                v.tensor_tensor(X[:, t, :], PS[:, 6 + t // 2, (t % 2) * D:(t % 2 + 1) * D], X[:, t, :], ALU.add)\
                    .then_inc(x_done, 1)

        def experts_gpsimd(g):
            g.wait_ge(LN["m_xh"], 1)
            g.tensor_tensor(xl, XN, xh, ALU.subtract).then_inc(LN["m_xl"], 1)
            g.wait_ge(LN["m_xl"], 1)

            def step(e, n):
                if is_expert(e + 3):
                    after(g, e_cast, e + 4)
                    after(g, e_split, e + 3)
                    g.tensor_tensor(wh[:, (n + 3) % 4, 1, :], slot[:, (n + 3) % NS, :], wh[:, (n + 3) % 4, 0, :],
                                    ALU.subtract).then_inc(e_split, 1)
            experts(g, step)

        def experts_sync(sp):
            def load(e, n):
                after(sp, e_split, e - NS + 1)
                gu = a["L1_ffn_expert_gate_up_w"]
                dn = a["L1_ffn_expert_down_w"]
                ge = gu[bass.ds(e, 1)] if not isinstance(e, int) else gu[e:e + 1]
                de = dn[bass.ds(e, 1)] if not isinstance(e, int) else dn[e:e + 1]
                sp.dma_start(slot[:, n, 0:512].rearrange("p (k f) -> p k f", k=2),
                             ge.rearrange("o (k p) f -> p (o k) f", p=P)).then_inc(e_w[n], 16)
                sp.dma_start(slot[:, n, 512:768], de.rearrange("o p f -> p (o f)")).then_inc(e_w[n], 16)
            for n in range(NS):
                load(n, n)
            with sp.Fori(1, E // NS) as c:
                for n in range(NS):
                    load(c * NS + n, n)

        gam = PT[:, 0:512].bitcast(F32)
        bet = PT[:, 512:1024].bitcast(F32)
        eo = small[:, 70:72]
        s_gb = sem("s_gb")

        block = ctx.enter_context(nc.Block())

        def row(ap):
            return ap.rearrange("(o n) -> o n", o=1).to_broadcast([P, D])

        @block.sync
        def _(sp):
            sp.dma_start(X, a["x"].rearrange("(t p) d -> p t d", p=P)).then_inc(s_x, 16)
            sp.dma_start(ident[:, :], a["ident"]).then_inc(s_ident, 16)
            w0 = {k: a["L0_xattn_" + n] for k, n in (("wq", "Wq"), ("wkT", "WkT"), ("wv", "Wv"), ("wo", "Wout"))}
            w1 = {k: a["L1_xattn_" + n] for k, n in (("wq", "Wq"), ("wkT", "WkT"), ("wv", "Wv"), ("wo", "Wo"))}
            cross_loads_qk(sp, L0, w0)
            sp.wait_ge(s_memset, 6)
            raw_loads(sp, L0, [0])
            for dst, n in ((cosT[:, :], "cos"), (sinT[:, :], "sin"), (cmask[:, :], "cmask"), (eo, "eo")):
                sp.dma_start(dst, a[n]).then_inc(s_const, 16)
            raw_loads(sp, L0, [1])
            cross_loads_vo(sp, L0, w0)
            sp.dma_start(bias_x0, row(a["L0_xattn_bout"])).then_inc(s_bias, 16)
            sp.dma_start(bias_f, row(a["L0_ffn_b2"])).then_inc(s_bias, 16)
            sp.dma_start(bias_x1, row(a["L1_xattn_bo"])).then_inc(s_bias, 16)
            for n, k in enumerate(("PQT", "PQsT", "PKT", "PKsT", "PVT", "POT")):
                sp.dma_start(WA[:, n, :, :], a["L0_attn_" + k].rearrange("(k p) n -> p k n", p=P)).then_inc(SA.wl, 16)
            sp.dma_start(W1, a["L0_ffn_w1"].rearrange("(k p) n -> p k n", p=P)).then_inc(LN["f_w"], 16)
            sp.dma_start(W2, a["L0_ffn_w2"].rearrange("(f p) n -> p f n", p=P)).then_inc(LN["f_w"], 16)
            sp.dma_start(b1_c, a["L0_ffn_b1_cols"]).then_inc(LN["f_w"], 16)
            sp.dma_start(b_c, a["L1_attn_b_cols"]).then_inc(SB.wl, 16)
            sp.wait_ge(L0.w, 2 * L0.heads)
            cross_loads_qk(sp, L1, w1)
            raw_loads(sp, L0, range(2, B))
            raw_loads(sp, L1, [0])
            sp.wait_ge(L0.y, NT)
            cross_loads_vo(sp, L1, w1)
            raw_loads(sp, L1, range(1, B))
            sp.wait_ge(L1.w, 2 * L1.heads)
            sp.dma_start(WQK[:, 0:6 * D].rearrange("p (k n) -> p k n", k=2),
                         a["L1_attn_w_qkvT"].rearrange("(k p) n -> p k n", p=P)).then_inc(SB.wl, 16)
            sp.dma_start(wsh, a["L1_ffn_shared_gate_up_w"].rearrange("(k p) n -> p k n", p=P)).then_inc(LN["m_w"], 16)
            sp.wait_ge(L1.prep, SPLITS * B)
            sp.dma_start(wdn, a["L1_ffn_shared_down_w"].rearrange("(c p) n -> p c n", p=P)).then_inc(LN["m_w"], 16)
            sp.dma_start(wrt, a["L1_ffn_gates"].rearrange("(k p) n -> p k n", p=P)).then_inc(LN["m_w"], 16)
            sp.dma_start(iota, a["iota16"]).then_inc(LN["m_w"], 16)
            sp.dma_start(id16, a["id16"]).then_inc(LN["m_w"], 16)
            sp.dma_start(tri, a["tri"].rearrange("p (i n) -> p i n", i=2)).then_inc(LN["m_w"], 16)
            sp.wait_ge(L1.pv, B * L1.np)
            sp.wait_ge(L1.rest, 4 * B * L1.np)
            sp.dma_start(gam, row(a["L1_attn_ln_gamma"])).then_inc(s_gb, 16)
            sp.dma_start(bet, row(a["L1_attn_ln_beta"])).then_inc(s_gb, 16)
            sp.wait_ge(L1.av, L1.np)
            experts_sync(sp)
            sp.wait_ge(x_done, NT)
            sp.dma_start(out.rearrange("(t p) d -> p t d", p=P), X).then_inc(s_out, 16)
            sp.wait_ge(s_out, 16)

        @block.gpsimd
        def _(g):
            g.memset(CR[:, :].rearrange("p (t n) -> p t n", n=386)[:, :, CD:CD + 1], 1.0).then_inc(s_memset, 1)
            g.memset(rawR[:, (KT - 1) * CD:], 0.0).then_inc(s_memset, 1)
            context_rests(g, L0, range(B))
            context_rests(g, L1, [0])
            split_values(g, L0)
            self_gpsimd(g, SA, L0)
            ffn_gpsimd(g)
            context_rests(g, L1, range(1, B))
            split_values(g, L1)
            self_gpsimd(g, SB, L1)
            experts_gpsimd(g)

        @block.scalar
        def _(s):
            s.wait_ge(s_memset, 6)
            s.activation(small[:, 81:82], eps_c, ACT.Sqrt)
            ln_scalar(s, "l0x")
            cross_scalar(s, L0)
            ln_scalar(s, "l0a")
            self_scalar(s, SA)
            ln_scalar(s, "l0f")
            ffn_scalar(s)
            ln_scalar(s, "l1x")
            cross_scalar(s, L1)
            ln_scalar(s, "l1a", 2)
            self_scalar(s, SB)
            ln_scalar(s, "l1m")
            router_scalar(s)
            experts_scalar(s)

        @block.vector
        def _(v):
            v.memset(eps_c, EPS).then_inc(s_memset, 1)
            v.memset(gel0, -STEP / 256).then_inc(s_memset, 1)
            v.memset(gel1, -STEP / 256 + 0.25).then_inc(s_memset, 1)
            v.memset(nstep, -STEP).then_inc(s_memset, 1)
            v.wait_ge(s_x, 16)
            ln_vector(v, "l0x")
            for part in range(SPLITS):
                context_head(v, L0, 0, 0, part)
            cross_vector(v, L0)
            ln_vector(v, "l0a", project_finish(L0))
            self_vector(v, SA)
            ln_vector(v, "l0f", self_finish(SA))
            ffn_vector(v)
            ln_vector(v, "l1x", ffn_finish)
            cross_vector(v, L1)
            ln_vector(v, "l1a", project_finish(L1), (gam, bet, s_gb))
            self_vector(v, SB)
            ln_vector(v, "l1m", self_finish(SB))
            router_vector(v)
            experts_vector(v)

        @block.tensor
        def _(pe):
            ln_tensor(pe, "l0x")
            cross_tensor(pe, L0)
            ln_tensor(pe, "l0a")
            self_tensor(pe, SA)
            ln_tensor(pe, "l0f")
            ffn_tensor(pe)
            ln_tensor(pe, "l1x")
            cross_tensor(pe, L1)
            ln_tensor(pe, "l1a")
            self_tensor(pe, SB)
            ln_tensor(pe, "l1m")
            router_tensor(pe)
            experts_tensor(pe)


def kernel(**inputs):
    import concourse.bacc as bacc
    from concourse.bass_utils import run_bass_kernel_spmd as run

    i = {k: np.asarray(v) for k, v in inputs.items()}
    cos, sin = rope_tables()
    arrays = {
        "x": i["x"].reshape(T, D),
        "ctx": i["ctx_768"],
        "ctxT": i["ctx_768"].transpose(0, 2, 1),
        "L0_xattn_WkT": i["L0_xattn_Wk"].T,
        "L1_xattn_WkT": i["L1_xattn_Wk"].T,
        "ident": np.eye(P, dtype=np.float32),
        "cos": cos,
        "sin": sin,
        "cmask": np.where(np.arange(S)[None, :] <= (np.arange(P) % S)[:, None], 0.0, -1e30).astype(np.float32),
    }
    swap = np.arange(D) ^ 1
    for n, k in (("PQT", "P_Q"), ("PKT", "P_K"), ("PVT", "P_V"), ("POT", "P_O")):
        arrays["L0_attn_" + n] = i["L0_attn_" + k].T
    arrays["L0_attn_PQsT"] = i["L0_attn_P_Q"][swap].T
    arrays["L0_attn_PKsT"] = i["L0_attn_P_K"][swap].T
    arrays["L0_ffn_b1_cols"] = i["L0_ffn_b1"].reshape(-1, P).T
    arrays["L1_attn_b_cols"] = i["L1_attn_b_qkv"].reshape(-1, P).T
    arrays["L1_ffn_gates"] = np.concatenate([i["L1_ffn_gate_w"], i["L1_ffn_shared_gate_w"]], 1)
    arrays["L1_attn_w_qkvT"] = i["L1_attn_w_qkv"].T
    part = np.arange(P)
    arrays["eo"] = np.stack([part // DK % 2 == 0, part // DK % 2 == 1], 1).astype(np.float32)
    arrays["iota16"] = np.broadcast_to(np.arange(P), (P, P)).astype(np.float16)
    arrays["id16"] = np.eye(P, dtype=np.float16)
    arrays["tri"] = np.concatenate([part[:, None] < part[None, :], np.ones((P, P), bool)], 1).astype(np.float32)
    for k in i:
        if k not in ("x", "ctx_768", "L0_xattn_Wk", "L1_xattn_Wk", "L1_attn_w_qkv", "L1_attn_b_qkv", "L0_ffn_b1", "L1_ffn_gate_w", "L1_ffn_shared_gate_w") and "_attn_P" not in k:
            arrays[k] = i[k]
    arrays = {k: np.ascontiguousarray(v) for k, v in arrays.items()}
    nc = bacc.Bacc("TRN2", target_bir_lowering=False, num_devices=1)
    a = {k: nc.dram_tensor(k + "_dram", v.shape, mybir.dt.from_np(v.dtype), kind="ExternalInput").ap() for k, v in arrays.items()}
    out = nc.dram_tensor("out_dram", (T, D), F32, kind="ExternalOutput").ap()
    perceiver(nc, a, out)
    r = run(nc, [{k + "_dram": v for k, v in arrays.items()}], core_ids=[0])
    return r.results[0]["out_dram"].reshape(B, S, D)
```
